# Optimizing a Trainium2 kernel written in Bass

```python
import numpy as np
import jax
import jax.numpy as jnp

def _softmax(x, axis=-1):
    return jax.nn.softmax(x, axis=axis)

def _gelu(x):
    return jax.nn.gelu(x, approximate=True)

def _silu(x):
    return jax.nn.silu(x)

def _sigmoid(x):
    return jax.nn.sigmoid(x)

def _layernorm(x, axis=-1, eps=1e-05):
    m = jnp.mean(x, axis=axis, keepdims=True)
    v = jnp.var(x, axis=axis, keepdims=True)
    return (x - m) / jnp.sqrt(v + eps)

def _scatter_add(tgt, idx, src, axis=0):
    return tgt.at[idx].add(src)

def _segment_sum(src, seg, n):
    return jax.ops.segment_sum(src, seg, n)
kernel_name = 'mk_gps_d1_gnn_r32_b459bb'

def setup_inputs(seed: int=0):
    np.random.seed(seed)
    _w = jnp.asarray

    def _rec_inputs():
        import jax
        import jax.numpy as jnp
        _gk = jax.random.key(seed)
        x = -0.0002117 + 1 * jax.random.normal(jax.random.fold_in(_gk, 1), (3125, 256), jnp.float32)
        src = jax.random.randint(jax.random.fold_in(_gk, 2), (50000,), 0, 3125, jnp.int32)
        dst = jax.random.randint(jax.random.fold_in(_gk, 3), (50000,), 0, 3125, jnp.int32)
        _o = jnp.argsort(dst, stable=True)
        src = src[_o]
        dst = dst[_o]
        edge_weight = jax.random.uniform(jax.random.fold_in(_gk, 12), (50000,), jnp.float32, 0.0, 1)
        return (x, src, dst, edge_weight)
    x, src, dst, edge_weight = _rec_inputs()

    def _L0_gnn_setup():
        import jax, jax.numpy as jnp
        import numpy as np
        N = 3125
        E = 100000
        D_IN = 256
        D_OUT = 256
        EPS = 1e-12
        key = jax.random.key(seed)
        k1, k2, k3, k4, k5, k6 = jax.random.split(key, 6)
        x = jax.random.normal(k1, (N, D_IN), dtype=jnp.float32)
        edge_src = jax.random.randint(k2, (E,), 0, N, dtype=jnp.int32)
        edge_dst = jax.random.randint(k3, (E,), 0, N, dtype=jnp.int32)
        edge_w = jax.random.uniform(k4, (E,), dtype=jnp.float32)
        w_self = jax.random.normal(k5, (D_OUT, D_IN), dtype=jnp.float32) * 0.05
        w_neigh = jax.random.normal(k6, (D_OUT, D_IN), dtype=jnp.float32) * 0.05
        return {'x': x, 'edge_src': edge_src, 'edge_dst': edge_dst, 'edge_w': edge_w, 'w_self': w_self, 'w_neigh': w_neigh}
    _L0_gnn_all = _L0_gnn_setup()
    _L0_gnn_in = {k: v for k, v in _L0_gnn_all.items() if k in ('w_self', 'w_neigh')}
    del _L0_gnn_all

    def _L0_mix_setup():
        import jax, jax.numpy as jnp
        import numpy as np
        NHEAD = 8
        ATT_EPS = 1e-06
        LN_EPS = 1e-05

        def _layernorm(x, g, b):
            mu = jnp.mean(x, axis=-1, keepdims=True)
            var = jnp.mean(jnp.square(x - mu), axis=-1, keepdims=True)
            return (x - mu) * jax.lax.rsqrt(var + LN_EPS) * g + b
        key = jax.random.key(seed)
        ks = jax.random.split(key, 7)
        N, L, C = (4, 512, 256)
        s = 1.0 / np.sqrt(C)
        return {'x': jax.random.normal(ks[0], (N, L, C), jnp.float32), 'Wq': jax.random.normal(ks[1], (C, C), jnp.float32) * s, 'Wk': jax.random.normal(ks[2], (C, C), jnp.float32) * s, 'Wv': jax.random.normal(ks[3], (C, C), jnp.float32) * s, 'Wm': jax.random.normal(ks[4], (C, C), jnp.float32) * s, 'W1': jax.random.normal(ks[5], (2 * C, 2 * C), jnp.float32) * (1.0 / np.sqrt(2 * C)), 'W2': jax.random.normal(ks[6], (2 * C, C), jnp.float32) * (1.0 / np.sqrt(2 * C)), 'g1': jnp.ones((C,), jnp.float32), 'b1': jnp.zeros((C,), jnp.float32), 'g2': jnp.ones((C,), jnp.float32), 'b2': jnp.zeros((C,), jnp.float32)}
    _L0_mix_all = _L0_mix_setup()
    _L0_mix_in = {k: v for k, v in _L0_mix_all.items() if k in ('Wq', 'Wk', 'Wv', 'Wm', 'W1', 'W2', 'g1', 'b1', 'g2', 'b2')}
    del _L0_mix_all

    def _L0_ffn_setup():
        import jax, jax.numpy as jnp
        import numpy as np
        E, D, H, TOP_K = (6, 256, 256, 2)
        ROUTER_H = D // 2
        key = jax.random.key(seed)
        ks = jax.random.split(key, 12)
        s = 1.0 / np.sqrt(D)
        sh = 1.0 / np.sqrt(H)
        sr = 1.0 / np.sqrt(ROUTER_H)
        return {'features': jax.random.normal(ks[0], (8, 128, D), dtype=jnp.float32), 'router_w1': jax.random.uniform(ks[1], (D, ROUTER_H), jnp.float32, -s, s), 'router_b1': jnp.zeros((ROUTER_H,), jnp.float32), 'router_w2': jax.random.uniform(ks[2], (ROUTER_H, E), jnp.float32, -sr, sr), 'router_b2': jnp.zeros((E,), jnp.float32), 'expert_w1': jax.random.uniform(ks[3], (E, D, H), jnp.float32, -s, s), 'expert_b1': jnp.zeros((E, H), jnp.float32), 'expert_w2': jax.random.uniform(ks[4], (E, H, H), jnp.float32, -sh, sh), 'expert_b2': jnp.zeros((E, H), jnp.float32), 'expert_w3': jax.random.uniform(ks[5], (E, H, D), jnp.float32, -sh, sh), 'expert_b3': jnp.zeros((E, D), jnp.float32)}
    _L0_ffn_all = _L0_ffn_setup()
    _L0_ffn_in = {k: v for k, v in _L0_ffn_all.items() if k in ('router_w1', 'router_b1', 'router_w2', 'router_b2', 'expert_w1', 'expert_b1', 'expert_w2', 'expert_b2', 'expert_w3', 'expert_b3')}
    del _L0_ffn_all
    return {'x': x, 'src': src, 'dst': dst, 'edge_weight': edge_weight, 'L0_gnn_w_self': _L0_gnn_in['w_self'], 'L0_gnn_w_neigh': _L0_gnn_in['w_neigh'], 'L0_mix_Wq': _L0_mix_in['Wq'], 'L0_mix_Wk': _L0_mix_in['Wk'], 'L0_mix_Wv': _L0_mix_in['Wv'], 'L0_mix_Wm': _L0_mix_in['Wm'], 'L0_mix_W1': _L0_mix_in['W1'], 'L0_mix_W2': _L0_mix_in['W2'], 'L0_mix_g1': _L0_mix_in['g1'], 'L0_mix_b1': _L0_mix_in['b1'], 'L0_mix_g2': _L0_mix_in['g2'], 'L0_mix_b2': _L0_mix_in['b2'], 'L0_ffn_router_w1': _L0_ffn_in['router_w1'], 'L0_ffn_router_b1': _L0_ffn_in['router_b1'], 'L0_ffn_router_w2': _L0_ffn_in['router_w2'], 'L0_ffn_router_b2': _L0_ffn_in['router_b2'], 'L0_ffn_expert_w1': _L0_ffn_in['expert_w1'], 'L0_ffn_expert_b1': _L0_ffn_in['expert_b1'], 'L0_ffn_expert_w2': _L0_ffn_in['expert_w2'], 'L0_ffn_expert_b2': _L0_ffn_in['expert_b2'], 'L0_ffn_expert_w3': _L0_ffn_in['expert_w3'], 'L0_ffn_expert_b3': _L0_ffn_in['expert_b3']}

def reference(x, src, dst, edge_weight, L0_gnn_w_self, L0_gnn_w_neigh, L0_mix_Wq, L0_mix_Wk, L0_mix_Wv, L0_mix_Wm, L0_mix_W1, L0_mix_W2, L0_mix_g1, L0_mix_b1, L0_mix_g2, L0_mix_b2, L0_ffn_router_w1, L0_ffn_router_b1, L0_ffn_router_w2, L0_ffn_router_b2, L0_ffn_expert_w1, L0_ffn_expert_b1, L0_ffn_expert_w2, L0_ffn_expert_b2, L0_ffn_expert_w3, L0_ffn_expert_b3):
    import jax
    import jax.numpy as jnp

    def _L0_gnn_ref(x, edge_src, edge_dst, edge_w, w_self, w_neigh):
        import jax, jax.numpy as jnp
        import numpy as np
        N = 3125
        E = 100000
        D_IN = 256
        D_OUT = 256
        EPS = 1e-12
        x_self = x @ w_self.T
        msgs = edge_w[:, None] * x[edge_src]
        x_neigh = jax.ops.segment_sum(msgs, edge_dst, num_segments=N)
        x_neigh = x_neigh @ w_neigh.T
        out = x_self + x_neigh
        norm = jnp.sqrt(jnp.sum(out * out, axis=1, keepdims=True))
        return out / jnp.maximum(norm, EPS)

    def _L0_mix_ref(x, Wq, Wk, Wv, Wm, W1, W2, g1, b1, g2, b2):
        import jax, jax.numpy as jnp
        import numpy as np
        NHEAD = 8
        ATT_EPS = 1e-06
        LN_EPS = 1e-05

        def _layernorm(x, g, b):
            mu = jnp.mean(x, axis=-1, keepdims=True)
            var = jnp.mean(jnp.square(x - mu), axis=-1, keepdims=True)
            return (x - mu) * jax.lax.rsqrt(var + LN_EPS) * g + b
        N, L, C = x.shape
        H = NHEAD
        D = C // H
        q = (x @ Wq).reshape(N, L, H, D)
        k = (x @ Wk).reshape(N, L, H, D)
        v = (x @ Wv).reshape(N, L, H, D)
        Q = jax.nn.elu(q) + 1.0
        K = jax.nn.elu(k) + 1.0
        v = v / L
        KV = jnp.einsum('nshd,nshv->nhdv', K, v)
        Z = 1.0 / (jnp.einsum('nlhd,nhd->nlh', Q, K.sum(axis=1)) + ATT_EPS)
        msg = jnp.einsum('nlhd,nhdv,nlh->nlhv', Q, KV, Z) * L
        msg = msg.reshape(N, L, C) @ Wm
        msg = _layernorm(msg, g1, b1)
        h = jnp.concatenate([x, msg], axis=-1) @ W1
        h = jax.nn.relu(h) @ W2
        msg = _layernorm(h, g2, b2)
        return x + msg

    def _L0_ffn_ref(features, router_w1, router_b1, router_w2, router_b2, expert_w1, expert_b1, expert_w2, expert_b2, expert_w3, expert_b3):
        import jax, jax.numpy as jnp
        import numpy as np
        E, D, H, TOP_K = (6, 256, 256, 2)
        ROUTER_H = D // 2
        rh = jax.nn.relu(features @ router_w1 + router_b1)
        expert_logits = jax.nn.softmax(rh @ router_w2 + router_b2, axis=-1)
        top_w, top_i = jax.lax.top_k(expert_logits, TOP_K)
        routing_weights = jax.nn.softmax(top_w, axis=-1)
        h1 = jax.nn.relu(jnp.einsum('bsd,edh->bseh', features, expert_w1) + expert_b1)
        h2 = jax.nn.relu(jnp.einsum('bseh,ehf->bsef', h1, expert_w2) + expert_b2)
        expert_out = jnp.einsum('bsef,efo->bseo', h2, expert_w3) + expert_b3
        sel = jnp.take_along_axis(expert_out, top_i[:, :, :, None], axis=2)
        combined = jnp.sum(sel * routing_weights[..., None], axis=2)
        return combined
    xn = _layernorm(x, axis=-1)
    x = x + _L0_gnn_ref(xn, src, dst, edge_weight, L0_gnn_w_self, L0_gnn_w_neigh) + _L0_mix_ref(xn[None], L0_mix_Wq, L0_mix_Wk, L0_mix_Wv, L0_mix_Wm, L0_mix_W1, L0_mix_W2, L0_mix_g1, L0_mix_b1, L0_mix_g2, L0_mix_b2)[0]
    x = x + _L0_ffn_ref(_layernorm(x, axis=-1)[None], L0_ffn_router_w1, L0_ffn_router_b1, L0_ffn_router_w2, L0_ffn_router_b2, L0_ffn_expert_w1, L0_ffn_expert_b1, L0_ffn_expert_w2, L0_ffn_expert_b2, L0_ffn_expert_w3, L0_ffn_expert_b3)[0]
    return x

_drawn_inputs = setup_inputs


def setup_inputs(seed=0):
    import zlib

    import numpy as np

    out = dict(_drawn_inputs(seed))
    spreads = {'L0_mix_g1': (1.0, 0.2),
     'L0_mix_b1': (0.0, 0.1),
     'L0_mix_g2': (1.0, 0.2),
     'L0_mix_b2': (0.0, 0.1),
     'L0_ffn_router_b1': (0.0, 0.44),
     'L0_ffn_router_b2': (0.0, 0.302),
     'L0_ffn_expert_b1': (0.0, 0.8),
     'L0_ffn_expert_b2': (0.0, 0.639),
     'L0_ffn_expert_b3': (0.0, 0.1)}
    factors = {'edge_weight': 4.216, 'L0_gnn_w_self': 4.494}
    for name, (base, spread) in spreads.items():
        noise = np.random.default_rng([zlib.crc32(name.encode()), seed]).standard_normal(out[name].shape)
        drawn = base * np.exp(spread * noise) if base else spread * noise
        out[name] = jnp.asarray(drawn.astype(out[name].dtype))
    for name, factor in factors.items():
        out[name] = (out[name] * factor).astype(out[name].dtype)
    return out
```

```python
from contextlib import ExitStack

import concourse.bass as bass
from concourse import mybir

F32 = mybir.dt.float32
I32 = mybir.dt.int32
ALU = mybir.AluOpType
ACT = mybir.ActivationFunctionType
AX = mybir.AxisListType.X
DVE_ONLY = (mybir.EngineType.DVE,)

LN_EPS = 1e-5
ATT_EPS = 1e-6
NORM_EPS = 1e-12
RSQRT_SEED = float(0x5F3759DF)


class Links:

    def __init__(self, eng, sem, per=0, i=0):
        self.eng, self.sem, self.per, self.i, self.k = eng, sem, per, i, 0

    def add(self, ins):
        ins.then_inc(self.sem, 1)
        self.k += 1

    def value(self):
        return self.i * self.per + self.k if self.per else self.k

    def wait(self):
        self.eng.wait_ge(self.sem, self.value())

    def link(self, ins):
        self.add(ins)
        self.wait()

    def close(self):
        assert self.k == self.per, (self.k, self.per)


def rsqrt(nc, ln, out, v, t):
    ln.link(nc.vector.tensor_scalar(t.bitcast(I32), v.bitcast(I32), 1, None, ALU.logical_shift_right))
    ln.link(nc.vector.tensor_scalar(out.bitcast(I32), t.bitcast(I32), -1.0, RSQRT_SEED, ALU.mult, ALU.add))
    for _ in range(3):
        ln.link(nc.vector.tensor_tensor(out=t, in0=out, in1=out, op=ALU.mult))
        ln.link(nc.vector.scalar_tensor_tensor(out=t, in0=t, scalar=-0.5, in1=v, op0=ALU.mult, op1=ALU.mult))
        ln.link(nc.vector.scalar_tensor_tensor(out=out, in0=t, scalar=1.5, in1=out, op0=ALU.add, op1=ALU.mult))


RSQRT_LINKS = 11


def gps_layer_kernel(nc, x, src, dst, edge_w, w_self_t, w_neigh_t, wq, wk, wv, wm, w1, w2, g1c, b1c, g2, b2,
                     rw1, rb1c, rw2, rb2, ew1, eb1c, ew2, eb2c, ew3, eb3, out):
    N, D = x.shape
    E = src.shape[0]
    TR, TG = 125, 5
    NT = N // TR
    NG = NT // TG
    GN = TG * TR
    KC = D // 128
    H1 = w1.shape[1] // 128
    HEADS, HD = 8, 32
    HPC = 128 // HD
    HW = 128 + HPC
    NX = ew1.shape[0]
    RH = rw1.shape[1]
    WIN = 128
    NCH = E // TR
    ROWS = 4
    CR = NCH // ROWS
    CPG0 = 16
    CPG1 = (NCH - NG * CPG0) // NG
    RING = 16
    RP = RING // 2
    ACCW = N + WIN + 3
    PARTS = ((0, 3), (3, 2))
    MAXP = 3 * TR
    assert N == NT * TR and NT == NG * TG and E == NCH * TR and NCH == NG * (CPG0 + CPG1) and NCH == ROWS * CR
    assert CPG0 % RING == 0 and CPG1 % RING == 0 and RH == 128

    ctx = ExitStack()
    with ctx:
        def sb(name, shape, dt=F32):
            return ctx.enter_context(nc.sbuf_tensor(name, shape, dt))

        def pb(name, shape):
            return ctx.enter_context(nc.psum_tensor(name, shape, F32))

        def sem(name):
            return ctx.enter_context(nc.semaphore(name))

        xn_dram = nc.dram_tensor("xn_rows", (N, D), F32).ap()
        xnT_dram = nc.dram_tensor("xn_columns", (128, KC, N), F32).ap()
        low_dram = nc.dram_tensor("window_starts", (2, NCH), I32).ap()

        ident = sb("ident", [128, 128])
        win_iota_i = sb("win_iota_i", [TR, WIN], I32)
        win_iota = sb("win_iota", [TR, WIN])
        g2_bc = sb("g2_bc", [TR, D])
        b2_bc = sb("b2_bc", [TR, D])
        rb2_bc = sb("rb2_bc", [TR, NX])
        rev = sb("rev", [TR, NX])
        wkv_sb = sb("wkv_sb", [128, KC, 2 * D])
        wq_sb = sb("wq_sb", [128, KC, D])
        wm_sb = sb("wm_sb", [128, KC, D])
        w1_sb = sb("w1_sb", [128, 2 * KC, 2 * D])
        w2_sb = sb("w2_sb", [128, H1, D])
        g1_sb = sb("g1_sb", [128, KC])
        b1_sb = sb("b1_sb", [128, KC])
        ws_sb = sb("ws_sb", [128, KC, D])
        wn_sb = sb("wn_sb", [128, KC, D])
        rw1_sb = sb("rw1_sb", [128, KC, RH])
        rb1_sb = sb("rb1_sb", [128, 1])
        rw2_sb = sb("rw2_sb", [128, NX])
        ew_sb = sb("ew_sb", [128, 3, NX, KC, D])
        eb_sb = sb("eb_sb", [128, 2, NX, KC])
        b3_sb = sb("b3_sb", [128, D])
        resid = sb("resid", [TR, NT, D])
        accT = sb("accT", [128, KC, ACCW])
        mv_all = sb("mv_all", [TR, NT, 2])
        ve_all = sb("ve_all", [TR, NT])
        rstd_all = sb("rstd_all", [TR, NT])
        rtmp_all = sb("rtmp_all", [TR, NT])
        gates_all = sb("gates_all", [TR, NT, NX])
        kv_acc = sb("kv_acc", [128, KC, 129])
        kv_bd = sb("kv_bd", [128, KC, HW])
        low_f = sb("low_f", [CR, ROWS])
        span_f = sb("span_f", [CR, ROWS])
        low_i = sb("low_i", [CR, 2, ROWS], I32)
        low_row = sb("low_row", [1, 2, NCH], I32)
        relT = sb("relT", [TR, NCH])
        wT = sb("wT", [TR, NCH])
        srcT = sb("srcT", [TR, NCH], I32)
        rel_g = sb("rel_g", [TR, CPG1])
        w_g = sb("w_g", [TR, CPG1])
        src_g = sb("src_g", [TR, CPG1], I32)
        msg = sb("msg", [TR, RING, D])
        onehot = sb("onehot", [TR, 4, WIN])
        colA = sb("colA", [128, KC, GN])
        colB = sb("colB", [128, KC, GN])
        colC = sb("colC", [128, KC, GN])
        colD = sb("colD", [128, KC, GN])
        hid = sb("hid", [128, H1, GN])
        def early(buf, k):
            return buf[0:CR, k, 0:ROWS * TR].rearrange("p (j e) -> p j e", j=ROWS)

        dst_i, src_i, ew_r, dst_f = early(hid, 0).bitcast(I32), early(hid, 1).bitcast(I32), early(hid, 2), early(hid, 3)
        src_f = early(colD, 0)
        rowA = sb("rowA", [TR, TG, D])
        rowB = sb("rowB", [TR, TG, D])
        v_g = sb("v_g", [TR, TG, KC, 129])
        el_e = sb("el_e", [128, 2, MAXP])
        el_r = sb("el_r", [128, 2, MAXP])
        st_g = sb("st_g", [TR, TG, 6])
        mv_g = sb("mv_g", [TR, TG, 2])
        ve_g = sb("ve_g", [TR, TG])
        rs_g = sb("rs_g", [TR, TG])
        rt_g = sb("rt_g", [TR, TG])
        gate_pad = sb("gate_pad", [TR, TG, 128])
        gates_g = sb("gates_g", [TR, TG, NX])
        sm = sb("sm", [TR, 6, TG, NX])
        sv = sb("sv", [TR, 8, TG])
        spill_i = sb("spill_i", [1, 1], I32)
        over_f = sb("over_f", [TR, 4])
        over_at = sb("over_at", [1, 2])
        over_i = sb("over_i", [1, 2], I32)
        zv_g = sb("zv_g", [TR, TG])
        zr = sb("zr", [TR, KC, HPC])

        ps_agg = pb("ps_agg", [128, 2, 2, KC, WIN])
        ps_big = pb("ps_big", [128, 2, 512])
        ps_att = pb("ps_att", [128, 512])
        ps_tr = pb("ps_tr", [128, 512])
        ps_row = pb("ps_row", [128, 2, 512])

        s_edges = sem("s_edges")
        s_x = sem("s_x")
        s_wkv, s_wmix, s_wffn, s_bc = sem("s_wkv"), sem("s_wmix"), sem("s_wffn"), sem("s_bc")
        s_ident = sem("s_ident")
        s_id0 = sem("s_id0")
        s_prep = sem("s_prep")
        s_edge_ready = sem("s_edge_ready")
        s_edge_tr = sem("s_edge_tr")
        s_low_out, s_low_in = sem("s_low_out"), sem("s_low_in")
        s_lists = sem("s_lists")
        s_v0, s_v0a, s_v0b = sem("s_v0"), sem("s_v0a"), sem("s_v0b")
        s_zero = sem("s_zero")
        s_xn = sem("s_xn")
        s_xn_tr = sem("s_xn_tr")
        s_xnT = sem("s_xnT")
        s_xnT_out = sem("s_xnT_out")
        s_xn_out = sem("s_xn_out")
        s_stage = sem("s_stage")
        s_kv_mm, s_kv_ev, s_key, s_kvp, s_kvsum = (sem("s_kv_mm"), sem("s_kv_ev"), sem("s_key"), sem("s_kvp"),
                                                   sem("s_kvsum"))
        s_src = sem("s_src")
        s_stored = sem("s_stored")
        s_taken = sem("s_taken")
        s_held = {}
        s_msg = [sem(f"s_msg{k}") for k in range(RING)]
        s_hot = sem("s_hot")
        s_pair = sem("s_pair")
        s_add = sem("s_add")
        s_v1 = sem("s_v1")
        s_bd = sem("s_bd")
        s_phase = sem("s_phase")
        s_big_mm = sem("s_big_mm")
        s_big_free = sem("s_big_free")
        s_q = sem("s_q")
        s_att_mm, s_att = sem("s_att_mm"), sem("s_att")
        s_tr_mm, s_tr_free = sem("s_tr_mm"), sem("s_tr_free")
        s_row_mm, s_row_free = sem("s_row_mm"), sem("s_row_free")
        s_norm1 = sem("s_norm1")
        s_h2done = sem("s_h2done")
        s_over_src, s_over_msg, s_over_hot, s_over_mm, s_over_add, s_over_v = (
            sem("s_over_src"), sem("s_over_msg"), sem("s_over_hot"), sem("s_over_mm"), sem("s_over_add"),
            sem("s_over_v"))
        s_v2, s_v2b = sem("s_v2"), sem("s_v2b")
        s_proj_mm, s_proj_ev, s_xn2, s_tr2_mm, s_tr2_ev = (sem("s_proj_mm"), sem("s_proj_ev"), sem("s_xn2"),
                                                          sem("s_tr2_mm"), sem("s_tr2_ev"))
        s_rh_mm, s_rh_ev, s_lg_mm, s_lg, s_ex, s_gate = (sem("s_rh_mm"), sem("s_rh_ev"), sem("s_lg_mm"),
                                                        sem("s_lg"), sem("s_ex"), sem("s_gate"))
        s_gtr_mm, s_gtr_ev, s_b3_mm, s_b3_add, s_back = (sem("s_gtr_mm"), sem("s_gtr_ev"), sem("s_b3_mm"),
                                                        sem("s_b3_add"), sem("s_back"))
        s_e_mm, s_e_ev, s_y_mm, s_y_add, s_v3, s_out = (sem("s_e_mm"), sem("s_e_ev"), sem("s_y_mm"), sem("s_y_add"),
                                                       sem("s_v3"), sem("s_out"))
        s_colE = sem("s_colE")
        s_spill = sem("s_spill")
        s_sm, s_over_chunk = sem("s_sm"), sem("s_over_chunk")

        for name in ("sync", "gpsimd", "tensor", "vector"):
            s_held[name] = sem(f"s_held_{name}")

        def hold(eng, name, semaphore, value):
            eng.wait_ge(semaphore, value)
            eng.sem_inc(s_held[name], 1)

        x_t = x.rearrange("(n p) d -> p n d", p=TR)
        out_t = out.rearrange("(n p) d -> p n d", p=TR)
        xn_t = xn_dram.rearrange("(n p) d -> p n d", p=TR)

        def chunked(w):
            return w.rearrange("(c p) n -> p c n", p=128)

        def edge_rows(e):
            return e.rearrange("(j p e) -> p j e", p=CR, e=TR)

        block = ctx.enter_context(nc.Block())

        def pairs_before(phase):
            return 0 if phase == 0 else NG * CPG0 // 2

        @block.sync
        def _(sp):
            sp.sem_inc(s_stored, 1)
            sp.sem_inc(s_taken, 1)
            for e, t in ((dst, dst_i), (src, src_i), (edge_w, ew_r)):
                sp.dma_start(t[:, :, :], edge_rows(e)).then_inc(s_edges, 16)
            with sp.Fori(0, NG) as g:
                sp.dma_start(resid[:, bass.ds(g * TG, TG), :], x_t[:, bass.ds(g * TG, TG), :]).then_inc(s_x, 16)
                hold(sp, "sync", s_x, 16 * g + 16)
            sp.dma_start(wkv_sb[:, :, 0:D], chunked(wk)).then_inc(s_wkv, 16)
            sp.dma_start(wkv_sb[:, :, D:2 * D], chunked(wv)).then_inc(s_wkv, 16)
            for t, w in ((g2_bc, g2), (b2_bc, b2), (rb2_bc, rb2)):
                sp.dma_start(t[:, :], w.partition_broadcast(TR)).then_inc(s_bc, 16)
            sp.wait_ge(s_edge_ready, 2)
            for k in range(2):
                sp.dma_start(low_dram[k, :].rearrange("(j p) -> p j", p=CR), low_i[:, k, :],
                             allow_slow_non_contiguous=True).then_inc(s_low_out, 16)
            sp.wait_ge(s_low_out, 32)
            sp.dma_start(low_row[:, :, :], low_dram.rearrange("(a k) n -> a k n", a=1)).then_inc(s_low_in, 16)
            with sp.Fori(0, NG) as g:
                sp.wait_ge(s_xn, TG * g + TG)
                sp.dma_start(xn_t[:, bass.ds(g * TG, TG), :], rowA[:, :, :]).then_inc(s_xn_out, 16)
                sp.wait_ge(s_xnT, 1 + TG * g + TG)
                sp.dma_start(xnT_dram[:, :, bass.ds(g * GN, GN)], colC[:, :, :]).then_inc(s_xnT_out, 16)
                sp.wait_ge(s_xn_out, 16 * g + 16)
                hold(sp, "sync", s_xnT_out, 16 * g + 16)
                sp.sem_inc(s_stored, 1)
            for t, w in ((wq_sb, chunked(wq)), (wm_sb, chunked(wm)), (w1_sb, chunked(w1)), (w2_sb, chunked(w2)),
                         (g1_sb, g1c), (b1_sb, b1c)):
                sp.dma_start(t[:, :] if len(t.shape) == 2 else t[:, :, :], w).then_inc(s_wmix, 16)
            with sp.Fori(0, NG) as g:
                sp.wait_ge(s_kv_mm, 1 + TG * g)
                sp.dma_start(colA[:, :, :], xnT_dram[:, :, bass.ds(g * GN, GN)]).then_inc(s_stage, 16)
            sp.wait_ge(s_ident, 3)
            for t, w in ((ws_sb[:, :, :], chunked(w_self_t)), (wn_sb[:, :, :], chunked(w_neigh_t)),
                         (rw1_sb[:, :, :], chunked(rw1)), (rb1_sb[:, :], rb1c), (rw2_sb[:, :], rw2),
                         (b3_sb[0:NX, :], eb3), (eb_sb[:, 0, :, :], eb1c), (eb_sb[:, 1, :, :], eb2c),
                         (ew_sb[:, 0, :, :, :], ew1.rearrange("e (c p) n -> p e c n", p=128)),
                         (ew_sb[:, 1, :, :, :], ew2.rearrange("e (c p) n -> p e c n", p=128)),
                         (ew_sb[:, 2, :, :, :], ew3.rearrange("e (c p) n -> p e c n", p=128))):
                sp.dma_start(t, w).then_inc(s_wffn, 16)
            with sp.Fori(0, NG) as g:
                sp.wait_ge(s_kv_mm, 1 + TG * NG)
                sp.wait_ge(s_big_mm, 1 + (2 * KC + 2 * H1) * g)
                sp.dma_start(colA[:, :, :], xnT_dram[:, :, bass.ds(g * GN, GN)]).then_inc(s_stage, 16)
            sp.wait_ge(s_phase, 9)
            with sp.Fori(0, NG) as g:
                sp.wait_ge(s_proj_mm, 1 + TG * g)
                sp.dma_start(colA[:, :, :], xnT_dram[:, :, bass.ds(g * GN, GN)]).then_inc(s_stage, 16)
                sp.dma_start(colB[:, :, :], accT[:, :, bass.ds(g * GN, GN)]).then_inc(s_colE, 16)
                sp.wait_ge(s_tr2_ev, 1 + TG * g + TG)
                sp.wait_ge(s_stage, 16 * (2 * NG + 1) + 16 * g)
                sp.dma_start(xnT_dram[:, :, bass.ds(g * GN, GN)], colC[:, :, :]).then_inc(s_back, 16)
                hold(sp, "sync", s_back, 16 * g + 16)
                sp.sem_inc(s_taken, 1)
            sp.wait_ge(s_back, 16 * NG)
            sp.wait_ge(s_phase, 12)
            with sp.Fori(0, NG) as g:
                sp.wait_ge(s_e_mm, 1 + NX * 8 * g)
                sp.dma_start(colA[:, :, :], xnT_dram[:, :, bass.ds(g * GN, GN)]).then_inc(s_stage, 16)
                sp.wait_ge(s_y_add, 1 + NX * TG * g + NX * TG)
                sp.dma_start(out_t[:, bass.ds(g * TG, TG), :], resid[:, bass.ds(g * TG, TG), :]).then_inc(s_out, 16)
            sp.wait_ge(s_out, 16 * NG)

        @block.gpsimd
        def _(pool):
            nc.gpsimd.memset(ident[:, :], 0.0).then_inc(s_id0, 1)
            pool.wait_ge(s_id0, 1)
            nc.gpsimd.affine_select(out=ident[:, :], in_=ident[:, :], compare_op=ALU.not_equal, fill=1.0, base=0,
                                    pattern=[[-1, 128]], channel_multiplier=1).then_inc(s_ident, 1)
            nc.gpsimd.iota(win_iota_i[:, :], pattern=[[1, WIN]], base=0, channel_multiplier=0).then_inc(s_ident, 1)
            nc.gpsimd.memset(b3_sb[:, :], 0.0).then_inc(s_ident, 1)
            for e in range(NX):
                nc.gpsimd.memset(rev[:, e:e + 1], float(NX - e))
            nc.gpsimd.memset(accT[:, :, :], 0.0).then_inc(s_zero, 1)
            nc.gpsimd.memset(v_g[:, :, :, :], 1.0).then_inc(s_zero, 1)
            nc.gpsimd.memset(kv_bd[:, :, :], 0.0).then_inc(s_zero, 1)
            nc.gpsimd.memset(kv_acc[:, :, :], 0.0).then_inc(s_zero, 1)

            pool.wait_ge(s_lists, 3)
            pool.wait_ge(s_xn_out, 16 * NG)

            def gathers(g, phase, cpg):
                first = pairs_before(phase)
                turns = first * 2 // RING
                with_idx = first * 2
                nc.gpsimd.tensor_copy(src_g[:, 0:cpg], srcT[:, bass.ds(g * cpg + with_idx, cpg)]).then_inc(s_src, 1)
                pool.wait_ge(s_src, g + 1 + (NG if phase else 0))
                for c in range(cpg):
                    if c % 2 == 0:
                        hold(pool, "gpsimd", s_pair, g * (cpg // 2) + (first + c // 2 + 1))
                    nc.gpsimd.indirect_dma_start(
                        out=msg[:, c % RING, :], out_offset=None, in_=xn_dram[:, :],
                        in_offset=bass.IndirectOffsetOnAxis(ap=src_g[:, c:c + 1], axis=0),
                    ).then_inc(s_msg[c % RING], 16)
                pool.wait_ge(s_msg[RING - 1], 16 * (cpg // RING) * g + 16 * (turns + cpg // RING))

            with pool.Fori(0, NG) as g:
                gathers(g, 0, CPG0)
            with pool.Fori(0, NG) as g:
                gathers(g, 1, CPG1)

            pool.wait_ge(s_spill, 1)
            pool.wait_ge(s_phase, 6)
            with pool.If(pool.value_load(spill_i[0:1, 0:1], min_val=0, max_val=N) > WIN - 1):
                with pool.Fori(0, NCH) as c:
                    pool.wait_ge(s_over_chunk, 1 + c)
                    nc.gpsimd.tensor_copy(src_g[:, 0:1], srcT[:, bass.ds(c, 1)]).then_inc(s_over_src, 1)
                    hold(pool, "gpsimd", s_over_src, c + 1)
                    nc.gpsimd.indirect_dma_start(
                        out=msg[:, 0, :], out_offset=None, in_=xn_dram[:, :],
                        in_offset=bass.IndirectOffsetOnAxis(ap=src_g[:, 0:1], axis=0),
                    ).then_inc(s_over_msg, 16)

        @block.tensor
        def _(pe):
            pe.sem_inc(s_pair, RP)
            for started in (s_kvp, s_kv_mm, s_big_mm, s_proj_mm, s_tr2_mm, s_xn_tr, s_e_mm, s_gtr_mm):
                pe.sem_inc(started, 1)
            pe.wait_ge(s_ident, 1)
            pe.wait_ge(s_edge_ready, 2)
            pe.wait_ge(s_edges, 48)
            for k, (t, bank) in enumerate(((dst_f, ps_big[:, 0, :]), (src_f, ps_big[:, 1, :]), (ew_r, ps_att))):
                for j in range(ROWS):
                    last = nc.tensor.transpose(bank[0:TR, j * CR:(j + 1) * CR], t[:, j, :], ident[0:CR, 0:CR])
                last.then_inc(s_edge_tr, 1)

            with pe.Fori(0, NG) as g:
                for t in range(TG):
                    pe.wait_ge(s_xn, TG * g + t + 1)
                    pe.wait_ge(s_xnT, 1 + TG * g + max(t - 1, 0))
                    for c in range(KC):
                        last = nc.tensor.transpose(ps_row[:, t % 2, c * TR:(c + 1) * TR],
                                                   rowA[:, t, c * 128:(c + 1) * 128], ident[0:TR, 0:TR])
                    last.then_inc(s_xn_tr, 1)

            def agg(g, phase, cpg, q0, q1):
                first = pairs_before(phase)
                for q in range(q0, q1):
                    pe.wait_ge(s_hot, g * (cpg // 2) + (first + q + 1))
                    pe.wait_ge(s_add, g * cpg + (2 * (first + q) + 2))
                    for h in range(2):
                        c = 2 * q + h
                        pe.wait_ge(s_msg[c % RING], 16 * (cpg // RING) * g + 16 * (2 * first // RING + c // RING + 1))
                        for k in range(KC):
                            last = nc.tensor.matmul(ps_agg[:, q % 2, h, k, :], msg[:, c % RING, k * 128:(k + 1) * 128],
                                                    onehot[:, c % 4, :], start=True, stop=True)
                    last.then_inc(s_pair, 1)

            pe.wait_ge(s_wkv, 32)
            pe.wait_ge(s_lists, 3)
            with pe.Fori(0, NG) as g:
                def key_value_product(t):
                    pe.wait_ge(s_key, 1 + TG * g + t + 1)
                    if t == 0:
                        pe.wait_ge(s_kvsum, 1 + g)
                    for c in range(KC):
                        last = nc.tensor.matmul(ps_row[:, c, 0:129], rowB[:, t, c * 128:(c + 1) * 128],
                                                v_g[:, t, c, :], start=(t == 0), stop=(t == TG - 1))
                    last.then_inc(s_kvp, 1)

                for t in range(TG):
                    if t == 0:
                        pe.wait_ge(s_xnT, 1 + TG * NG)
                        pe.wait_ge(s_stage, 16 * g + 16)
                    pe.wait_ge(s_kv_ev, 1 + TG * g + max(t - 1, 0))
                    for c in range(KC):
                        last = nc.tensor.matmul(ps_big[0:TR, t % 2, :], colA[:, c, t * TR:(t + 1) * TR],
                                                wkv_sb[:, c, :], start=(c == 0), stop=(c == KC - 1))
                    last.then_inc(s_kv_mm, 1)
                    if t:
                        key_value_product(t - 1)
                    agg(g, 0, CPG0, t, t + 1)
                agg(g, 0, CPG0, TG, TG + 1)
                key_value_product(TG - 1)
                agg(g, 0, CPG0, TG + 1, CPG0 // 2)
            pe.drain().then_inc(s_phase, 1)
            pe.wait_ge(s_phase, 3)

            pe.wait_ge(s_wmix, 16 * 6)
            with pe.Fori(0, NG) as g:
                PP = CPG1 // 2

                def a(q0, q1):
                    agg(g, 1, CPG1, q0, q1)

                def big_done(i, ins):
                    ins.then_inc(s_big_mm, 1)

                def queries(part):
                    t0, n = PARTS[part]
                    for m in range(KC):
                        i = part * KC + m
                        pe.wait_ge(s_big_free, (2 * KC + 2 * H1) * g + (i + 1))
                        for c in range(KC):
                            last = nc.tensor.matmul(ps_big[:, i % 2, 0:n * TR], wq_sb[:, c, m * 128:(m + 1) * 128],
                                                    colA[:, c, t0 * TR:(t0 + n) * TR], start=(c == 0), stop=(c == KC - 1))
                        last.then_inc(s_big_mm, 1)

                def attend(t):
                    pe.wait_ge(s_q, 1 + 2 * KC * g + (KC if t < PARTS[1][0] else 2 * KC))
                    pe.wait_ge(s_att, 1 + TG * g + t)
                    for c in range(KC):
                        last = nc.tensor.matmul(ps_att[0:TR, c * HW:(c + 1) * HW], colB[:, c, t * TR:(t + 1) * TR],
                                                kv_bd[:, c, :], start=True, stop=True)
                    last.then_inc(s_att_mm, 1)

                def turn(t, rows, ready, n, i):
                    pe.wait_ge(ready, n)
                    pe.wait_ge(s_tr_free, 1 + 2 * TG * g + i)
                    for c in range(KC):
                        last = nc.tensor.transpose(ps_tr[:, c * TR:(c + 1) * TR], rows[:, t, c * 128:(c + 1) * 128],
                                                   ident[0:TR, 0:TR])
                    last.then_inc(s_tr_mm, 1)

                def merge(t):
                    pe.wait_ge(s_tr_free, 1 + 2 * TG * g + (t + 1))
                    pe.wait_ge(s_row_free, 2 * TG * g + (t + 1))
                    for c in range(KC):
                        last = nc.tensor.matmul(ps_row[0:TR, t % 2, 0:D], colC[:, c, t * TR:(t + 1) * TR], wm_sb[:, c, :],
                                                start=(c == 0), stop=(c == KC - 1))
                    last.then_inc(s_row_mm, 1)

                def hidden(part):
                    t0, n = PARTS[part]
                    pe.wait_ge(s_tr_free, 1 + 2 * TG * g + (TG + t0 + n))
                    for m in range(H1):
                        i = 2 * KC + part * H1 + m
                        pe.wait_ge(s_big_free, (2 * KC + 2 * H1) * g + (i + 1))
                        for c in range(2 * KC):
                            col = colA if c < KC else colD
                            last = nc.tensor.matmul(ps_big[:, i % 2, 0:n * TR], w1_sb[:, c, m * 128:(m + 1) * 128],
                                                    col[:, c % KC, t0 * TR:(t0 + n) * TR],
                                                    start=(c == 0), stop=(c == 2 * KC - 1))
                        last.then_inc(s_big_mm, 1)
                        a(20 + part * H1 + m, 21 + part * H1 + m)

                def project(t):
                    i = TG + t
                    pe.wait_ge(s_big_free, (2 * KC + 2 * H1) * g + (2 + 2 * KC + (H1 if t < PARTS[1][0] else 2 * H1)))
                    pe.wait_ge(s_row_free, 2 * TG * g + (i + 1))
                    for c in range(H1):
                        last = nc.tensor.matmul(ps_row[0:TR, i % 2, 0:D], hid[:, c, t * TR:(t + 1) * TR], w2_sb[:, c, :],
                                                start=(c == 0), stop=(c == H1 - 1))
                    last.then_inc(s_row_mm, 1)

                pe.wait_ge(s_stage, 16 * g + 16 * (NG + 1))
                queries(0)
                a(0, 2)
                queries(1)
                a(2, 4)
                for t in range(TG + 2):
                    if t < TG:
                        attend(t)
                    if 1 <= t <= TG:
                        turn(t - 1, rowB, s_att, 1 + TG * g + t, t - 1)
                    if t >= 2:
                        merge(t - 2)
                    a(4 + t, 5 + t)
                a(11, 15)
                for t in range(TG):
                    turn(t, rowA, s_norm1, TG * g + (t + 1), TG + t)
                    a(15 + t, 16 + t)
                hidden(0)
                hidden(1)
                for t in range(TG):
                    project(t)
                    if t < 4:
                        a(28 + t, 29 + t)
                assert PP == 32
            pe.drain().then_inc(s_phase, 1)
            pe.wait_ge(s_phase, 6)

            pe.wait_ge(s_spill, 1)
            with pe.If(pe.value_load(spill_i[0:1, 0:1], min_val=0, max_val=N) > WIN - 1):
                with pe.Fori(0, NCH) as c:
                    hold(pe, "tensor", s_over_msg, 16 * c + 16)
                    with pe.Fori(0, NT - 1) as w:
                        pe.wait_ge(s_over_hot, (NT - 1) * c + w + 1)
                        for k in range(KC):
                            last = nc.tensor.matmul(ps_agg[:, 0, 0, k, :], msg[:, 0, k * 128:(k + 1) * 128],
                                                    onehot[:, 0, :], start=True, stop=True)
                        last.then_inc(s_over_mm, 1)
            pe.drain().then_inc(s_phase, 1)
            pe.wait_ge(s_phase, 9)

            pe.wait_ge(s_wffn, 16 * 11)
            with pe.Fori(0, NG) as g:
                pe.wait_ge(s_stage, 16 * g + 16 * (2 * NG + 1))
                pe.wait_ge(s_colE, 16 * g + 16)
                for t in range(TG):
                    pe.wait_ge(s_proj_ev, 1 + TG * g + max(t - 1, 0))
                    if t < 2:
                        pe.wait_ge(s_b3_add, 1 + TG * g)
                    for k, (col, w) in enumerate(((colA, ws_sb), (colB, wn_sb))):
                        for c in range(KC):
                            last = nc.tensor.matmul(ps_row[0:TR, t % 2, 0:D], col[:, c, t * TR:(t + 1) * TR], w[:, c, :],
                                                    start=(k == 0 and c == 0), stop=(k == 1 and c == KC - 1))
                    last.then_inc(s_proj_mm, 1)
                for t in range(TG):
                    pe.wait_ge(s_xn2, TG * g + (t + 1))
                    pe.wait_ge(s_tr2_ev, 1 + TG * g + t)
                    pe.wait_ge(s_gtr_ev, 1 + TG * g)
                    for c in range(KC):
                        last = nc.tensor.transpose(ps_tr[:, c * TR:(c + 1) * TR], rowA[:, t, c * 128:(c + 1) * 128],
                                                   ident[0:TR, 0:TR])
                    last.then_inc(s_tr2_mm, 1)
                for part, (t0, n) in enumerate(PARTS):
                    pe.wait_ge(s_tr2_ev, 1 + TG * g + (t0 + n))
                    pe.wait_ge(s_rh_ev, 1 + 2 * g)
                    for c in range(KC):
                        last = nc.tensor.matmul(ps_big[:, part, 0:n * TR], rw1_sb[:, c, :],
                                                colC[:, c, t0 * TR:(t0 + n) * TR], start=(c == 0), stop=(c == KC - 1))
                    last.then_inc(s_rh_mm, 1)
                pe.wait_ge(s_rh_ev, 1 + 2 * g + 2)
                pe.wait_ge(s_lg, 1 + g)
                for t in range(TG):
                    last = nc.tensor.matmul(ps_att[0:TR, t * NX:(t + 1) * NX], hid[:, 0, t * TR:(t + 1) * TR], rw2_sb[:, :],
                                            start=True, stop=True)
                last.then_inc(s_lg_mm, 1)
                pe.wait_ge(s_gate, g + 1)
                for t in range(TG):
                    pe.wait_ge(s_gtr_ev, 1 + TG * g + t)
                    nc.tensor.transpose(ps_tr[:, 0:TR], gate_pad[:, t, :], ident[0:TR, 0:TR]).then_inc(s_gtr_mm, 1)
                    pe.wait_ge(s_gtr_ev, 1 + TG * g + (t + 1))
                    pe.wait_ge(s_b3_add, 1 + TG * g + max(t - 1, 0))
                    pe.wait_ge(s_proj_ev, 1 + TG * g + TG)
                    nc.tensor.matmul(ps_row[0:TR, t % 2, 0:D], colD[:, 0, t * TR:(t + 1) * TR], b3_sb[:, :],
                                     start=True, stop=True).then_inc(s_b3_mm, 1)
            pe.drain().then_inc(s_phase, 1)
            pe.wait_ge(s_phase, 12)

            with pe.Fori(0, NG) as g:
                pe.wait_ge(s_stage, 16 * g + 16 * (3 * NG + 1))
                for e in range(NX):
                    for layer, (cin, cout) in enumerate(((colA, colB), (colB, colC))):
                        for part, (t0, n) in enumerate(PARTS):
                            for m in range(KC):
                                i = e * 8 + layer * 4 + part * KC + m
                                pe.wait_ge(s_e_ev, 1 + NX * 8 * g + max(i - 1, 0))
                                if layer:
                                    pe.wait_ge(s_e_ev, 1 + NX * 8 * g + (e * 8 + (part + 1) * KC))
                                for c in range(KC):
                                    last = nc.tensor.matmul(ps_big[:, i % 2, 0:n * TR],
                                                            ew_sb[:, layer, e, c, m * 128:(m + 1) * 128],
                                                            cin[:, c, t0 * TR:(t0 + n) * TR],
                                                            start=(c == 0), stop=(c == KC - 1))
                                last.then_inc(s_e_mm, 1)
                    for t in range(TG):
                        i = e * TG + t
                        pe.wait_ge(s_e_ev, 1 + NX * 8 * g + (e * 8 + 4 + (KC if t < PARTS[1][0] else 2 * KC)))
                        pe.wait_ge(s_y_add, 1 + NX * TG * g + max(i - 1, 0))
                        for c in range(KC):
                            last = nc.tensor.matmul(ps_row[0:TR, i % 2, 0:D], colC[:, c, t * TR:(t + 1) * TR],
                                                    ew_sb[:, 2, e, c, :], start=(c == 0), stop=(c == KC - 1))
                        last.then_inc(s_y_mm, 1)

        @block.scalar
        def _(act):
            act.sem_inc(s_big_free, 2)
            act.sem_inc(s_row_free, 2)
            for started in (s_xnT, s_kv_ev, s_tr_free, s_proj_ev, s_tr2_ev, s_gtr_ev, s_rh_ev, s_e_ev):
                act.sem_inc(started, 1)

            def cols(ps):
                return ps.rearrange("p (c n) -> p c n", c=KC)

            with act.Fori(0, NG) as g:
                for t in range(TG):
                    act.wait_ge(s_xn_tr, 1 + TG * g + (t + 1))
                    act.wait_ge(s_stored, 1 + g)
                    nc.scalar.copy(colC[:, :, t * TR:(t + 1) * TR],
                                   cols(ps_row[:, t % 2, 0:KC * TR])).then_inc(s_xnT, 1)

            act.wait_ge(s_zero, 4)
            with act.Fori(0, NG) as g:
                for t in range(TG):
                    act.wait_ge(s_kv_mm, 1 + TG * g + (t + 1))
                    act.wait_ge(s_key, 1 + TG * g + max(t - 1, 0))
                    act.wait_ge(s_kvp, 1 + TG * g)
                    nc.scalar.activation(el_e[0:TR, t % 2, 0:D], ps_big[0:TR, t % 2, 0:D], ACT.Exp)
                    nc.scalar.activation(el_r[0:TR, t % 2, 0:D], ps_big[0:TR, t % 2, 0:D], ACT.Relu)
                    nc.scalar.activation(v_g[:, t, :, 0:128], cols(ps_big[0:TR, t % 2, D:2 * D]), ACT.Copy,
                                         scale=1.0 / N).then_inc(s_kv_ev, 1)
            act.drain().then_inc(s_phase, 1)
            act.wait_ge(s_phase, 3)

            act.wait_ge(s_wmix, 16 * 6)
            with act.Fori(0, NG) as g:
                BIG = 2 * KC + 2 * H1

                def query(part):
                    t0, n = PARTS[part]
                    for m in range(KC):
                        i = part * KC + m
                        act.wait_ge(s_big_mm, 1 + BIG * g + (i + 1))
                        act.wait_ge(s_q, 1 + 2 * KC * g + max(i - 1, 0))
                        nc.scalar.activation(el_e[:, i % 2, 0:n * TR], ps_big[:, i % 2, 0:n * TR], ACT.Exp)
                        nc.scalar.activation(el_r[:, i % 2, 0:n * TR], ps_big[:, i % 2, 0:n * TR],
                                             ACT.Relu).then_inc(s_big_free, 1)

                query(0)
                query(1)
                for t in range(1, TG + 2):
                    if t <= TG:
                        act.wait_ge(s_tr_mm, 2 * TG * g + t)
                        nc.scalar.copy(colC[:, :, (t - 1) * TR:t * TR], cols(ps_tr[:, 0:KC * TR])).then_inc(s_tr_free, 1)
                    if t >= 2:
                        act.wait_ge(s_row_mm, 2 * TG * g + (t - 1))
                        act.wait_ge(s_h2done, 1 + TG * g)
                        nc.scalar.copy(rowA[:, t - 2, :], ps_row[0:TR, t % 2, 0:D]).then_inc(s_row_free, 1)
                for t in range(TG):
                    act.wait_ge(s_tr_mm, 2 * TG * g + (TG + t + 1))
                    for c in range(KC):
                        last = nc.scalar.activation(colD[:, c, t * TR:(t + 1) * TR], ps_tr[:, c * TR:(c + 1) * TR],
                                                    ACT.Identity, bias=b1_sb[:, c:c + 1], scale=g1_sb[:, c:c + 1])
                    last.then_inc(s_tr_free, 1)
                for part, (t0, n) in enumerate(PARTS):
                    for m in range(H1):
                        i = 2 * KC + part * H1 + m
                        act.wait_ge(s_big_mm, 1 + BIG * g + (i + 1))
                        nc.scalar.activation(hid[:, m, t0 * TR:(t0 + n) * TR], ps_big[:, i % 2, 0:n * TR],
                                             ACT.Relu).then_inc(s_big_free, 1)
                for t in range(TG):
                    act.wait_ge(s_row_mm, 2 * TG * g + (TG + t + 1))
                    nc.scalar.copy(rowA[:, t, :], ps_row[0:TR, (TG + t) % 2, 0:D]).then_inc(s_row_free, 1)
            act.drain().then_inc(s_phase, 1)
            act.wait_ge(s_phase, 6)
            act.drain().then_inc(s_phase, 1)
            act.wait_ge(s_phase, 9)

            act.wait_ge(s_wffn, 16 * 11)
            with act.Fori(0, NG) as g:
                for t in range(TG):
                    act.wait_ge(s_proj_mm, 1 + TG * g + (t + 1))
                    act.wait_ge(s_tr2_mm, 1 + TG * g)
                    nc.scalar.copy(rowA[:, t, :], ps_row[0:TR, t % 2, 0:D])
                    nc.scalar.activation(rowB[:, t, :], ps_row[0:TR, t % 2, 0:D], ACT.Square,
                                         accum_out=ve_g[:, t:t + 1]).then_inc(s_proj_ev, 1)
                act.wait_ge(s_taken, 1 + g)
                for t in range(TG):
                    act.wait_ge(s_tr2_mm, 1 + TG * g + (t + 1))
                    nc.scalar.copy(colC[:, :, t * TR:(t + 1) * TR], cols(ps_tr[:, 0:KC * TR])).then_inc(s_tr2_ev, 1)
                for part, (t0, n) in enumerate(PARTS):
                    act.wait_ge(s_rh_mm, 2 * g + (part + 1))
                    nc.scalar.activation(hid[:, 0, t0 * TR:(t0 + n) * TR], ps_big[:, part, 0:n * TR], ACT.Relu,
                                         bias=rb1_sb[:, 0:1]).then_inc(s_rh_ev, 1)
                act.wait_ge(s_sm, 2 * g + 1)
                nc.scalar.activation(sm[:, 1, :, :], sm[:, 0, :, :], ACT.Exp).then_inc(s_ex, 1)
                act.wait_ge(s_sm, 2 * g + 2)
                nc.scalar.activation(sv[:, 5, :], sv[:, 4, :], ACT.Exp).then_inc(s_ex, 1)
                for t in range(TG):
                    act.wait_ge(s_gtr_mm, 1 + TG * g + (t + 1))
                    nc.scalar.copy(colD[:, 0, t * TR:(t + 1) * TR], ps_tr[:, 0:TR]).then_inc(s_gtr_ev, 1)
            act.drain().then_inc(s_phase, 1)
            act.wait_ge(s_phase, 12)

            with act.Fori(0, NG) as g:
                for e in range(NX):
                    for layer, cout in enumerate((colB, colC)):
                        for part, (t0, n) in enumerate(PARTS):
                            for m in range(KC):
                                i = e * 8 + layer * 4 + part * KC + m
                                act.wait_ge(s_e_mm, 1 + NX * 8 * g + (i + 1))
                                nc.scalar.activation(cout[:, m, t0 * TR:(t0 + n) * TR], ps_big[:, i % 2, 0:n * TR],
                                                     ACT.Relu, bias=eb_sb[:, layer, e, m:m + 1]).then_inc(s_e_ev, 1)

        @block.vector
        def _(dve):
            dve.sem_inc(s_add, 4)
            for started in (s_key, s_q, s_att, s_kvsum, s_b3_add, s_lg, s_y_add, s_h2done, s_over_chunk):
                dve.sem_inc(started, 1)

            def bc(ap, shape):
                return ap.unsqueeze(len(shape) - 1).broadcast_to(shape)

            p = Links(dve, s_prep)
            dve.wait_ge(s_edges, 48)
            p.add(nc.vector.tensor_copy(src_f[:, :, :], src_i[:, :, :]))
            p.link(nc.vector.tensor_copy(dst_f[:, :, :], dst_i[:, :, :]))
            p.add(nc.vector.tensor_reduce(out=low_f[:, :], in_=dst_f[:, :, :], op=ALU.min, axis=AX))
            p.link(nc.vector.tensor_reduce(out=span_f[:, :], in_=dst_f[:, :, :], op=ALU.max, axis=AX))
            p.add(nc.vector.tensor_tensor(out=span_f[:, :], in0=span_f[:, :], in1=low_f[:, :], op=ALU.subtract))
            p.link(nc.vector.tensor_tensor(out=dst_f[:, :, :], in0=dst_f[:, :, :],
                                           in1=bc(low_f[:, :], [CR, ROWS, TR]), op=ALU.subtract))
            nc.vector.tensor_copy(low_i[:, 0, :], low_f[:, :]).then_inc(s_edge_ready, 1)
            nc.vector.tensor_copy(low_i[:, 1, :], span_f[:, :]).then_inc(s_edge_ready, 1)
            dve.wait_ge(s_ident, 2)
            p.add(nc.vector.tensor_copy(win_iota[:, :], win_iota_i[:, :]))
            p.add(nc.vector.memset(gate_pad[:, :, :], 0.0))
            dve.wait_ge(s_edge_tr, 3)
            nc.vector.tensor_copy(relT[:, :], ps_big[0:TR, 0, 0:NCH]).then_inc(s_lists, 1)
            nc.vector.tensor_copy(srcT[:, :], ps_big[0:TR, 1, 0:NCH]).then_inc(s_lists, 1)
            nc.vector.tensor_copy(wT[:, :], ps_att[0:TR, 0:NCH]).then_inc(s_lists, 1)

            with dve.Fori(0, NG) as g:
                ln = Links(dve, s_v0, 2 * TG + 1, g)
                hold(dve, "vector", s_x, 16 * g + 16)
                for t in range(TG):
                    ln.add(nc.vector.bn_stats(st_g[:, t, :], resid[:, bass.ds(g * TG + t, 1), :]))
                hold(dve, "vector", s_v0, ln.value())
                for t in range(TG):
                    ln.add(nc.vector.bn_aggr(mv_g[:, t, :], st_g[:, t, :]))
                ln.wait()
                ln.link(nc.vector.tensor_copy(mv_all[:, bass.ds(g * TG, TG), :], mv_g[:, :, :]))
                ln.close()
            ln = Links(dve, s_v0a)
            ln.link(nc.vector.tensor_scalar(ve_all[:, :], mv_all[:, :, 1], LN_EPS, None, ALU.add))
            rsqrt(nc, ln, rstd_all[:, :], ve_all[:, :], rtmp_all[:, :])
            with dve.Fori(0, NG) as g:
                dve.wait_ge(s_stored, 1 + g)
                dve.wait_ge(s_xn_tr, 1 + TG * g)
                for t in range(TG):
                    nc.vector.tensor_scalar(rowA[:, t, :], resid[:, bass.ds(g * TG + t, 1), :].squeeze(1),
                                            mv_all[:, bass.ds(g * TG + t, 1), 0], rstd_all[:, bass.ds(g * TG + t, 1)],
                                            ALU.subtract, ALU.mult).then_inc(s_xn, 1)
                dve.wait_ge(s_xn, TG * g + TG)
                nc.vector.tensor_tensor(out=resid[:, bass.ds(g * TG, TG), :], in0=resid[:, bass.ds(g * TG, TG), :],
                                        in1=rowA[:, :, :], op=ALU.add).then_inc(s_v0b, 1)
                dve.wait_ge(s_v0b, g + 1)

            def stage_edges(g, phase, cpg, ln):
                off = 2 * pairs_before(phase)
                ln.add(nc.vector.tensor_copy(rel_g[:, 0:cpg], relT[:, bass.ds(g * cpg + off, cpg)]))
                ln.link(nc.vector.tensor_copy(w_g[:, 0:cpg], wT[:, bass.ds(g * cpg + off, cpg)]))

            at = {}

            def build(g, phase, cpg, q):
                first = pairs_before(phase)
                dve.wait_ge(s_pair, g * (cpg // 2) + (first + q + RP - 1))
                for h in range(2):
                    c = 2 * q + h
                    last = nc.vector.tensor_scalar(onehot[:, c % 4, :], win_iota[:, :], rel_g[:, c:c + 1],
                                                   w_g[:, c:c + 1], ALU.is_equal, ALU.mult)
                last.then_inc(s_hot, 1)

            def add(g, phase, cpg, q):
                first = pairs_before(phase)
                if 2 * q % RING == 0:
                    at["starts"] = nc.values_load_multi_w_load_instructions(
                        low_row[0:1, 0, bass.ds(g * cpg + 2 * (first + q), RING)], engines=DVE_ONLY,
                        min_val=0, max_val=N - 1, skip_runtime_bounds_check_because="destinations are nodes")[1]
                dve.wait_ge(s_pair, g * (cpg // 2) + (first + q + RP + 1))
                for h in range(2):
                    c = 2 * q + h
                    w = accT[:, :, bass.ds(at["starts"][c % RING], WIN)]
                    dve.wait_ge(s_add, g * cpg + (2 * first + c + 4))
                    nc.vector.tensor_tensor(out=w, in0=w, in1=ps_agg[:, q % 2, h, :, :], op=ALU.add).then_inc(s_add, 1)

            dve.wait_ge(s_low_in, 16)
            dve.wait_ge(s_bc, 48)
            dve.wait_ge(s_zero, 4)
            ln = Links(dve, s_v0a)
            ln.k = 1 + 11
            ln.link(nc.vector.tensor_reduce(out=over_at[:, 0:1], in_=low_row[:, 1, :], op=ALU.max, axis=AX))
            nc.vector.tensor_copy(spill_i[:, :], over_at[:, 0:1]).then_inc(s_spill, 1)
            with dve.Fori(0, NG) as g:
                ln = Links(dve, s_v1, 4, g)
                stage_edges(g, 0, CPG0, ln)
                PP = CPG0 // 2
                for q in range(PP):
                    if q < TG:
                        dve.wait_ge(s_kv_ev, 1 + TG * g + (q + 1))
                        dve.wait_ge(s_kvp, 1 + TG * g)
                        nc.vector.scalar_tensor_tensor(out=rowB[:, q, :], in0=el_e[0:TR, q % 2, 0:D], scalar=1.0,
                                                       in1=el_r[0:TR, q % 2, 0:D], op0=ALU.min, op1=ALU.add
                                                       ).then_inc(s_key, 1)
                    build(g, 0, CPG0, q)
                    if q:
                        add(g, 0, CPG0, q - 1)
                add(g, 0, CPG0, PP - 1)
                ln.link(nc.vector.tensor_tensor(out=resid[:, bass.ds(g * TG, TG), :],
                                                in0=resid[:, bass.ds(g * TG, TG), :],
                                                in1=b2_bc[:, :].unsqueeze(1).broadcast_to([TR, TG, D]), op=ALU.add))
                dve.wait_ge(s_kvp, 1 + TG * g + TG)
                dve.wait_ge(s_kvsum, 1 + g)
                nc.vector.tensor_tensor(out=kv_acc[:, :, :], in0=kv_acc[:, :, :], in1=ps_row[:, :, 0:129],
                                        op=ALU.add).then_inc(s_kvsum, 1)
                dve.wait_ge(s_kvsum, 1 + g + 1)
                ln.link(nc.vector.memset(zr[:, :, :], 0.0))
                ln.close()
            for j in range(HPC):
                r = slice(HD * j, HD * (j + 1))
                nc.vector.tensor_copy(kv_bd[r, :, r], kv_acc[r, :, r])
                nc.vector.tensor_copy(kv_bd[r, :, 128 + j:129 + j], kv_acc[r, :, 128:129])
            dve.drain().then_inc(s_phase, 1)
            dve.wait_ge(s_phase, 3)

            with dve.Fori(0, NG) as g:
                BIG = 2 * KC + 2 * H1
                ln = Links(dve, s_v2, MIX_LINKS, g)

                def step(q):
                    if q < CPG1 // 2:
                        build(g, 1, CPG1, q)
                    if q:
                        add(g, 1, CPG1, q - 1)

                def query(part):
                    t0, n = PARTS[part]
                    for m in range(KC):
                        i = part * KC + m
                        dve.wait_ge(s_big_free, BIG * g + (2 + i + 1))
                        nc.vector.scalar_tensor_tensor(out=colB[:, m, t0 * TR:(t0 + n) * TR], in0=el_e[:, i % 2, 0:n * TR],
                                                       scalar=1.0, in1=el_r[:, i % 2, 0:n * TR], op0=ALU.min,
                                                       op1=ALU.add).then_inc(s_q, 1)

                def attend(t):
                    dve.wait_ge(s_att_mm, TG * g + (t + 1))
                    halves = ps_att[0:TR, 0:KC * HW].rearrange("p (c n) -> p c n", c=KC)
                    ln.link(nc.vector.tensor_scalar(zr[:, :, :], halves[:, :, 128:HW], ATT_EPS, 1.0 / N, ALU.add, ALU.mult))
                    ln.link(nc.vector.reciprocal(zr[:, :, :], zr[:, :, :]))
                    nc.vector.tensor_tensor(
                        out=rowB[:, t, :].rearrange("p (c j d) -> p c j d", c=KC, j=HPC),
                        in0=halves[:, :, 0:128].rearrange("p c (j d) -> p c j d", j=HPC),
                        in1=bc(zr[:, :, :], [TR, KC, HPC, HD]), op=ALU.mult).then_inc(s_att, 1)

                def stats(t, i):
                    dve.wait_ge(s_row_free, 2 * TG * g + (2 + i + 1))
                    ln.add(nc.vector.bn_stats(st_g[:, t, :], rowA[:, t, :]))

                def spread():
                    hold(dve, "vector", s_v2, ln.value())
                    for t in range(TG):
                        ln.add(nc.vector.bn_aggr(mv_g[:, t, :], st_g[:, t, :]))
                    ln.wait()
                    ln.link(nc.vector.tensor_scalar(ve_g[:, :], mv_g[:, :, 1], LN_EPS, None, ALU.add))
                    rsqrt(nc, ln, rs_g[:, :], ve_g[:, :], rt_g[:, :])

                stage_edges(g, 1, CPG1, ln)
                query(0)
                step(0)
                step(1)
                query(1)
                step(2)
                step(3)
                for t in range(TG + 2):
                    if t < TG:
                        attend(t)
                    if t >= 2:
                        stats(t - 2, t - 2)
                    step(4 + t)
                step(11)
                spread()
                for t in range(TG):
                    nc.vector.tensor_scalar(rowA[:, t, :], rowA[:, t, :], mv_g[:, t, 0:1], rs_g[:, t:t + 1],
                                            ALU.subtract, ALU.mult).then_inc(s_norm1, 1)
                for q in range(12, 28):
                    step(q)
                for t in range(TG):
                    stats(t, TG + t)
                    step(28 + t)
                spread()
                for t in range(TG):
                    ln.add(nc.vector.scalar_tensor_tensor(out=rowA[:, t, :], in0=rowA[:, t, :], scalar=mv_g[:, t, 0:1],
                                                          in1=g2_bc[:, :], op0=ALU.subtract, op1=ALU.mult))
                ln.wait()
                for t in range(TG):
                    tile = resid[:, bass.ds(g * TG + t, 1), :].squeeze(1)
                    nc.vector.scalar_tensor_tensor(out=tile, in0=rowA[:, t, :], scalar=rs_g[:, t:t + 1], in1=tile,
                                                   op0=ALU.mult, op1=ALU.add).then_inc(s_h2done, 1)
                ln.close()
            dve.drain().then_inc(s_phase, 1)
            dve.wait_ge(s_phase, 6)

            with dve.If(dve.value_load(spill_i[0:1, 0:1], min_val=0, max_val=N) > WIN - 1):
                with dve.Fori(0, NCH) as c:
                    head = Links(dve, s_over_v, 3 + 3 * (NT - 1), c)
                    head.add(nc.vector.tensor_copy(over_f[:, 0:1], relT[:, bass.ds(c, 1)]))
                    head.add(nc.vector.tensor_copy(over_f[:, 1:2], wT[:, bass.ds(c, 1)]))
                    head.add(nc.vector.tensor_copy(over_at[:, 0:1], low_row[:, 0, bass.ds(c, 1)]))
                    hold(dve, "vector", s_over_v, head.value())
                    with dve.Fori(0, NT - 1) as w:
                        k = (3 + 3 * (NT - 1)) * c + 3 * w
                        nc.vector.tensor_scalar(over_at[:, 0:1], over_at[:, 0:1], float(WIN), float(N), ALU.add,
                                                ALU.min).then_inc(s_over_v, 1)
                        nc.vector.tensor_scalar(over_f[:, 0:1], over_f[:, 0:1], float(-WIN), None,
                                                ALU.add).then_inc(s_over_v, 1)
                        dve.wait_ge(s_over_v, k + 5)
                        nc.vector.tensor_copy(over_i[:, 0:1], over_at[:, 0:1]).then_inc(s_over_v, 1)
                        nc.vector.tensor_scalar(onehot[:, 0, :], win_iota[:, :], over_f[:, 0:1], over_f[:, 1:2],
                                                ALU.is_equal, ALU.mult).then_inc(s_over_hot, 1)
                        hold(dve, "vector", s_over_v, k + 6)
                        start = dve.value_load(over_i[0:1, 0:1], min_val=0, max_val=N)
                        dve.wait_ge(s_over_mm, (NT - 1) * c + w + 1)
                        window = accT[:, :, bass.ds(start, WIN)]
                        nc.vector.tensor_tensor(out=window, in0=window, in1=ps_agg[:, 0, 0, :, :],
                                                op=ALU.add).then_inc(s_over_add, 1)
                        dve.wait_ge(s_over_add, (NT - 1) * c + w + 1)
                    dve.sem_inc(s_over_chunk, 1)
            dve.drain().then_inc(s_phase, 1)
            dve.wait_ge(s_phase, 9)

            with dve.Fori(0, NG) as g:
                ln = Links(dve, s_v2b, ROUTE_LINKS, g)

                def tile(t):
                    return resid[:, bass.ds(g * TG + t, 1), :].squeeze(1)

                dve.wait_ge(s_proj_ev, 1 + TG * g + TG)
                ln.link(nc.vector.tensor_scalar(ve_g[:, :], ve_g[:, :], NORM_EPS ** 2, None, ALU.max))
                rsqrt(nc, ln, rs_g[:, :], ve_g[:, :], rt_g[:, :])
                for t in range(TG):
                    ln.add(nc.vector.scalar_tensor_tensor(out=tile(t), in0=rowA[:, t, :], scalar=rs_g[:, t:t + 1],
                                                          in1=tile(t), op0=ALU.mult, op1=ALU.add))
                hold(dve, "vector", s_v2b, ln.value())
                for t in range(TG):
                    ln.add(nc.vector.bn_stats(st_g[:, t, :], tile(t)))
                hold(dve, "vector", s_v2b, ln.value())
                for t in range(TG):
                    ln.add(nc.vector.bn_aggr(mv_g[:, t, :], st_g[:, t, :]))
                ln.wait()
                ln.link(nc.vector.tensor_scalar(rs_g[:, :], mv_g[:, :, 1], LN_EPS, None, ALU.add))
                ln.link(nc.vector.tensor_copy(rt_g[:, :], rs_g[:, :]))
                rsqrt(nc, ln, rs_g[:, :], rt_g[:, :], zv_g[:, :])
                for t in range(TG):
                    nc.vector.tensor_scalar(rowA[:, t, :], tile(t), mv_g[:, t, 0:1], rs_g[:, t:t + 1],
                                            ALU.subtract, ALU.mult).then_inc(s_xn2, 1)

                shape = [TR, TG, NX]
                lg, ex, pr, o1, o2, tmp = (sm[:, k, :, :] for k in range(6))
                mx, rs, p1, p2, df, e2, r1, r2 = (sv[:, k, :] for k in range(8))
                dve.wait_ge(s_lg_mm, g + 1)
                nc.vector.tensor_tensor(out=lg, in0=ps_att[0:TR, 0:TG * NX].rearrange("p (t e) -> p t e", t=TG),
                                        in1=rb2_bc[:, :].unsqueeze(1).broadcast_to(shape), op=ALU.add).then_inc(s_lg, 1)
                dve.wait_ge(s_lg, 1 + g + 1)
                ln.link(nc.vector.tensor_reduce(out=mx, in_=lg, op=ALU.max, axis=AX))
                nc.vector.tensor_tensor(out=lg, in0=lg, in1=bc(mx, shape), op=ALU.subtract).then_inc(s_sm, 1)
                dve.wait_ge(s_ex, 2 * g + 1)
                ln.link(nc.vector.tensor_reduce(out=rs, in_=ex, op=ALU.add, axis=AX))
                ln.link(nc.vector.reciprocal(rs, rs))
                ln.link(nc.vector.tensor_tensor(out=pr, in0=ex, in1=bc(rs, shape), op=ALU.mult))

                def pick(values, top, one):
                    ln.link(nc.vector.tensor_reduce(out=top, in_=values, op=ALU.max, axis=AX))
                    ln.link(nc.vector.tensor_tensor(out=one, in0=values, in1=bc(top, shape), op=ALU.is_equal))
                    ln.link(nc.vector.tensor_tensor(out=one, in0=one, in1=rev[:, :].unsqueeze(1).broadcast_to(shape),
                                                    op=ALU.mult))
                    ln.link(nc.vector.tensor_reduce(out=mx, in_=one, op=ALU.max, axis=AX))
                    ln.link(nc.vector.tensor_tensor(out=one, in0=one, in1=bc(mx, shape), op=ALU.is_equal))

                pick(pr, p1, o1)
                ln.link(nc.vector.scalar_tensor_tensor(out=tmp, in0=o1, scalar=-2.0, in1=pr, op0=ALU.mult, op1=ALU.add))
                pick(tmp, p2, o2)
                nc.vector.tensor_tensor(out=df, in0=p2, in1=p1, op=ALU.subtract).then_inc(s_sm, 1)
                dve.wait_ge(s_ex, 2 * g + 2)
                ln.link(nc.vector.tensor_scalar(r1, e2, 1.0, None, ALU.add))
                ln.link(nc.vector.reciprocal(r1, r1))
                ln.link(nc.vector.tensor_tensor(out=r2, in0=e2, in1=r1, op=ALU.mult))
                ln.add(nc.vector.tensor_tensor(out=o1, in0=o1, in1=bc(r1, shape), op=ALU.mult))
                ln.link(nc.vector.tensor_tensor(out=o2, in0=o2, in1=bc(r2, shape), op=ALU.mult))
                dve.wait_ge(s_gtr_mm, 1 + TG * g)
                ln.add(nc.vector.tensor_tensor(out=gates_all[:, bass.ds(g * TG, TG), :], in0=o1, in1=o2, op=ALU.add))
                nc.vector.tensor_tensor(out=gate_pad[:, :, 0:NX], in0=o1, in1=o2, op=ALU.add).then_inc(s_gate, 1)
                for t in range(TG):
                    dve.wait_ge(s_b3_mm, TG * g + (t + 1))
                    nc.vector.tensor_tensor(out=tile(t), in0=tile(t), in1=ps_row[0:TR, t % 2, 0:D],
                                            op=ALU.add).then_inc(s_b3_add, 1)
                ln.close()
            dve.drain().then_inc(s_phase, 1)
            dve.wait_ge(s_phase, 12)

            with dve.Fori(0, NG) as g:
                dve.wait_ge(s_y_add, 1 + NX * TG * g)
                nc.vector.tensor_copy(gates_g[:, :, :], gates_all[:, bass.ds(g * TG, TG), :]).then_inc(s_v3, 1)
                dve.wait_ge(s_v3, g + 1)
                for e in range(NX):
                    for t in range(TG):
                        i = e * TG + t
                        tile = resid[:, bass.ds(g * TG + t, 1), :].squeeze(1)
                        dve.wait_ge(s_y_mm, NX * TG * g + (i + 1))
                        if e:
                            dve.wait_ge(s_y_add, 1 + NX * TG * g + (i + 1 - TG))
                        nc.vector.scalar_tensor_tensor(out=tile, in0=ps_row[0:TR, i % 2, 0:D],
                                                       scalar=gates_g[:, t, e:e + 1], in1=tile, op0=ALU.mult,
                                                       op1=ALU.add).then_inc(s_y_add, 1)


MIX_LINKS = 2 + 2 * 5 + 2 * (5 + 5 + 1 + 11) + 5
ROUTE_LINKS = 1 + 11 + 15 + 2 + 11 + 1 + 3 + 5 + 1 + 5 + 3 + 2 + 1


def _columns(a):
    import numpy as _np
    a = _np.asarray(a)
    return _np.ascontiguousarray(_np.moveaxis(a.reshape(a.shape[:-1] + (-1, 128)), -1, 0))


def kernel(**inputs):
    import numpy as _np
    import concourse.bacc as _bacc
    from concourse.bass_utils import run_bass_kernel_spmd as _run

    i = {k: _np.asarray(v) for k, v in inputs.items()}
    mix, ffn = "L0_mix_", "L0_ffn_"
    laid = {
        "x": i["x"], "src": i["src"], "dst": i["dst"], "edge_w": i["edge_weight"],
        "w_self_t": i["L0_gnn_w_self"].T, "w_neigh_t": i["L0_gnn_w_neigh"].T,
        "wq": i[mix + "Wq"], "wk": i[mix + "Wk"], "wv": i[mix + "Wv"], "wm": i[mix + "Wm"],
        "w1": i[mix + "W1"], "w2": i[mix + "W2"], "g1c": _columns(i[mix + "g1"]), "b1c": _columns(i[mix + "b1"]),
        "g2": i[mix + "g2"], "b2": i[mix + "b2"],
        "rw1": i[ffn + "router_w1"], "rb1c": _columns(i[ffn + "router_b1"]), "rw2": i[ffn + "router_w2"],
        "rb2": i[ffn + "router_b2"],
        "ew1": i[ffn + "expert_w1"], "eb1c": _columns(i[ffn + "expert_b1"]),
        "ew2": i[ffn + "expert_w2"], "eb2c": _columns(i[ffn + "expert_b2"]),
        "ew3": i[ffn + "expert_w3"], "eb3": i[ffn + "expert_b3"],
    }
    nc = _bacc.Bacc("TRN2", target_bir_lowering=False, num_devices=1)
    arrays, args = {}, []
    for name, a in laid.items():
        a = _np.ascontiguousarray(a)
        arrays[f"in_{name}"] = a
        args.append(nc.dram_tensor(f"in_{name}", a.shape, mybir.dt.from_np(a.dtype), kind="ExternalInput").ap())
    out = nc.dram_tensor("out_rows", i["x"].shape, F32, kind="ExternalOutput").ap()
    gps_layer_kernel(nc, *args, out)
    r = _run(nc, [arrays], core_ids=[0])
    return r.results[0]["out_rows"]
```

```python
from contextlib import ExitStack

import concourse.bass as bass
from concourse import mybir

F32 = mybir.dt.float32
I32 = mybir.dt.int32
ALU = mybir.AluOpType
ACT = mybir.ActivationFunctionType
AX = mybir.AxisListType.X
DVE_ONLY = (mybir.EngineType.DVE,)

LN_EPS = 1e-5
ATT_EPS = 1e-6
NORM_EPS = 1e-12
RSQRT_SEED = float(0x5F3759DF)


class Links:

    def __init__(self, eng, sem, per=0, i=0):
        self.eng, self.sem, self.per, self.i, self.k = eng, sem, per, i, 0

    def add(self, ins):
        ins.then_inc(self.sem, 1)
        self.k += 1

    def value(self):
        return self.i * self.per + self.k if self.per else self.k

    def wait(self):
        self.eng.wait_ge(self.sem, self.value())

    def link(self, ins):
        self.add(ins)
        self.wait()

    def close(self):
        assert self.k == self.per, (self.k, self.per)


def rsqrt(nc, ln, out, v, t):
    ln.link(nc.vector.tensor_scalar(t.bitcast(I32), v.bitcast(I32), 1, None, ALU.logical_shift_right))
    ln.link(nc.vector.tensor_scalar(out.bitcast(I32), t.bitcast(I32), -1.0, RSQRT_SEED, ALU.mult, ALU.add))
    for _ in range(3):
        ln.link(nc.vector.tensor_tensor(out=t, in0=out, in1=out, op=ALU.mult))
        ln.link(nc.vector.scalar_tensor_tensor(out=t, in0=t, scalar=-0.5, in1=v, op0=ALU.mult, op1=ALU.mult))
        ln.link(nc.vector.scalar_tensor_tensor(out=out, in0=t, scalar=1.5, in1=out, op0=ALU.add, op1=ALU.mult))


RSQRT_LINKS = 11


def gps_layer_kernel(nc, x, src, dst, edge_w, w_self_t, w_neigh_t, wq, wk, wv, wm, w1, w2, g1c, b1c, g2, b2,
                     rw1, rb1c, rw2, rb2, ew1, eb1c, ew2, eb2c, ew3, eb3, out):
    N, D = x.shape
    E = src.shape[0]
    TR, TG = 125, 5
    NT = N // TR
    NG = NT // TG
    GN = TG * TR
    KC = D // 128
    H1 = w1.shape[1] // 128
    HEADS, HD = 8, 32
    HPC = 128 // HD
    HW = 128 + HPC
    NX = ew1.shape[0]
    RH = rw1.shape[1]
    WIN = 64
    NCH = E // TR
    QC = 4
    NQ = NCH // QC
    RQ = 5
    RING = RQ * QC
    QPG0 = 5
    QPG1 = NQ // NG - QPG0
    AHEAD = 3
    ACCW = N + WIN + 3
    MORE = -(-N // WIN)
    PARTS = ((0, 3), (3, 2))
    MAXP = 3 * TR
    assert N == NT * TR and NT == NG * TG and E == NCH * TR and NCH == NQ * QC and NQ == NG * (QPG0 + QPG1)
    TILE_QUADS = ((), (1,), (), (2,), (), (3,), ())
    NORM_QUADS = (4, 5, 6)
    HIDDEN_QUADS = ((7,), (), (8,), (9,), (10,), (), (11,), ())
    PROJECT_QUADS = ((12,), (), (13,), (), (14,))
    assert QPG1 == 15 and QPG0 == TG
    SRC_QUADS = ((0, 1, 2), (3, 4))
    assert QPG0 % RQ == 0 and QPG1 % RQ == 0 and NQ <= 128 and RH == 128

    ctx = ExitStack()
    with ctx:
        def sb(name, shape, dt=F32):
            return ctx.enter_context(nc.sbuf_tensor(name, shape, dt))

        def pb(name, shape):
            return ctx.enter_context(nc.psum_tensor(name, shape, F32))

        def sem(name):
            return ctx.enter_context(nc.semaphore(name))

        xn_dram = nc.dram_tensor("xn_rows", (N, D), F32).ap()
        low_dram = nc.dram_tensor("window_starts", (2, NQ), I32).ap()

        ident = sb("ident", [128, 128])
        win_iota_i = sb("win_iota_i", [TR, WIN], I32)
        win_iota = sb("win_iota", [TR, WIN])
        g2_bc = sb("g2_bc", [TR, D])
        b2_bc = sb("b2_bc", [TR, D])
        rb2_bc = sb("rb2_bc", [TR, NX])
        rev = sb("rev", [TR, NX])
        mix_w = sb("mix_w", [128, 2 * KC * D + 2 * KC * D + 2 * KC * 2 * D + H1 * D])
        at = [0]

        def mix_weight(chunks, width):
            lo, at[0] = at[0], at[0] + chunks * width
            return mix_w[:, lo:at[0]].rearrange("p (c n) -> p c n", c=chunks)

        wkv_sb = mix_weight(KC, 2 * D)
        wq_sb = mix_weight(KC, D)
        wm_sb = mix_weight(KC, D)
        w1_sb = mix_weight(2 * KC, 2 * D)
        w2_sb = mix_weight(H1, D)
        g1_sb = sb("g1_sb", [128, KC])
        b1_sb = sb("b1_sb", [128, KC])
        ws_sb = sb("ws_sb", [128, KC, D])
        wn_sb = sb("wn_sb", [128, KC, D])
        rw1_sb = sb("rw1_sb", [128, KC, RH])
        rb1_sb = sb("rb1_sb", [128, 1])
        rw2_sb = sb("rw2_sb", [128, NX])
        eb_sb = sb("eb_sb", [128, 2, NX, KC])
        b3_sb = sb("b3_sb", [128, D])
        resid = sb("resid", [TR, NT, D])
        arena = sb("arena", [128, KC * (ACCW + N)])
        accT = arena[:, 0:KC * ACCW].rearrange("p (c n) -> p c n", c=KC)
        xnT = arena[:, KC * ACCW:KC * (ACCW + N)].rearrange("p (c n) -> p c n", c=KC)
        assert 2 * NX * KC * D <= KC * ACCW and NX * KC * D <= at[0]
        ew_sb = [arena[:, k * NX * KC * D:(k + 1) * NX * KC * D].rearrange("p (e c n) -> p e c n", e=NX, c=KC)
                 for k in range(2)]
        ew_sb.append(mix_w[:, 0:NX * KC * D].rearrange("p (e c n) -> p e c n", e=NX, c=KC))
        mv_all = sb("mv_all", [TR, NT, 2])
        ve_all = sb("ve_all", [TR, NT])
        rstd_all = sb("rstd_all", [TR, NT])
        rtmp_all = sb("rtmp_all", [TR, NT])
        gates_all = sb("gates_all", [TR, NT, NX])
        kv_acc = sb("kv_acc", [128, KC, 129])
        kv_bd = sb("kv_bd", [128, KC, HW])
        low_f = sb("low_f", [NQ, 1])
        span_f = sb("span_f", [NQ, 1])
        low_i = sb("low_i", [NQ, 2], I32)
        low_row = sb("low_row", [1, 2, NQ], I32)
        relT = sb("relT", [TR, NCH + AHEAD * QC])
        wT = sb("wT", [TR, NCH + AHEAD * QC])
        srcT = sb("srcT", [TR, NCH], I32)
        rel_g = sb("rel_g", [TR, QPG1 * QC])
        w_g = sb("w_g", [TR, QPG1 * QC])
        src_g = sb("src_g", [TR, RING], I32)
        msg = sb("msg", [TR, RING, D])
        onehot = sb("onehot", [TR, RING, WIN])
        colA = sb("colA", [128, KC, GN])
        colB = sb("colB", [128, KC, GN])
        colC = sb("colC", [128, KC, GN])
        colD = sb("colD", [128, KC, GN])
        hid = sb("hid", [128, H1, GN])
        def early(buf, k):
            return buf[0:NQ, k, 0:QC * TR]

        dst_i, src_i, ew_r, dst_f = early(hid, 0).bitcast(I32), early(hid, 1).bitcast(I32), early(hid, 2), early(hid, 3)
        src_f = early(colD, 0)
        rowA = sb("rowA", [TR, TG, D])
        rowB = sb("rowB", [TR, TG, D])
        v_g = sb("v_g", [TR, TG, KC, 129])
        el_e = sb("el_e", [128, 2, MAXP])
        el_r = sb("el_r", [128, 2, MAXP])
        st_g = sb("st_g", [TR, TG, 6])
        mv_g = sb("mv_g", [TR, TG, 2])
        ve_g = sb("ve_g", [TR, TG])
        rs_g = sb("rs_g", [TR, TG])
        rt_g = sb("rt_g", [TR, TG])
        gate_pad = sb("gate_pad", [TR, TG, 128])
        gates_g = sb("gates_g", [TR, TG, NX])
        sm = sb("sm", [TR, 6, NT, NX])
        sv = sb("sv", [TR, 8, NT])
        spill_i = sb("spill_i", [1, 1], I32)
        low_all = sb("low_all", [1, NCH])
        over_f = sb("over_f", [TR, 4])
        over_at = sb("over_at", [1, 2])
        over_i = sb("over_i", [1, 2], I32)
        st_all = sb("st_all", [TR, NT, 6])
        zv_g = sb("zv_g", [TR, TG])
        zr = sb("zr", [TR, KC, HPC])

        ps_agg = pb("ps_agg", [128, 2, 512])
        ps_big = pb("ps_big", [128, 2, 512])
        ps_att = pb("ps_att", [128, 512])
        ps_tr = pb("ps_tr", [128, 512])
        ps_row = pb("ps_row", [128, 2, 512])

        s_src_in = sem("s_src_in")
        s_edges = sem("s_edges")
        s_x = [sem(f"s_x{g}") for g in range(NG)]
        s_rows_out = [sem(f"s_rows_out{g}") for g in range(NG)]
        s_srcf = sem("s_srcf")
        s_wkv, s_wmix, s_wffn, s_bc = sem("s_wkv"), sem("s_wmix"), sem("s_wffn"), sem("s_bc")
        s_ident = sem("s_ident")
        s_id0 = sem("s_id0")
        s_prep = sem("s_prep")
        s_edge_ready = sem("s_edge_ready")
        s_edge_tr = sem("s_edge_tr")
        s_low_out, s_low_in = sem("s_low_out"), sem("s_low_in")
        s_srcT = sem("s_srcT")
        s_lists = sem("s_lists")
        s_v0, s_v0a, s_v0b = sem("s_v0"), sem("s_v0a"), sem("s_v0b")
        s_zero = sem("s_zero")
        s_xn = sem("s_xn")
        s_xn_tr = sem("s_xn_tr")
        s_xnT = sem("s_xnT")
        s_stage = sem("s_stage")
        s_kv_mm, s_kv_ev, s_key, s_kvp, s_kvsum = (sem("s_kv_mm"), sem("s_kv_ev"), sem("s_key"), sem("s_kvp"),
                                                   sem("s_kvsum"))
        s_src = sem("s_src")
        s_taken = sem("s_taken")
        s_held = {}
        s_msg = [sem(f"s_msg{k}") for k in range(RQ)]
        s_hot = sem("s_hot")
        s_quad = sem("s_quad")
        s_add = sem("s_add")
        s_v1 = sem("s_v1")
        s_bd = sem("s_bd")
        s_phase = sem("s_phase")
        s_big_mm = sem("s_big_mm")
        s_big_free = sem("s_big_free")
        s_q = sem("s_q")
        s_att_mm, s_att = sem("s_att_mm"), sem("s_att")
        s_tr_mm, s_tr_free = sem("s_tr_mm"), sem("s_tr_free")
        s_row_mm, s_row_free = sem("s_row_mm"), sem("s_row_free")
        s_norm1 = sem("s_norm1")
        s_h2done = sem("s_h2done")
        s_over_src, s_over_msg, s_over_hot, s_over_mm, s_over_add, s_over_v = (
            sem("s_over_src"), sem("s_over_msg"), sem("s_over_hot"), sem("s_over_mm"), sem("s_over_add"),
            sem("s_over_v"))
        s_v2, s_v2b = sem("s_v2"), sem("s_v2b")
        s_proj_mm, s_proj_ev, s_xn2, s_tr2_mm, s_tr2_ev = (sem("s_proj_mm"), sem("s_proj_ev"), sem("s_xn2"),
                                                          sem("s_tr2_mm"), sem("s_tr2_ev"))
        s_rh_mm, s_rh_ev, s_lg_mm, s_lg, s_ex, s_gate = (sem("s_rh_mm"), sem("s_rh_ev"), sem("s_lg_mm"),
                                                        sem("s_lg"), sem("s_ex"), sem("s_gate"))
        s_gtr_mm, s_gtr_ev, s_b3_mm, s_b3_add, s_back = (sem("s_gtr_mm"), sem("s_gtr_ev"), sem("s_b3_mm"),
                                                        sem("s_b3_add"), sem("s_back"))
        s_e_mm, s_e_ev, s_y_mm, s_y_add, s_v3, s_out = (sem("s_e_mm"), sem("s_e_ev"), sem("s_y_mm"), sem("s_y_add"),
                                                       sem("s_v3"), sem("s_out"))
        s_ew = sem("s_ew")
        s_colE = sem("s_colE")
        s_spill = sem("s_spill")
        s_sm, s_over_chunk = sem("s_sm"), sem("s_over_chunk")

        for name in ("sync", "gpsimd", "tensor", "vector"):
            s_held[name] = sem(f"s_held_{name}")

        def hold(eng, name, semaphore, value):
            eng.wait_ge(semaphore, value)
            eng.sem_inc(s_held[name], 1)

        x_t = x.rearrange("(n p) d -> p n d", p=TR)
        out_t = out.rearrange("(n p) d -> p n d", p=TR)
        xn_t = xn_dram.rearrange("(n p) d -> p n d", p=TR)

        def chunked(w):
            return w.rearrange("(c p) n -> p c n", p=128)

        def edge_rows(e):
            return e.rearrange("(p e) -> p e", e=QC * TR)

        xn_rows = [rowA[:, :, :], rowB[:, :, :]] + [msg[:, k * TG:(k + 1) * TG, :] for k in range(NG - 2)]
        assert RING >= (NG - 2) * TG

        pair_rows = (rowA, rowB)
        TURN_BANKS = (ps_tr, ps_agg[:, 0, :], ps_agg[:, 1, :])
        EXPERT_BANKS = (ps_big[:, 0, :], ps_big[:, 1, :], ps_agg[:, 0, :], ps_agg[:, 1, :])
        EVS = NX * 2 * len(PARTS) * KC
        ROWS = (NX + 1) * TG

        block = ctx.enter_context(nc.Block())

        def quads_before(phase):
            return 0 if phase == 0 else NG * QPG0

        @block.sync
        def _(sp):
            for g in range(NG):
                sp.dma_start(resid[:, g * TG:(g + 1) * TG, :], x_t[:, g * TG:(g + 1) * TG, :]).then_inc(s_x[g], 16)
            for g in range(NG):
                sp.wait_ge(s_xn, TG * g + TG)
                sp.dma_start(xn_t[:, g * TG:(g + 1) * TG, :], xn_rows[g]).then_inc(s_rows_out[g], 16)
            sp.wait_ge(s_edge_ready, 2)
            for k in range(2):
                sp.dma_start(low_dram[k:k + 1, :].rearrange("k p -> p k"), low_i[:, k:k + 1],
                             allow_slow_non_contiguous=True).then_inc(s_low_out, 16)
            sp.wait_ge(s_low_out, 32)
            sp.dma_start(low_row[:, :, :], low_dram.rearrange("(a k) n -> a k n", a=1)).then_inc(s_low_in, 16)
            sp.wait_ge(s_xnT, 1 + TG * NG)
            with sp.Fori(0, NG) as g:
                sp.wait_ge(s_kv_mm, 1 + TG * g)
                sp.dma_start(colA[:, :, :], xnT[:, :, bass.ds(g * GN, GN)]).then_inc(s_stage, 16)
            sp.wait_ge(s_ident, 3)
            for t, w in ((ws_sb[:, :, :], chunked(w_self_t)), (wn_sb[:, :, :], chunked(w_neigh_t)),
                         (rw1_sb[:, :, :], chunked(rw1)), (rb1_sb[:, :], rb1c), (rw2_sb[:, :], rw2),
                         (b3_sb[0:NX, :], eb3), (eb_sb[:, 0, :, :], eb1c), (eb_sb[:, 1, :, :], eb2c)):
                sp.dma_start(t, w).then_inc(s_wffn, 16)
            with sp.Fori(0, NG) as g:
                sp.wait_ge(s_kv_mm, 1 + TG * NG)
                sp.wait_ge(s_big_mm, 1 + (2 * KC + 2 * H1) * g)
                sp.dma_start(colA[:, :, :], xnT[:, :, bass.ds(g * GN, GN)]).then_inc(s_stage, 16)
            sp.wait_ge(s_phase, 6)
            for e in range(NX):
                sp.dma_start(ew_sb[2][:, e, :, :], chunked(ew3[e, :, :])).then_inc(s_ew, 16)
            sp.wait_ge(s_proj_mm, NT)
            for k, w in enumerate((ew1, ew2)):
                for e in range(NX):
                    sp.dma_start(ew_sb[k][:, e, :, :], chunked(w[e, :, :])).then_inc(s_ew, 16)
            with sp.Fori(0, NG) as g:
                sp.wait_ge(s_y_add, 1 + ROWS * g + ROWS)
                sp.dma_start(out_t[:, bass.ds(g * TG, TG), :], resid[:, bass.ds(g * TG, TG), :]).then_inc(s_out, 16)
            sp.wait_ge(s_out, 16 * NG)

        @block.gpsimd
        def _(pool):
            nc.gpsimd.memset(ident[:, :], 0.0).then_inc(s_id0, 1)
            pool.wait_ge(s_id0, 1)
            nc.gpsimd.affine_select(out=ident[:, :], in_=ident[:, :], compare_op=ALU.not_equal, fill=1.0, base=0,
                                    pattern=[[-1, 128]], channel_multiplier=1).then_inc(s_ident, 1)
            nc.gpsimd.iota(win_iota_i[:, :], pattern=[[1, WIN]], base=0, channel_multiplier=0).then_inc(s_ident, 1)
            nc.gpsimd.memset(b3_sb[:, :], 0.0).then_inc(s_ident, 1)
            for e in range(NX):
                nc.gpsimd.memset(rev[:, e:e + 1], float(NX - e))
            nc.gpsimd.memset(accT[:, :, :], 0.0).then_inc(s_zero, 1)
            nc.gpsimd.memset(v_g[:, :, :, :], 1.0).then_inc(s_zero, 1)
            nc.gpsimd.memset(kv_bd[:, :, :], 0.0).then_inc(s_zero, 1)
            nc.gpsimd.memset(kv_acc[:, :, :], 0.0).then_inc(s_zero, 1)

            pool.wait_ge(s_srcT, 1)
            for g in range(NG):
                pool.wait_ge(s_rows_out[g], 16)
            pool.wait_ge(s_v0b, NG - 2)
            pool.wait_ge(s_xn_tr, 1 + NT)

            def gathers(g, phase, qpg):
                first, blocks = quads_before(phase), qpg // RQ
                for b in range(blocks):
                    turn = blocks * g + (first // RQ + b)
                    for k, quads in enumerate(SRC_QUADS):
                        if k:
                            pool.wait_ge(s_quad, g * qpg + (first + b * RQ + quads[-1] + 1))
                        lo, n = quads[0] * QC, len(quads) * QC
                        nc.gpsimd.tensor_copy(src_g[:, lo:lo + n],
                                              srcT[:, bass.ds(g * (qpg * QC) + ((first + b * RQ) * QC + lo), n)]
                                              ).then_inc(s_src, 1)
                        pool.wait_ge(s_src, len(SRC_QUADS) * turn + (k + 1))
                        for q in quads:
                            hold(pool, "gpsimd", s_quad, g * qpg + (first + b * RQ + q + 1))
                            for c in range(q * QC, (q + 1) * QC):
                                nc.gpsimd.indirect_dma_start(
                                    out=msg[:, c, :], out_offset=None, in_=xn_dram[:, :],
                                    in_offset=bass.IndirectOffsetOnAxis(ap=src_g[:, c:c + 1], axis=0),
                                ).then_inc(s_msg[q], 16)
                    for q in SRC_QUADS[0]:
                        pool.wait_ge(s_msg[q], 16 * QC * turn + 16 * QC)

            with pool.Fori(0, NG) as g:
                gathers(g, 0, QPG0)
            with pool.Fori(0, NG) as g:
                gathers(g, 1, QPG1)

            pool.wait_ge(s_spill, 1)
            pool.wait_ge(s_phase, 6)
            with pool.If(pool.value_load(spill_i[0:1, 0:1], min_val=0, max_val=N) > WIN - 1):
                with pool.Fori(0, NCH) as c:
                    pool.wait_ge(s_over_chunk, 1 + c)
                    nc.gpsimd.tensor_copy(src_g[:, 0:1], srcT[:, bass.ds(c, 1)]).then_inc(s_over_src, 1)
                    hold(pool, "gpsimd", s_over_src, c + 1)
                    nc.gpsimd.indirect_dma_start(
                        out=msg[:, 0, :], out_offset=None, in_=xn_dram[:, :],
                        in_offset=bass.IndirectOffsetOnAxis(ap=src_g[:, 0:1], axis=0),
                    ).then_inc(s_over_msg, 16)

        @block.tensor
        def _(pe):
            pe.sem_inc(s_quad, RQ)
            for started in (s_kvp, s_kv_mm, s_big_mm, s_xn_tr):
                pe.sem_inc(started, 1)
            def turn_list(t, bank):
                for j in range(QC):
                    last = nc.tensor.transpose(bank[0:TR, j * NQ:(j + 1) * NQ], t[:, j * TR:(j + 1) * TR],
                                               ident[0:NQ, 0:NQ])
                last.then_inc(s_edge_tr, 1)

            pe.wait_ge(s_ident, 1)
            pe.wait_ge(s_srcf, 1)
            turn_list(src_f, ps_big[:, 1, :])
            for n in range(NT):
                pe.wait_ge(s_xn, n + 1)
                pe.wait_ge(s_xnT, 1 + max(n - 1, 0))
                for c in range(KC):
                    last = nc.tensor.transpose(ps_row[:, n % 2, c * TR:(c + 1) * TR],
                                               xn_rows[n // TG][:, n % TG, c * 128:(c + 1) * 128], ident[0:TR, 0:TR])
                last.then_inc(s_xn_tr, 1)
            pe.wait_ge(s_edges, 32)
            turn_list(ew_r, ps_att)
            pe.wait_ge(s_edge_ready, 1)
            turn_list(dst_f, ps_big[:, 0, :])

            def agg(g, phase, qpg, q):
                first = quads_before(phase)
                place = q % RQ
                pe.wait_ge(s_hot, g * qpg + (first + q + 1))
                pe.wait_ge(s_add, g * qpg + (first + max(q - 1, 0) + 1))
                pe.wait_ge(s_msg[place], 16 * QC * (qpg // RQ) * g + 16 * QC * (first // RQ + q // RQ + 1))
                for k in range(KC):
                    for c in range(QC):
                        last = nc.tensor.matmul(ps_agg[:, q % 2, k * WIN:(k + 1) * WIN],
                                                msg[:, place * QC + c, k * 128:(k + 1) * 128],
                                                onehot[:, place * QC + c, :], start=(c == 0), stop=(c == QC - 1))
                last.then_inc(s_quad, 1)

            pe.wait_ge(s_wkv, 32)
            pe.wait_ge(s_srcT, 1)
            pe.wait_ge(s_lists, 1)
            with pe.Fori(0, NG) as g:
                def key_value_product(t):
                    pe.wait_ge(s_key, 1 + TG * g + t + 1)
                    if t == 0:
                        pe.wait_ge(s_kvsum, 1 + g)
                    for c in range(KC):
                        last = nc.tensor.matmul(ps_row[:, c, 0:129], rowB[:, t, c * 128:(c + 1) * 128],
                                                v_g[:, t, c, :], start=(t == 0), stop=(t == TG - 1))
                    last.then_inc(s_kvp, 1)

                for t in range(TG):
                    if t == 0:
                        pe.wait_ge(s_xnT, 1 + TG * NG)
                        pe.wait_ge(s_stage, 16 * g + 16)
                    pe.wait_ge(s_kv_ev, 1 + TG * g + max(t - 1, 0))
                    for c in range(KC):
                        last = nc.tensor.matmul(ps_big[0:TR, t % 2, :], colA[:, c, t * TR:(t + 1) * TR],
                                                wkv_sb[:, c, :], start=(c == 0), stop=(c == KC - 1))
                    last.then_inc(s_kv_mm, 1)
                    if t:
                        key_value_product(t - 1)
                    agg(g, 0, QPG0, t)
                key_value_product(TG - 1)
            pe.drain().then_inc(s_phase, 1)
            pe.wait_ge(s_phase, 3)

            pe.wait_ge(s_wmix, 16 * 6)
            with pe.Fori(0, NG) as g:
                def a(*quads):
                    for q in quads:
                        agg(g, 1, QPG1, q)

                def queries(part):
                    t0, n = PARTS[part]
                    for m in range(KC):
                        i = part * KC + m
                        pe.wait_ge(s_big_free, (2 * KC + 2 * H1) * g + (i + 1))
                        for c in range(KC):
                            last = nc.tensor.matmul(ps_big[:, i % 2, 0:n * TR], wq_sb[:, c, m * 128:(m + 1) * 128],
                                                    colA[:, c, t0 * TR:(t0 + n) * TR], start=(c == 0), stop=(c == KC - 1))
                        last.then_inc(s_big_mm, 1)

                def attend(t):
                    pe.wait_ge(s_q, 1 + 2 * KC * g + (KC if t < PARTS[1][0] else 2 * KC))
                    pe.wait_ge(s_att, 1 + TG * g + t)
                    for c in range(KC):
                        last = nc.tensor.matmul(ps_att[0:TR, c * HW:(c + 1) * HW], colB[:, c, t * TR:(t + 1) * TR],
                                                kv_bd[:, c, :], start=True, stop=True)
                    last.then_inc(s_att_mm, 1)

                def turn(t, rows, ready, n, i):
                    pe.wait_ge(ready, n)
                    pe.wait_ge(s_tr_free, 1 + 2 * TG * g + i)
                    for c in range(KC):
                        last = nc.tensor.transpose(ps_tr[:, c * TR:(c + 1) * TR], rows[:, t, c * 128:(c + 1) * 128],
                                                   ident[0:TR, 0:TR])
                    last.then_inc(s_tr_mm, 1)

                def merge(t):
                    pe.wait_ge(s_tr_free, 1 + 2 * TG * g + (t + 1))
                    pe.wait_ge(s_row_free, 2 * TG * g + (t + 1))
                    for c in range(KC):
                        last = nc.tensor.matmul(ps_row[0:TR, t % 2, 0:D], colC[:, c, t * TR:(t + 1) * TR], wm_sb[:, c, :],
                                                start=(c == 0), stop=(c == KC - 1))
                    last.then_inc(s_row_mm, 1)

                def hidden(part):
                    t0, n = PARTS[part]
                    pe.wait_ge(s_tr_free, 1 + 2 * TG * g + (TG + t0 + n))
                    for m in range(H1):
                        i = 2 * KC + part * H1 + m
                        pe.wait_ge(s_big_free, (2 * KC + 2 * H1) * g + (i + 1))
                        for c in range(2 * KC):
                            col = colA if c < KC else colD
                            last = nc.tensor.matmul(ps_big[:, i % 2, 0:n * TR], w1_sb[:, c, m * 128:(m + 1) * 128],
                                                    col[:, c % KC, t0 * TR:(t0 + n) * TR],
                                                    start=(c == 0), stop=(c == 2 * KC - 1))
                        last.then_inc(s_big_mm, 1)
                        a(*HIDDEN_QUADS[part * H1 + m])

                def project(t):
                    i = TG + t
                    pe.wait_ge(s_big_free, (2 * KC + 2 * H1) * g + (2 + 2 * KC + (H1 if t < PARTS[1][0] else 2 * H1)))
                    pe.wait_ge(s_row_free, 2 * TG * g + (i + 1))
                    for c in range(H1):
                        last = nc.tensor.matmul(ps_row[0:TR, i % 2, 0:D], hid[:, c, t * TR:(t + 1) * TR], w2_sb[:, c, :],
                                                start=(c == 0), stop=(c == H1 - 1))
                    last.then_inc(s_row_mm, 1)

                pe.wait_ge(s_stage, 16 * g + 16 * (NG + 1))
                queries(0)
                a(0)
                queries(1)
                for t in range(TG + 2):
                    if t < TG:
                        attend(t)
                    if 1 <= t <= TG:
                        turn(t - 1, rowB, s_att, 1 + TG * g + t, t - 1)
                    if t >= 2:
                        merge(t - 2)
                    a(*TILE_QUADS[t])
                a(*NORM_QUADS)
                for t in range(TG):
                    turn(t, rowA, s_norm1, TG * g + (t + 1), TG + t)
                hidden(0)
                hidden(1)
                for t in range(TG):
                    project(t)
                    a(*PROJECT_QUADS[t])
            pe.drain().then_inc(s_phase, 1)
            pe.wait_ge(s_phase, 6)

            pe.wait_ge(s_spill, 1)
            with pe.If(pe.value_load(spill_i[0:1, 0:1], min_val=0, max_val=N) > WIN - 1):
                with pe.Fori(0, NCH) as c:
                    hold(pe, "tensor", s_over_msg, 16 * c + 16)
                    with pe.Fori(0, MORE) as w:
                        pe.wait_ge(s_over_hot, MORE * c + w + 1)
                        for k in range(KC):
                            last = nc.tensor.matmul(ps_agg[:, 0, k * WIN:(k + 1) * WIN], msg[:, 0, k * 128:(k + 1) * 128],
                                                    onehot[:, 0, :], start=True, stop=True)
                        last.then_inc(s_over_mm, 1)
            pe.drain().then_inc(s_phase, 1)
            pe.wait_ge(s_phase, 8)

            pe.wait_ge(s_wffn, 16 * 8)
            for g in range(NG + 2):
                if g < NG:
                    for n in range(g * TG, (g + 1) * TG):
                        if n >= 2:
                            pe.wait_ge(s_proj_ev, n - 1)
                        rows = slice(n * TR, (n + 1) * TR)
                        for k, (col, w) in enumerate(((xnT, ws_sb), (accT, wn_sb))):
                            for c in range(KC):
                                last = nc.tensor.matmul(ps_row[0:TR, n % 2, 0:D], col[:, c, rows], w[:, c, :],
                                                        start=(k == 0 and c == 0), stop=(k == 1 and c == KC - 1))
                        last.then_inc(s_proj_mm, 1)
                if g >= 2:
                    pe.wait_ge(s_rh_ev, 2 * (g - 1))
                    for n in range((g - 2) * TG, (g - 1) * TG):
                        t = n % TG
                        last = nc.tensor.matmul(ps_att[0:TR, n * NX:(n + 1) * NX], hid[:, (g - 1) % 2, t * TR:(t + 1) * TR],
                                                rw2_sb[:, :], start=True, stop=True)
                    last.then_inc(s_lg_mm, 1)
                if 1 <= g <= NG:
                    for n in range((g - 1) * TG, g * TG):
                        pe.wait_ge(s_xn2, n + 1)
                        if n >= 3:
                            pe.wait_ge(s_tr2_ev, n - 2)
                        for c in range(KC):
                            last = nc.tensor.transpose(TURN_BANKS[n % 3][:, c * TR:(c + 1) * TR],
                                                       pair_rows[(g - 1) % 2][:, n % TG, c * 128:(c + 1) * 128],
                                                       ident[0:TR, 0:TR])
                        last.then_inc(s_tr2_mm, 1)
                    for part, (t0, n) in enumerate(PARTS):
                        pe.wait_ge(s_tr2_ev, (g - 1) * TG + t0 + n)
                        if g > 1:
                            pe.wait_ge(s_rh_ev, 2 * (g - 2) + part + 1)
                        lo = ((g - 1) * TG + t0) * TR
                        for c in range(KC):
                            last = nc.tensor.matmul(ps_big[:, part, 0:n * TR], rw1_sb[:, c, :], xnT[:, c, lo:lo + n * TR],
                                                    start=(c == 0), stop=(c == KC - 1))
                        last.then_inc(s_rh_mm, 1)

            pe.wait_ge(s_rh_ev, 2 * NG)
            pe.wait_ge(s_ew, 16 * 3 * NX)
            with pe.Fori(0, NG) as g:
                for e in range(NX):
                    for layer in range(2):
                        for part, (t0, n) in enumerate(PARTS):
                            for m in range(KC):
                                i = e * 8 + layer * 4 + part * KC + m
                                pe.wait_ge(s_e_ev, EVS * g + (i + 1))
                                if layer:
                                    pe.wait_ge(s_e_ev, 4 + EVS * g + (e * 8 + (part + 1) * KC))
                                for c in range(KC):
                                    cin = (colB[:, c, t0 * TR:(t0 + n) * TR] if layer else
                                           xnT[:, c, bass.ds(g * GN + t0 * TR, n * TR)])
                                    last = nc.tensor.matmul(EXPERT_BANKS[i % 4][:, 0:n * TR],
                                                            ew_sb[layer][:, e, c, m * 128:(m + 1) * 128],
                                                            cin, start=(c == 0), stop=(c == KC - 1))
                                last.then_inc(s_e_mm, 1)
                    if e == 0:
                        pe.wait_ge(s_gate, g + 1)
                        for part, (t0, n) in enumerate(PARTS):
                            for t in range(n):
                                last = nc.tensor.transpose((ps_tr, ps_att)[part][:, t * TR:(t + 1) * TR],
                                                           gate_pad[:, t0 + t, :], ident[0:TR, 0:TR])
                            last.then_inc(s_gtr_mm, 1)
                    for t in range(TG):
                        i = (e + (e > 0)) * TG + t
                        pe.wait_ge(s_e_ev, 4 + EVS * g + (e * 8 + 4 + (KC if t < PARTS[1][0] else 2 * KC)))
                        pe.wait_ge(s_y_add, 1 + ROWS * g + max(i - 1, 0))
                        for c in range(KC):
                            last = nc.tensor.matmul(ps_row[0:TR, i % 2, 0:D], colC[:, c, t * TR:(t + 1) * TR],
                                                    ew_sb[2][:, e, c, :], start=(c == 0), stop=(c == KC - 1))
                        last.then_inc(s_y_mm, 1)
                    if e == 0:
                        for t in range(TG):
                            i = TG + t
                            pe.wait_ge(s_gtr_ev, 2 * g + (1 if t < PARTS[1][0] else 2))
                            pe.wait_ge(s_y_add, 1 + ROWS * g + (i - 1))
                            nc.tensor.matmul(ps_row[0:TR, i % 2, 0:D], colD[:, 0, t * TR:(t + 1) * TR], b3_sb[:, :],
                                             start=True, stop=True).then_inc(s_y_mm, 1)

        @block.scalar
        def _(act):
            act.sem_inc(s_big_free, 2)
            act.sem_inc(s_row_free, 2)
            for started in (s_xnT, s_kv_ev, s_tr_free):
                act.sem_inc(started, 1)
            act.sem_inc(s_e_ev, 4)

            def cols(ps):
                return ps.rearrange("p (c n) -> p c n", c=KC)

            for k, (e, t) in enumerate(((src, src_i), (dst, dst_i), (edge_w, ew_r))):
                act.dma_start(t, edge_rows(e)).then_inc(s_src_in if k == 0 else s_edges, 16)
            for k, (t, w) in enumerate(((wkv_sb[:, :, 0:D], chunked(wk)), (wkv_sb[:, :, D:2 * D], chunked(wv)))):
                act.dma_start(t, w).then_inc(s_wkv, 16)
            for t, w in ((g2_bc, g2), (b2_bc, b2), (rb2_bc, rb2)):
                act.dma_start(t[:, :], w.partition_broadcast(TR)).then_inc(s_bc, 16)
            for t, w in ((wq_sb, chunked(wq)), (wm_sb, chunked(wm)), (w1_sb, chunked(w1)), (w2_sb, chunked(w2)),
                         (g1_sb, g1c), (b1_sb, b1c)):
                act.dma_start(t[:, :] if len(t.shape) == 2 else t[:, :, :], w).then_inc(s_wmix, 16)
            act.wait_ge(s_src_in, 16)
            nc.scalar.copy(src_f, src_i).then_inc(s_srcf, 1)
            act.wait_ge(s_edge_tr, 1)
            nc.scalar.copy(srcT[:, :].rearrange("p (q j) -> p j q", j=QC),
                           ps_big[0:TR, 1, 0:NCH].rearrange("p (j q) -> p j q", j=QC)).then_inc(s_srcT, 1)
            for n in range(NT):
                act.wait_ge(s_xn_tr, 1 + n + 1)
                nc.scalar.copy(xnT[:, :, n * TR:(n + 1) * TR], cols(ps_row[:, n % 2, 0:KC * TR])).then_inc(s_xnT, 1)

            act.wait_ge(s_zero, 4)
            with act.Fori(0, NG) as g:
                for t in range(TG):
                    act.wait_ge(s_kv_mm, 1 + TG * g + (t + 1))
                    act.wait_ge(s_key, 1 + TG * g + max(t - 1, 0))
                    act.wait_ge(s_kvp, 1 + TG * g)
                    nc.scalar.activation(el_e[0:TR, t % 2, 0:D], ps_big[0:TR, t % 2, 0:D], ACT.Exp)
                    nc.scalar.activation(el_r[0:TR, t % 2, 0:D], ps_big[0:TR, t % 2, 0:D], ACT.Relu)
                    nc.scalar.activation(v_g[:, t, :, 0:128], cols(ps_big[0:TR, t % 2, D:2 * D]), ACT.Copy,
                                         scale=1.0 / N).then_inc(s_kv_ev, 1)
            act.drain().then_inc(s_phase, 1)
            act.wait_ge(s_phase, 3)

            act.wait_ge(s_wmix, 16 * 6)
            with act.Fori(0, NG) as g:
                BIG = 2 * KC + 2 * H1

                def query(part):
                    t0, n = PARTS[part]
                    for m in range(KC):
                        i = part * KC + m
                        act.wait_ge(s_big_mm, 1 + BIG * g + (i + 1))
                        act.wait_ge(s_q, 1 + 2 * KC * g + max(i - 1, 0))
                        nc.scalar.activation(el_e[:, i % 2, 0:n * TR], ps_big[:, i % 2, 0:n * TR], ACT.Exp)
                        nc.scalar.activation(el_r[:, i % 2, 0:n * TR], ps_big[:, i % 2, 0:n * TR],
                                             ACT.Relu).then_inc(s_big_free, 1)

                query(0)
                query(1)
                for t in range(1, TG + 2):
                    if t <= TG:
                        act.wait_ge(s_tr_mm, 2 * TG * g + t)
                        nc.scalar.copy(colC[:, :, (t - 1) * TR:t * TR], cols(ps_tr[:, 0:KC * TR])).then_inc(s_tr_free, 1)
                    if t >= 2:
                        act.wait_ge(s_row_mm, 2 * TG * g + (t - 1))
                        act.wait_ge(s_h2done, 1 + TG * g)
                        nc.scalar.copy(rowA[:, t - 2, :], ps_row[0:TR, t % 2, 0:D]).then_inc(s_row_free, 1)
                for t in range(TG):
                    act.wait_ge(s_tr_mm, 2 * TG * g + (TG + t + 1))
                    for c in range(KC):
                        last = nc.scalar.activation(colD[:, c, t * TR:(t + 1) * TR], ps_tr[:, c * TR:(c + 1) * TR],
                                                    ACT.Identity, bias=b1_sb[:, c:c + 1], scale=g1_sb[:, c:c + 1])
                    last.then_inc(s_tr_free, 1)
                for part, (t0, n) in enumerate(PARTS):
                    for m in range(H1):
                        i = 2 * KC + part * H1 + m
                        act.wait_ge(s_big_mm, 1 + BIG * g + (i + 1))
                        nc.scalar.activation(hid[:, m, t0 * TR:(t0 + n) * TR], ps_big[:, i % 2, 0:n * TR],
                                             ACT.Relu).then_inc(s_big_free, 1)
                for t in range(TG):
                    act.wait_ge(s_row_mm, 2 * TG * g + (TG + t + 1))
                    nc.scalar.copy(rowA[:, t, :], ps_row[0:TR, (TG + t) % 2, 0:D]).then_inc(s_row_free, 1)
            act.drain().then_inc(s_phase, 1)
            act.wait_ge(s_phase, 6)
            act.wait_ge(s_wffn, 16 * 8)
            for g in range(NG + 1):
                if g < NG:
                    for n in range(g * TG, (g + 1) * TG):
                        act.wait_ge(s_proj_mm, n + 1)
                        if g >= 2:
                            act.wait_ge(s_tr2_mm, (g - 1) * TG)
                        nc.scalar.copy(pair_rows[g % 2][:, n % TG, :], ps_row[0:TR, n % 2, 0:D])
                        nc.scalar.activation(msg[:, n % RING, :], ps_row[0:TR, n % 2, 0:D], ACT.Square,
                                             accum_out=ve_all[:, n:n + 1]).then_inc(s_proj_ev, 1)
                if g:
                    for n in range((g - 1) * TG, g * TG):
                        act.wait_ge(s_tr2_mm, n + 1)
                        nc.scalar.copy(xnT[:, :, n * TR:(n + 1) * TR], cols(TURN_BANKS[n % 3][:, 0:KC * TR])
                                       ).then_inc(s_tr2_ev, 1)
                    for part, (t0, n) in enumerate(PARTS):
                        act.wait_ge(s_rh_mm, 2 * (g - 1) + (part + 1))
                        if g > 2:
                            act.wait_ge(s_lg_mm, g - 2)
                        nc.scalar.activation(hid[:, g % 2, t0 * TR:(t0 + n) * TR], ps_big[:, part, 0:n * TR], ACT.Relu,
                                             bias=rb1_sb[:, 0:1]).then_inc(s_rh_ev, 1)
            act.wait_ge(s_sm, 1)
            nc.scalar.activation(sm[:, 1, :, :], sm[:, 0, :, :], ACT.Exp).then_inc(s_ex, 1)
            act.wait_ge(s_sm, 2)
            nc.scalar.activation(sv[:, 5, :], sv[:, 4, :], ACT.Exp).then_inc(s_ex, 1)

            with act.Fori(0, NG) as g:
                for e in range(NX):
                    for layer, cout in enumerate((colB, colC)):
                        for part, (t0, n) in enumerate(PARTS):
                            for m in range(KC):
                                i = e * 8 + layer * 4 + part * KC + m
                                act.wait_ge(s_e_mm, EVS * g + (i + 1))
                                nc.scalar.activation(cout[:, m, t0 * TR:(t0 + n) * TR], EXPERT_BANKS[i % 4][:, 0:n * TR],
                                                     ACT.Relu, bias=eb_sb[:, layer, e, m:m + 1]).then_inc(s_e_ev, 1)
                    if e == 0:
                        for part, (t0, n) in enumerate(PARTS):
                            act.wait_ge(s_gtr_mm, 2 * g + (part + 1))
                            nc.scalar.copy(colD[:, 0, t0 * TR:(t0 + n) * TR], (ps_tr, ps_att)[part][:, 0:n * TR]
                                           ).then_inc(s_gtr_ev, 1)

        @block.vector
        def _(dve):
            dve.sem_inc(s_add, 1)
            for started in (s_key, s_q, s_att, s_kvsum, s_y_add, s_h2done, s_over_chunk):
                dve.sem_inc(started, 1)

            def bc(ap, shape):
                return ap.unsqueeze(len(shape) - 1).broadcast_to(shape)

            ln = Links(dve, s_v0)
            for g in range(NG):
                dve.wait_ge(s_x[g], 16)
                for t in range(TG):
                    ln.add(nc.vector.bn_stats(st_all[:, g * TG + t, :], resid[:, g * TG + t, :]))
            for n in range(NT):
                if n == 0:
                    ln.wait()
                ln.add(nc.vector.bn_aggr(mv_all[:, n, :], st_all[:, n, :]))
            ln.wait()
            ln.link(nc.vector.tensor_scalar(ve_all[:, :], mv_all[:, :, 1], LN_EPS, None, ALU.add))
            rsqrt(nc, ln, rstd_all[:, :], ve_all[:, :], rtmp_all[:, :])
            for n in range(NT):
                nc.vector.tensor_scalar(xn_rows[n // TG][:, n % TG, :], resid[:, n, :], mv_all[:, n, 0:1],
                                        rstd_all[:, n:n + 1], ALU.subtract, ALU.mult).then_inc(s_xn, 1)
            p = Links(dve, s_prep)
            dve.wait_ge(s_edges, 32)
            p.link(nc.vector.tensor_copy(dst_f, dst_i))
            p.add(nc.vector.tensor_reduce(out=low_f[:, :], in_=dst_f, op=ALU.min, axis=AX))
            p.link(nc.vector.tensor_reduce(out=span_f[:, :], in_=dst_f, op=ALU.max, axis=AX))
            p.add(nc.vector.tensor_tensor(out=span_f[:, :], in0=span_f[:, :], in1=low_f[:, :], op=ALU.subtract))
            nc.vector.tensor_scalar(dst_f, dst_f, low_f[:, 0:1], None, ALU.subtract).then_inc(s_edge_ready, 1)
            p.wait()
            p.add(nc.vector.tensor_copy(low_i[:, 0:1], low_f[:, :]))
            nc.vector.tensor_copy(low_i[:, 1:2], span_f[:, :]).then_inc(s_edge_ready, 1)
            for g in (*range(2, NG), 0, 1):
                dve.wait_ge(s_xn, NT)
                nc.vector.tensor_tensor(out=resid[:, g * TG:(g + 1) * TG, :], in0=resid[:, g * TG:(g + 1) * TG, :],
                                        in1=xn_rows[g], op=ALU.add).then_inc(s_v0b, 1)
            dve.wait_ge(s_ident, 2)
            p.add(nc.vector.tensor_copy(win_iota[:, :], win_iota_i[:, :]))
            p.add(nc.vector.memset(gate_pad[:, :, :], 0.0))
            p.add(nc.vector.memset(relT[:, NCH:NCH + AHEAD * QC], -1.0))
            p.add(nc.vector.memset(wT[:, NCH:NCH + AHEAD * QC], 0.0))
            dve.wait_ge(s_edge_tr, 3)
            for t, bank in ((relT, ps_big[0:TR, 0, 0:NCH]), (wT, ps_att[0:TR, 0:NCH])):
                p.add(nc.vector.tensor_copy(t[:, 0:NCH].rearrange("p (q j) -> p j q", j=QC),
                                            bank.rearrange("p (j q) -> p j q", j=QC)))
            p.wait()
            nc.vector.memset(zr[:, :, :], 0.0).then_inc(s_lists, 1)

            def stage_edges(g, phase, qpg, ln):
                n, off = qpg * QC, (quads_before(phase) + AHEAD) * QC
                dve.wait_ge(s_hot, g * qpg + (quads_before(phase) + AHEAD))
                ln.add(nc.vector.tensor_copy(rel_g[:, 0:n], relT[:, bass.ds(g * n + off, n)]))
                ln.link(nc.vector.tensor_copy(w_g[:, 0:n], wT[:, bass.ds(g * n + off, n)]))

            spots = {}

            def build(place, c0):
                for c in range(QC):
                    last = nc.vector.tensor_scalar(onehot[:, place * QC + c, :], win_iota[:, :], rel_g[:, c0 + c:c0 + c + 1],
                                                   w_g[:, c0 + c:c0 + c + 1], ALU.is_equal, ALU.mult)
                last.then_inc(s_hot, 1)

            def step(g, phase, qpg, q):
                first = quads_before(phase)
                if q < qpg:
                    dve.wait_ge(s_quad, g * qpg + (first + q + AHEAD + 1))
                    build((q + AHEAD) % RQ, q * QC)
                if not q:
                    return
                q -= 1
                if q % RQ == 0:
                    spots["starts"] = nc.values_load_multi_w_load_instructions(
                        low_row[0:1, 0, bass.ds(g * qpg + first + q, RQ)], engines=DVE_ONLY,
                        min_val=0, max_val=N - 1, skip_runtime_bounds_check_because="destinations are nodes")[1]
                w = accT[:, :, bass.ds(spots["starts"][q % RQ], WIN)]
                dve.wait_ge(s_quad, g * qpg + (first + q + RQ + 1))
                dve.wait_ge(s_add, g * qpg + (first + q + 1))
                nc.vector.tensor_tensor(out=w, in0=w,
                                        in1=ps_agg[:, q % 2, 0:KC * WIN].rearrange("p (k n) -> p k n", k=KC),
                                        op=ALU.add).then_inc(s_add, 1)

            dve.wait_ge(s_low_in, 16)
            dve.wait_ge(s_bc, 48)
            dve.wait_ge(s_zero, 4)
            ln = Links(dve, s_v0a)
            ln.link(nc.vector.tensor_reduce(out=over_at[:, 0:1], in_=low_row[:, 1, :], op=ALU.max, axis=AX))
            nc.vector.tensor_copy(spill_i[:, :], over_at[:, 0:1]).then_inc(s_spill, 1)
            ln.add(nc.vector.tensor_copy(low_all[:, :].rearrange("p (q j) -> p q j", j=QC),
                                         low_row[:, 0, :].unsqueeze(2).broadcast_to([1, NQ, QC])))
            ln.add(nc.vector.tensor_copy(rel_g[:, 0:AHEAD * QC], relT[:, 0:AHEAD * QC]))
            ln.link(nc.vector.tensor_copy(w_g[:, 0:AHEAD * QC], wT[:, 0:AHEAD * QC]))
            for q in range(AHEAD):
                build(q, q * QC)
            with dve.Fori(0, NG) as g:
                ln = Links(dve, s_v1, 3, g)
                stage_edges(g, 0, QPG0, ln)
                for q in range(TG):
                    step(g, 0, QPG0, q)
                    dve.wait_ge(s_kv_ev, 1 + TG * g + (q + 1))
                    dve.wait_ge(s_kvp, 1 + TG * g)
                    nc.vector.scalar_tensor_tensor(out=rowB[:, q, :], in0=el_e[0:TR, q % 2, 0:D], scalar=1.0,
                                                   in1=el_r[0:TR, q % 2, 0:D], op0=ALU.min, op1=ALU.add
                                                   ).then_inc(s_key, 1)
                ln.link(nc.vector.tensor_tensor(out=resid[:, bass.ds(g * TG, TG), :],
                                                in0=resid[:, bass.ds(g * TG, TG), :],
                                                in1=b2_bc[:, :].unsqueeze(1).broadcast_to([TR, TG, D]), op=ALU.add))
                step(g, 0, QPG0, QPG0)
                dve.wait_ge(s_kvp, 1 + TG * g + TG)
                dve.wait_ge(s_kvsum, 1 + g)
                nc.vector.tensor_tensor(out=kv_acc[:, :, :], in0=kv_acc[:, :, :], in1=ps_row[:, :, 0:129],
                                        op=ALU.add).then_inc(s_kvsum, 1)
                dve.wait_ge(s_kvsum, 1 + g + 1)
                ln.close()
            for j in range(HPC):
                r = slice(HD * j, HD * (j + 1))
                nc.vector.tensor_copy(kv_bd[r, :, r], kv_acc[r, :, r])
                nc.vector.tensor_copy(kv_bd[r, :, 128 + j:129 + j], kv_acc[r, :, 128:129])
            dve.drain().then_inc(s_phase, 1)
            dve.wait_ge(s_phase, 3)

            with dve.Fori(0, NG) as g:
                BIG = 2 * KC + 2 * H1
                ln = Links(dve, s_v2, MIX_LINKS, g)

                def a(*quads):
                    for q in quads:
                        step(g, 1, QPG1, q)

                def query(part):
                    t0, n = PARTS[part]
                    for m in range(KC):
                        i = part * KC + m
                        dve.wait_ge(s_big_free, BIG * g + (2 + i + 1))
                        nc.vector.scalar_tensor_tensor(out=colB[:, m, t0 * TR:(t0 + n) * TR], in0=el_e[:, i % 2, 0:n * TR],
                                                       scalar=1.0, in1=el_r[:, i % 2, 0:n * TR], op0=ALU.min,
                                                       op1=ALU.add).then_inc(s_q, 1)

                def attend(t):
                    dve.wait_ge(s_att_mm, TG * g + (t + 1))
                    halves = ps_att[0:TR, 0:KC * HW].rearrange("p (c n) -> p c n", c=KC)
                    ln.link(nc.vector.tensor_scalar(zr[:, :, :], halves[:, :, 128:HW], ATT_EPS, 1.0 / N, ALU.add, ALU.mult))
                    ln.link(nc.vector.reciprocal(zr[:, :, :], zr[:, :, :]))
                    nc.vector.tensor_tensor(
                        out=rowB[:, t, :].rearrange("p (c j d) -> p c j d", c=KC, j=HPC),
                        in0=halves[:, :, 0:128].rearrange("p c (j d) -> p c j d", j=HPC),
                        in1=bc(zr[:, :, :], [TR, KC, HPC, HD]), op=ALU.mult).then_inc(s_att, 1)

                def stats(t, i):
                    dve.wait_ge(s_row_free, 2 * TG * g + (2 + i + 1))
                    ln.add(nc.vector.bn_stats(st_g[:, t, :], rowA[:, t, :]))

                def spread():
                    hold(dve, "vector", s_v2, ln.value())
                    for t in range(TG):
                        ln.add(nc.vector.bn_aggr(mv_g[:, t, :], st_g[:, t, :]))
                    ln.wait()
                    ln.link(nc.vector.tensor_scalar(ve_g[:, :], mv_g[:, :, 1], LN_EPS, None, ALU.add))
                    rsqrt(nc, ln, rs_g[:, :], ve_g[:, :], rt_g[:, :])

                stage_edges(g, 1, QPG1, ln)
                query(0)
                a(0)
                query(1)
                for t in range(TG + 2):
                    if t < TG:
                        attend(t)
                    if t >= 2:
                        stats(t - 2, t - 2)
                    a(*TILE_QUADS[t])
                spread()
                for t in range(TG):
                    nc.vector.tensor_scalar(rowA[:, t, :], rowA[:, t, :], mv_g[:, t, 0:1], rs_g[:, t:t + 1],
                                            ALU.subtract, ALU.mult).then_inc(s_norm1, 1)
                a(*NORM_QUADS)
                for quads in HIDDEN_QUADS:
                    a(*quads)
                for t in range(TG):
                    stats(t, TG + t)
                    a(*PROJECT_QUADS[t])
                a(QPG1)
                spread()
                for t in range(TG):
                    ln.add(nc.vector.scalar_tensor_tensor(out=rowA[:, t, :], in0=rowA[:, t, :], scalar=mv_g[:, t, 0:1],
                                                          in1=g2_bc[:, :], op0=ALU.subtract, op1=ALU.mult))
                ln.wait()
                for t in range(TG):
                    tile = resid[:, bass.ds(g * TG + t, 1), :].squeeze(1)
                    nc.vector.scalar_tensor_tensor(out=tile, in0=rowA[:, t, :], scalar=rs_g[:, t:t + 1], in1=tile,
                                                   op0=ALU.mult, op1=ALU.add).then_inc(s_h2done, 1)
                ln.close()
            dve.drain().then_inc(s_phase, 1)
            dve.wait_ge(s_phase, 6)

            with dve.If(dve.value_load(spill_i[0:1, 0:1], min_val=0, max_val=N) > WIN - 1):
                with dve.Fori(0, NCH) as c:
                    head = Links(dve, s_over_v, 3 + 3 * MORE, c)
                    head.add(nc.vector.tensor_copy(over_f[:, 0:1], relT[:, bass.ds(c, 1)]))
                    head.add(nc.vector.tensor_copy(over_f[:, 1:2], wT[:, bass.ds(c, 1)]))
                    head.add(nc.vector.tensor_copy(over_at[:, 0:1], low_all[:, bass.ds(c, 1)]))
                    hold(dve, "vector", s_over_v, head.value())
                    with dve.Fori(0, MORE) as w:
                        k = (3 + 3 * MORE) * c + 3 * w
                        nc.vector.tensor_scalar(over_at[:, 0:1], over_at[:, 0:1], float(WIN), float(N), ALU.add,
                                                ALU.min).then_inc(s_over_v, 1)
                        nc.vector.tensor_scalar(over_f[:, 0:1], over_f[:, 0:1], float(-WIN), None,
                                                ALU.add).then_inc(s_over_v, 1)
                        dve.wait_ge(s_over_v, k + 5)
                        nc.vector.tensor_copy(over_i[:, 0:1], over_at[:, 0:1]).then_inc(s_over_v, 1)
                        nc.vector.tensor_scalar(onehot[:, 0, :], win_iota[:, :], over_f[:, 0:1], over_f[:, 1:2],
                                                ALU.is_equal, ALU.mult).then_inc(s_over_hot, 1)
                        hold(dve, "vector", s_over_v, k + 6)
                        start = dve.value_load(over_i[0:1, 0:1], min_val=0, max_val=N)
                        dve.wait_ge(s_over_mm, MORE * c + w + 1)
                        window = accT[:, :, bass.ds(start, WIN)]
                        nc.vector.tensor_tensor(out=window, in0=window, in1=ps_agg[:, 0, 0:KC * WIN].rearrange("p (k n) -> p k n", k=KC),
                                                op=ALU.add).then_inc(s_over_add, 1)
                        dve.wait_ge(s_over_add, MORE * c + w + 1)
                    dve.sem_inc(s_over_chunk, 1)
            dve.drain().then_inc(s_phase, 1)
            dve.wait_ge(s_phase, 8)

            ln = Links(dve, s_v2b)
            for g in range(NG):
                tiles = range(g * TG, (g + 1) * TG)
                group = slice(g * TG, (g + 1) * TG)
                rows = pair_rows[g % 2]
                ve, rs, rt = ve_all[:, group], rstd_all[:, group], rtmp_all[:, group]
                dve.wait_ge(s_proj_ev, (g + 1) * TG)
                ln.link(nc.vector.tensor_scalar(ve, ve, NORM_EPS ** 2, None, ALU.max))
                rsqrt(nc, ln, rs, ve, rt)
                for n in tiles:
                    ln.add(nc.vector.scalar_tensor_tensor(out=resid[:, n, :], in0=rows[:, n % TG, :],
                                                          scalar=rstd_all[:, n:n + 1], in1=resid[:, n, :],
                                                          op0=ALU.mult, op1=ALU.add))
                summed = ln.k
                for n in tiles:
                    dve.wait_ge(s_v2b, summed - TG + n % TG + 1)
                    ln.add(nc.vector.bn_stats(st_all[:, n, :], resid[:, n, :]))
                for n in tiles:
                    dve.wait_ge(s_v2b, summed + n % TG + 1)
                    ln.add(nc.vector.bn_aggr(mv_all[:, n, :], st_all[:, n, :]))
                ln.wait()
                ln.link(nc.vector.tensor_scalar(ve, mv_all[:, group, 1], LN_EPS, None, ALU.add))
                rsqrt(nc, ln, rs, ve, rt)
                for n in tiles:
                    nc.vector.tensor_scalar(rows[:, n % TG, :], resid[:, n, :], mv_all[:, n, 0:1],
                                            rstd_all[:, n:n + 1], ALU.subtract, ALU.mult).then_inc(s_xn2, 1)

            shape = [TR, NT, NX]
            lg, ex, pr, o1, o2, tmp = (sm[:, k, :, :] for k in range(6))
            mx, rs, p1, p2, df, e2, r1, r2 = (sv[:, k, :] for k in range(8))
            dve.wait_ge(s_lg_mm, NG)
            ln.link(nc.vector.tensor_tensor(out=lg, in0=ps_att[0:TR, 0:NT * NX].rearrange("p (t e) -> p t e", t=NT),
                                            in1=rb2_bc[:, :].unsqueeze(1).broadcast_to(shape), op=ALU.add))
            ln.link(nc.vector.tensor_reduce(out=mx, in_=lg, op=ALU.max, axis=AX))
            nc.vector.tensor_tensor(out=lg, in0=lg, in1=bc(mx, shape), op=ALU.subtract).then_inc(s_sm, 1)
            dve.wait_ge(s_ex, 1)
            ln.link(nc.vector.tensor_reduce(out=rs, in_=ex, op=ALU.add, axis=AX))
            ln.link(nc.vector.reciprocal(rs, rs))
            ln.link(nc.vector.tensor_tensor(out=pr, in0=ex, in1=bc(rs, shape), op=ALU.mult))

            def pick(values, top, one):
                ln.link(nc.vector.tensor_reduce(out=top, in_=values, op=ALU.max, axis=AX))
                ln.link(nc.vector.tensor_tensor(out=one, in0=values, in1=bc(top, shape), op=ALU.is_equal))
                ln.link(nc.vector.tensor_tensor(out=one, in0=one, in1=rev[:, :].unsqueeze(1).broadcast_to(shape),
                                                op=ALU.mult))
                ln.link(nc.vector.tensor_reduce(out=mx, in_=one, op=ALU.max, axis=AX))
                ln.link(nc.vector.tensor_tensor(out=one, in0=one, in1=bc(mx, shape), op=ALU.is_equal))

            pick(pr, p1, o1)
            ln.link(nc.vector.scalar_tensor_tensor(out=tmp, in0=o1, scalar=-2.0, in1=pr, op0=ALU.mult, op1=ALU.add))
            pick(tmp, p2, o2)
            nc.vector.tensor_tensor(out=df, in0=p2, in1=p1, op=ALU.subtract).then_inc(s_sm, 1)
            dve.wait_ge(s_ex, 2)
            ln.link(nc.vector.tensor_scalar(r1, e2, 1.0, None, ALU.add))
            ln.link(nc.vector.reciprocal(r1, r1))
            ln.link(nc.vector.tensor_tensor(out=r2, in0=e2, in1=r1, op=ALU.mult))
            ln.add(nc.vector.tensor_tensor(out=o1, in0=o1, in1=bc(r1, shape), op=ALU.mult))
            ln.link(nc.vector.tensor_tensor(out=o2, in0=o2, in1=bc(r2, shape), op=ALU.mult))
            ln.link(nc.vector.tensor_tensor(out=gates_all[:, :, :], in0=o1, in1=o2, op=ALU.add))

            with dve.Fori(0, NG) as g:
                dve.wait_ge(s_y_add, 1 + ROWS * g)
                nc.vector.tensor_copy(gates_g[:, :, :], gates_all[:, bass.ds(g * TG, TG), :]).then_inc(s_v3, 1)
                nc.vector.tensor_copy(gate_pad[:, :, 0:NX], gates_all[:, bass.ds(g * TG, TG), :]).then_inc(s_gate, 1)
                dve.wait_ge(s_v3, g + 1)
                for k, e in enumerate((0, None, *range(1, NX))):
                    for t in range(TG):
                        i = k * TG + t
                        tile = resid[:, bass.ds(g * TG + t, 1), :].squeeze(1)
                        dve.wait_ge(s_y_mm, ROWS * g + (i + 1))
                        if k:
                            dve.wait_ge(s_y_add, 1 + ROWS * g + (i + 1 - TG))
                        y = ps_row[0:TR, i % 2, 0:D]
                        if e is None:
                            nc.vector.tensor_tensor(out=tile, in0=tile, in1=y, op=ALU.add).then_inc(s_y_add, 1)
                        else:
                            nc.vector.scalar_tensor_tensor(out=tile, in0=y, scalar=gates_g[:, t, e:e + 1], in1=tile,
                                                           op0=ALU.mult, op1=ALU.add).then_inc(s_y_add, 1)


MIX_LINKS = 2 + 2 * 5 + 2 * (5 + 5 + 1 + 11) + 5


def _columns(a):
    import numpy as _np
    a = _np.asarray(a)
    return _np.ascontiguousarray(_np.moveaxis(a.reshape(a.shape[:-1] + (-1, 128)), -1, 0))


def kernel(**inputs):
    import numpy as _np
    import concourse.bacc as _bacc
    from concourse.bass_utils import run_bass_kernel_spmd as _run

    i = {k: _np.asarray(v) for k, v in inputs.items()}
    mix, ffn = "L0_mix_", "L0_ffn_"
    laid = {
        "x": i["x"], "src": i["src"], "dst": i["dst"], "edge_w": i["edge_weight"],
        "w_self_t": i["L0_gnn_w_self"].T, "w_neigh_t": i["L0_gnn_w_neigh"].T,
        "wq": i[mix + "Wq"], "wk": i[mix + "Wk"], "wv": i[mix + "Wv"], "wm": i[mix + "Wm"],
        "w1": i[mix + "W1"], "w2": i[mix + "W2"], "g1c": _columns(i[mix + "g1"]), "b1c": _columns(i[mix + "b1"]),
        "g2": i[mix + "g2"], "b2": i[mix + "b2"],
        "rw1": i[ffn + "router_w1"], "rb1c": _columns(i[ffn + "router_b1"]), "rw2": i[ffn + "router_w2"],
        "rb2": i[ffn + "router_b2"],
        "ew1": i[ffn + "expert_w1"], "eb1c": _columns(i[ffn + "expert_b1"]),
        "ew2": i[ffn + "expert_w2"], "eb2c": _columns(i[ffn + "expert_b2"]),
        "ew3": i[ffn + "expert_w3"], "eb3": i[ffn + "expert_b3"],
    }
    nc = _bacc.Bacc("TRN2", target_bir_lowering=False, num_devices=1)
    arrays, args = {}, []
    for name, a in laid.items():
        a = _np.ascontiguousarray(a)
        arrays[f"in_{name}"] = a
        args.append(nc.dram_tensor(f"in_{name}", a.shape, mybir.dt.from_np(a.dtype), kind="ExternalInput").ap())
    out = nc.dram_tensor("out_rows", i["x"].shape, F32, kind="ExternalOutput").ap()
    gps_layer_kernel(nc, *args, out)
    r = _run(nc, [arrays], core_ids=[0])
    return r.results[0]["out_rows"]
```

```python
from contextlib import ExitStack

import concourse.bass as bass
from concourse import mybir

F32 = mybir.dt.float32
I32 = mybir.dt.int32
F32R = mybir.dt.float32r
ALU = mybir.AluOpType
ACT = mybir.ActivationFunctionType
AX = mybir.AxisListType.X
DVE_ONLY = (mybir.EngineType.DVE,)

LN_EPS = 1e-5
ATT_EPS = 1e-6
NORM_EPS = 1e-12
RSQRT_SEED = float(0x5F3759DF)


class Links:

    def __init__(self, eng, sem, per=0, i=0):
        self.eng, self.sem, self.per, self.i, self.k = eng, sem, per, i, 0

    def add(self, ins):
        ins.then_inc(self.sem, 1)
        self.k += 1

    def value(self):
        return self.i * self.per + self.k if self.per else self.k

    def wait(self):
        self.eng.wait_ge(self.sem, self.value())

    def link(self, ins):
        self.add(ins)
        self.wait()

    def close(self):
        assert self.k == self.per, (self.k, self.per)


def rsqrt(nc, ln, out, v, t):
    ln.link(nc.vector.tensor_scalar(t.bitcast(I32), v.bitcast(I32), 1, None, ALU.logical_shift_right))
    ln.link(nc.vector.tensor_scalar(out.bitcast(I32), t.bitcast(I32), -1.0, RSQRT_SEED, ALU.mult, ALU.add))
    for _ in range(3):
        ln.link(nc.vector.tensor_tensor(out=t, in0=out, in1=out, op=ALU.mult))
        ln.link(nc.vector.scalar_tensor_tensor(out=t, in0=t, scalar=-0.5, in1=v, op0=ALU.mult, op1=ALU.mult))
        ln.link(nc.vector.scalar_tensor_tensor(out=out, in0=t, scalar=1.5, in1=out, op0=ALU.add, op1=ALU.mult))



def gps_layer_kernel(nc, x, src, dst, edge_w, w_self_t, w_neigh_t, wq, wk, wv, wm, w1, w2, g1c, b1c, g2, b2,
                     rw1, rb1c, rw2, rb2, ew1, eb1c, ew2, eb2c, ew3, eb3, out):
    N, D = x.shape
    E = src.shape[0]
    TR, TG = 125, 5
    NT = N // TR
    NG = NT // TG
    GN = TG * TR
    KC = D // 128
    H1 = w1.shape[1] // 128
    HD = 32
    HPC = 128 // HD
    HW = 128 + HPC
    NX = ew1.shape[0]
    RH = rw1.shape[1]
    WIN = 64
    NCH = E // TR
    QC = 4
    NQ = NCH // QC
    RQ = 5
    RING = RQ * QC
    QPG0 = 5
    RAW = 2
    AHEAD = 3
    ACCW = N + WIN + 3
    MORE = -(-N // WIN)
    PARTS = ((0, 3), (3, 2))
    EVEN = tuple((t0 * TR + t0 * TR % 2, n * TR + n * TR % 2, t0 * TR) for t0, n in PARTS)
    GE = EVEN[-1][0] + EVEN[-1][1]
    assert EVEN[-1][1] == PARTS[-1][1] * TR
    assert N == NT * TR and NT == NG * TG and E == NCH * TR and NCH == NQ * QC

    OPEN, LOOP, CLOSE, FINISH = 0, 1, 2, 3
    STEPS = tuple(tuple((s[0], int(s[1:] or 0)) for s in steps.split()) for steps in (
        """Q0 Q1 G0 Q2 Q3 G1 A0 G2 A1 T0 G3 A2 T1 M0 G4 A3 T2 M1 G5 A4 T3 M2 G6 T4 M3 G7 M4 G8 S G9
           N0 N1 N2 N3 N4 F""",
        """H0 Q0 G0 H1 Q1 G1 Q2 H2 G2 Q3 H3 G3 A0 G4 A1 T0 H4 A2 T1 M0 G5 A3 T2 M1 H5 A4 T3 M2 G6
           T4 M3 H6 M4 G7 S H7 P0 G8 P1 G9 N0 P2 G10 N1 P3 N2 G11 P4 N3 G12 N4 G13 G14 F R""",
        """H0 H1 G0 H2 H3 G1 H4 H5 G2 H6 H7 G3 P0 P1 G4 P2 P3 P4 F""",
        """R"""))
    PASSES = (1, NG - 1, 1, 1)

    def count(stage, kinds):
        return sum(kind in kinds for kind, _ in STEPS[stage])

    def before(stage, kinds):
        return sum(PASSES[k] * count(k, kinds) for k in range(stage))

    QUADS = [count(k, "G") for k in range(4)]
    QUADS_BEFORE = [NG * QPG0 + before(k, "G") for k in range(4)]
    QMAX = max(QUADS)
    assert QUADS_BEFORE[FINISH] == NQ and all(q % RQ == 0 for q in (*QUADS, *QUADS_BEFORE))
    assert QPG0 == TG and QPG0 == RQ and NQ <= 128 and RH == 128

    class Turns:

        def __init__(self, stage, kinds, g):
            self.start, self.per, self.g, self.k, self.of = before(stage, kinds), count(stage, kinds), g, 0, {}

        def take(self, step):
            self.of[step] = self.start + self.k
            self.k += 1
            return self.of[step]

        def value(self, turns):
            return self.per * self.g + turns

    class Groups:

        def __init__(self, g, shift):
            self.g, self.shift = g, shift

        def value(self, per, k):
            return per * self.g + (per * self.shift + k)

        def nodes(self, lo, n):
            return bass.ds(self.g * GN + (self.shift * GN + lo), n)

    ctx = ExitStack()
    with ctx:
        def sb(name, shape, dt=F32):
            return ctx.enter_context(nc.sbuf_tensor(name, shape, dt))

        def region(name, columns):
            start = -(-nc.sbuf_base // 32) * 32
            return sb(name, [128, columns]), start

        def pb(name, shape):
            return ctx.enter_context(nc.psum_tensor(name, shape, F32))

        def sem(name):
            return ctx.enter_context(nc.semaphore(name))

        xn_dram = nc.dram_tensor("xn_rows", (N, D), F32).ap()
        low_dram = nc.dram_tensor("window_starts", (2, NQ), I32).ap()

        ident = sb("ident", [128, 128])
        win_iota = sb("win_iota", [TR, WIN])
        g2_bc = sb("g2_bc", [TR, D])
        b2_bc = sb("b2_bc", [TR, D])
        rb2_bc = sb("rb2_bc", [TR, NX])
        rev = sb("rev", [TR, NX])
        XW = NX * KC * D
        mix_w, mix_w_at = region("mix_w", max(2 * KC * D + 2 * KC * D + 2 * KC * 2 * D + H1 * D, 2 * XW))
        at = [0]

        def mix_weight(chunks, width):
            lo, at[0] = at[0], at[0] + chunks * width
            return mix_w[:, lo:at[0]].rearrange("p (c n) -> p c n", c=chunks)

        wkv_sb = mix_weight(KC, 2 * D)
        wq_sb = mix_weight(KC, D)
        wm_sb = mix_weight(KC, D)
        w1_sb = mix_weight(2 * KC, 2 * D)
        w2_sb = mix_weight(H1, D)
        g1_sb = sb("g1_sb", [128, KC])
        b1_sb = sb("b1_sb", [128, KC])
        ws_sb = sb("ws_sb", [128, KC, D])
        wn_sb = sb("wn_sb", [128, KC, D])
        rw1_sb = sb("rw1_sb", [128, KC, RH])
        rw1_hl = sb("rw1_hl", [128, 2, KC, RH], F32R)
        raw = sb("raw", [128, RAW, KC, D])
        rb1_sb = sb("rb1_sb", [128, 1])
        rw2_sb = sb("rw2_sb", [128, NX])
        eb_sb = sb("eb_sb", [128, 2, NX, KC])
        b3_sb = sb("b3_sb", [128, D])
        resid = sb("resid", [TR, NT, D])
        arena, arena_at = region("arena", KC * (ACCW + N))
        accT = arena[:, 0:KC * ACCW].rearrange("p (c n) -> p c n", c=KC)
        xnT = arena[:, KC * ACCW:KC * (ACCW + N)].rearrange("p (c n) -> p c n", c=KC)
        mv_all = sb("mv_all", [TR, NT, 2])
        ve_all = sb("ve_all", [TR, NT])
        rstd_all = sb("rstd_all", [TR, NT])
        rtmp_all = sb("rtmp_all", [TR, NT])
        gates_all = sb("gates_all", [TR, NT, NX])
        kv_acc = sb("kv_acc", [128, KC, 129])
        kv_bd = sb("kv_bd", [128, KC, HW])
        low_f = sb("low_f", [NQ, 1])
        span_f = sb("span_f", [NQ, 1])
        low_i = sb("low_i", [NQ, 2], I32)
        low_row = sb("low_row", [1, 2, NQ], I32)
        relT = sb("relT", [TR, NCH + AHEAD * QC])
        wT = sb("wT", [TR, NCH + AHEAD * QC])
        srcT = sb("srcT", [TR, NCH + RING], I32)
        rel_g = sb("rel_g", [TR, QMAX * QC])
        w_g = sb("w_g", [TR, QMAX * QC])
        src_g = sb("src_g", [TR, 2 * RING], I32)
        ring, ring_at = region("ring", max(RING * (D + WIN), 2 * XW))
        msg = ring[0:TR, 0:RING * D].rearrange("p (c n) -> p c n", c=RING)
        onehot = ring[0:TR, RING * D:RING * (D + WIN)].rearrange("p (c n) -> p c n", c=RING)
        cols_sb, cols_at = region("cols", (4 * KC + H1) * GN)

        def columns(first, chunks):
            return cols_sb[:, first * GN:(first + chunks) * GN].rearrange("p (c n) -> p c n", c=chunks)

        colA = columns(0, KC)
        colB = columns(KC, KC)
        colC = columns(2 * KC, KC)
        colD = columns(3 * KC, KC)
        hid = columns(4 * KC, H1)
        def early(buf, k):
            return buf[0:NQ, k, 0:QC * TR]

        dst_i, src_i, ew_r, dst_f = early(hid, 0).bitcast(I32), early(hid, 1).bitcast(I32), early(hid, 2), early(hid, 3)
        src_f = early(colD, 0)
        rows_sb, rows_at = region("rows", 3 * TG * D)

        def row_tiles(k):
            return rows_sb[0:TR, k * TG * D:(k + 1) * TG * D].rearrange("p (t d) -> p t d", t=TG)

        rowA = row_tiles(0)
        rowB = row_tiles(1)
        rowC = row_tiles(2)
        low_all = rows_sb[0:1, 0:NCH]
        vg_sb, values_at = region("values", TG * KC * 129)
        v_g = vg_sb[0:TR, :].rearrange("p (t c n) -> p t c n", t=TG, c=KC)
        el_e = sb("el_e", [128, 2, EVEN[0][1]])
        el_r = sb("el_r", [128, 2, EVEN[0][1]])
        st_g = sb("st_g", [TR, TG, 6])
        mv_g = sb("mv_g", [TR, TG, 2])
        ve_g = sb("ve_g", [TR, TG])
        rs_g = sb("rs_g", [TR, TG])
        rt_g = sb("rt_g", [TR, TG])
        gate_pad = sb("gate_pad", [TR, TG, 128])
        win_iota_i = gate_pad[:, 0, 0:WIN].bitcast(I32)
        gates_g = sb("gates_g", [TR, TG, NX])
        sv = sb("sv", [TR, 8, NT])
        spill_i = sb("spill_i", [1, 1], I32)
        over_f = sb("over_f", [TR, 4])
        over_at = sb("over_at", [1, 2])
        over_i = sb("over_i", [1, 2], I32)
        st_all = sb("st_all", [TR, NT, 6])
        zr = sb("zr", [TR, KC, HPC])

        ps_agg = pb("ps_agg", [128, 2, 512])
        ps_big = pb("ps_big", [128, 2, 512])
        ps_att = pb("ps_att", [128, 512])
        ps_tr = pb("ps_tr", [128, 512])
        ps_row = pb("ps_row", [128, 2, 512])

        s_src_in = sem("s_src_in")
        s_edges = sem("s_edges")
        s_x = [sem(f"s_x{g}") for g in range(NG)]
        s_rows_out = [sem(f"s_rows_out{g}") for g in range(NG)]
        s_srcf = sem("s_srcf")
        s_wkv, s_wmix, s_wffn, s_bc = sem("s_wkv"), sem("s_wmix"), sem("s_wffn"), sem("s_bc")
        s_id0, s_ident = sem("s_id0"), sem("s_ident")
        s_prep = sem("s_prep")
        s_edge_ready = sem("s_edge_ready")
        s_edge_tr = sem("s_edge_tr")
        s_low_all = sem("s_low_all")
        s_low_out, s_low_in = sem("s_low_out"), sem("s_low_in")
        s_srcT = sem("s_srcT")
        s_lists = sem("s_lists")
        s_v0, s_v0a, s_v0b = sem("s_v0"), sem("s_v0a"), sem("s_v0b")
        s_zero = sem("s_zero")
        s_xn = sem("s_xn")
        s_xn_tr = sem("s_xn_tr")
        s_xnT = sem("s_xnT")
        s_stage = sem("s_stage")
        s_kv_mm, s_kv_ev = sem("s_kv_mm"), sem("s_kv_ev")
        s_key = sem("s_key")
        s_kvp, s_kvsum = sem("s_kvp"), sem("s_kvsum")
        s_src = sem("s_src")
        s_held = {}
        s_msg = [sem(f"s_msg{k}") for k in range(RQ)]
        s_hot = sem("s_hot")
        s_quad = sem("s_quad")
        s_add = sem("s_add")
        s_v1 = sem("s_v1")
        s_bd = sem("s_bd")
        s_phase = sem("s_phase")
        s_big_mm, s_big_free = sem("s_big_mm"), sem("s_big_free")
        s_q = sem("s_q")
        s_att_mm, s_att = sem("s_att_mm"), sem("s_att")
        s_tr_mm, s_tr_free = sem("s_tr_mm"), sem("s_tr_free")
        s_row_mm, s_row_free = sem("s_row_mm"), sem("s_row_free")
        s_norm1 = sem("s_norm1")
        s_h2done = sem("s_h2done")
        s_over_src, s_over_msg, s_over_hot, s_over_mm, s_over_add, s_over_v = (
            sem("s_over_src"), sem("s_over_msg"), sem("s_over_hot"), sem("s_over_mm"), sem("s_over_add"),
            sem("s_over_v"))
        s_open, s_v2, s_close, s_finish, s_v2b = (sem("s_open"), sem("s_v2"), sem("s_close"), sem("s_finish"),
                                                  sem("s_v2b"))
        s_proj_mm, s_proj_ev = sem("s_proj_mm"), sem("s_proj_ev")
        s_xn2 = sem("s_xn2")
        s_tr2_mm, s_tr2_hi, s_tr2_ev = sem("s_tr2_mm"), sem("s_tr2_hi"), sem("s_tr2_ev")
        s_rh_mm, s_rh_ev = sem("s_rh_mm"), sem("s_rh_ev")
        s_lg_mm = sem("s_lg_mm")
        s_sm, s_ex = sem("s_sm"), sem("s_ex")
        s_gate = sem("s_gate")
        s_gtr_mm, s_gtr_ev = sem("s_gtr_mm"), sem("s_gtr_ev")
        s_e_mm = sem("s_e_mm")
        s_e_ev = sem("s_e_ev")
        s_y_mm, s_y_add = sem("s_y_mm"), sem("s_y_add")
        s_v3 = sem("s_v3")
        s_out = sem("s_out")
        s_ew = [sem(f"s_ew{k}") for k in range(RAW)]
        s_rsplit = sem("s_rsplit")
        s_hi, s_split = sem("s_hi"), sem("s_split")
        s_lo = sem("s_lo")
        s_spill = sem("s_spill")
        s_over_chunk = sem("s_over_chunk")

        for name in ("sync", "gpsimd", "tensor", "vector"):
            s_held[name] = sem(f"s_held_{name}")

        def hold(eng, name, semaphore, value):
            eng.wait_ge(semaphore, value)
            eng.sem_inc(s_held[name], 1)

        x_t = x.rearrange("(n p) d -> p n d", p=TR)
        out_t = out.rearrange("(n p) d -> p n d", p=TR)
        xn_t = xn_dram.rearrange("(n p) d -> p n d", p=TR)

        def chunked(w):
            return w.rearrange("(c p) n -> p c n", p=128)

        def edge_rows(e):
            return e.rearrange("(p e) -> p e", e=QC * TR)

        xn_rows = [rowA[:, :, :], rowB[:, :, :]] + [msg[:, k * TG:(k + 1) * TG, :] for k in range(NG - 2)]
        assert RING >= (NG - 2) * TG

        def turn_bank(step):
            return ps_att if step[0] == "N" and step[1] % 2 else ps_tr

        r2, v2, t2 = rstd_all[:, 0:2 * TG], rstd_all[:, 2 * TG:4 * TG], rtmp_all[:, 0:2 * TG]
        sm = vg_sb[0:TR, 0:6 * NT * NX].rearrange("p (k t e) -> p k t e", k=6, t=NT)
        gates_col = columns(4 * KC + H1 - 1, 1)[:, 0, :]
        def over(name, shape, at):
            return nc.alloc_sbuf_tensor_at(name, shape, F32R, offset=at)

        assert 2 * XW <= KC * ACCW and KC * N <= (4 * KC + H1 - 2) * GN and 3 * KC * GE <= 3 * TG * D
        assert KC * GE <= TG * KC * 129
        ew_sb = [over(f"ew{k}_hl", [128, 2, NX, KC, D], at) for k, at in enumerate((mix_w_at, ring_at, arena_at))]
        xT_hl = (over("x_hi", [128, KC, N], arena_at + 4 * KC * ACCW),
                 over("x_lo", [128, KC, N], cols_at))
        hidden_hl = over("hidden_hl", [128, 3, KC, GE], rows_at)
        h1_hl = (hidden_hl[:, 0, :, :], hidden_hl[:, 1, :, :])
        h2_hl = (hidden_hl[:, 2, :, :],
                 over("hidden2_lo", [128, KC, GE], values_at)[:, :, :])
        rhid = columns(4 * KC + H1 - 2, 2)
        turn_rows = (rowA, rowB, rowC)
        LAG = 2
        TURN_BANKS = (ps_tr, ps_agg[:, 0, :], ps_agg[:, 1, :])
        EXPERT_BANKS = (ps_big[:, 0, :], ps_big[:, 1, :], ps_agg[:, 0, :], ps_agg[:, 1, :])
        WHOLE = (el_e[:, 0, :], el_e[:, 1, :], el_r[:, 0, :], el_r[:, 1, :])
        OUTPUT_BANKS = (ps_row[:, 0, :], ps_row[:, 1, :], ps_tr)

        def added(i):
            return max(i - (2, 2, TG, 3, 3)[i % TG] + 1, 0)

        GATES_AFTER = (3, 4)
        EVS = NX * 2 * len(PARTS) * KC
        ROWS = (NX + 1) * TG

        block = ctx.enter_context(nc.Block())

        @block.sync
        def _(sp):
            for g in range(NG):
                sp.dma_start(resid[:, g * TG:(g + 1) * TG, :], x_t[:, g * TG:(g + 1) * TG, :]).then_inc(s_x[g], 16)
            for g in range(NG):
                sp.wait_ge(s_xn, TG * g + TG)
                sp.dma_start(xn_t[:, g * TG:(g + 1) * TG, :], xn_rows[g]).then_inc(s_rows_out[g], 16)
            sp.wait_ge(s_xnT, 1 + TG * NG)
            with sp.Fori(0, NG) as g:
                sp.wait_ge(s_kv_mm, 1 + TG * g)
                sp.dma_start(colA[:, :, :], xnT[:, :, bass.ds(g * GN, GN)]).then_inc(s_stage, 16)
            sp.wait_ge(s_ident, 3)
            for t, w in ((ws_sb[:, :, :], chunked(w_self_t)), (wn_sb[:, :, :], chunked(w_neigh_t)),
                         (rw1_sb[:, :, :], chunked(rw1)), (rb1_sb[:, :], rb1c), (rw2_sb[:, :], rw2),
                         (b3_sb[0:NX, :], eb3), (eb_sb[:, 0, :, :], eb1c), (eb_sb[:, 1, :, :], eb2c)):
                sp.dma_start(t, w).then_inc(s_wffn, 16)
            sp.wait_ge(s_phase, 3)
            for k, w in enumerate((ew1, ew2, ew3)):
                for e in range(NX):
                    i = k * NX + e
                    if i >= RAW:
                        sp.wait_ge(s_split, i - RAW + 1)
                    sp.dma_start(raw[:, i % RAW, :, :], chunked(w[e, :, :])).then_inc(s_ew[i % RAW], 16)
            with sp.Fori(0, NG) as g:
                for t0, n in PARTS:
                    sp.wait_ge(s_y_add, 1 + ROWS * g + (ROWS - TG + t0 + n))
                    sp.dma_start(out_t[:, bass.ds(g * TG + t0, n), :], resid[:, bass.ds(g * TG + t0, n), :]
                                 ).then_inc(s_out, 16)
            sp.wait_ge(s_out, 16 * len(PARTS) * NG)

        @block.gpsimd
        def _(pool):
            nc.gpsimd.memset(ident[:, :], 0.0).then_inc(s_id0, 1)
            pool.wait_ge(s_id0, 1)
            nc.gpsimd.affine_select(out=ident[:, :], in_=ident[:, :], compare_op=ALU.not_equal, fill=1.0, base=0,
                                    pattern=[[-1, 128]], channel_multiplier=1).then_inc(s_ident, 1)
            nc.gpsimd.iota(win_iota_i, pattern=[[1, WIN]], base=0, channel_multiplier=0).then_inc(s_ident, 1)
            nc.gpsimd.memset(b3_sb[:, :], 0.0).then_inc(s_ident, 1)
            for e in range(NX):
                nc.gpsimd.memset(rev[:, e:e + 1], float(NX - e))
            nc.gpsimd.memset(srcT[:, NCH:NCH + RING], 0)
            nc.gpsimd.memset(accT[:, :, :], 0.0).then_inc(s_zero, 1)
            nc.gpsimd.memset(v_g[:, :, :, :], 1.0).then_inc(s_zero, 1)
            nc.gpsimd.memset(kv_bd[:, :, :], 0.0).then_inc(s_zero, 1)
            nc.gpsimd.memset(kv_acc[:, :, :], 0.0).then_inc(s_zero, 1)

            pool.wait_ge(s_srcT, 1)
            nc.gpsimd.tensor_copy(src_g[:, 0:RING], srcT[:, 0:RING]).then_inc(s_src, 1)
            for g in range(NG):
                pool.wait_ge(s_rows_out[g], 16)
            pool.wait_ge(s_v0b, NG - 2)
            pool.wait_ge(s_xn_tr, 1 + NT)

            with pool.Fori(0, NQ // RQ // 2) as b:
                for half in range(2):
                    pool.wait_ge(s_src, 2 * b + (half + 1))
                    for q in range(RQ):
                        hold(pool, "gpsimd", s_quad, 2 * RQ * b + (half * RQ + q + 1))
                        if q == RQ - 1:
                            other = (1 - half) * RING
                            nc.gpsimd.tensor_copy(src_g[:, other:other + RING],
                                                  srcT[:, bass.ds(2 * RING * b + (half + 1) * RING, RING)]
                                                  ).then_inc(s_src, 1)
                        for c in range(q * QC, (q + 1) * QC):
                            nc.gpsimd.indirect_dma_start(
                                out=msg[:, c, :], out_offset=None, in_=xn_dram[:, :],
                                in_offset=bass.IndirectOffsetOnAxis(
                                    ap=src_g[:, half * RING + c:half * RING + c + 1], axis=0),
                            ).then_inc(s_msg[q], 16)

            pool.wait_ge(s_src, 1 + NQ // RQ)
            pool.wait_ge(s_spill, 1)
            pool.wait_ge(s_phase, 3)
            with pool.If(pool.value_load(spill_i[0:1, 0:1], min_val=0, max_val=N) > WIN - 1):
                with pool.Fori(0, NCH) as c:
                    pool.wait_ge(s_over_chunk, 1 + c)
                    nc.gpsimd.tensor_copy(src_g[:, 0:1], srcT[:, bass.ds(c, 1)]).then_inc(s_over_src, 1)
                    hold(pool, "gpsimd", s_over_src, c + 1)
                    nc.gpsimd.indirect_dma_start(
                        out=msg[:, 0, :], out_offset=None, in_=xn_dram[:, :],
                        in_offset=bass.IndirectOffsetOnAxis(ap=src_g[:, 0:1], axis=0),
                    ).then_inc(s_over_msg, 16)

            pool.wait_ge(s_wffn, 16 * 8)
            nc.gpsimd.tensor_copy(rw1_hl[:, 0, :, :], rw1_sb[:, :, :]).then_inc(s_rsplit, 1)
            pool.wait_ge(s_rsplit, 1)
            nc.gpsimd.tensor_tensor(out=rw1_hl[:, 1, :, :], in0=rw1_sb[:, :, :], in1=rw1_hl[:, 0, :, :].bitcast(F32),
                                    op=ALU.subtract).then_inc(s_rsplit, 1)
            for k in range(3):
                if k == 1:
                    pool.wait_ge(s_phase, 5)
                elif k == 2:
                    pool.wait_ge(s_proj_mm, NT)
                for e in range(NX):
                    i = k * NX + e
                    pool.wait_ge(s_ew[i % RAW], 16 * (i // RAW + 1))
                    hi, lo, whole = ew_sb[k][:, 0, e, :, :], ew_sb[k][:, 1, e, :, :], raw[:, i % RAW, :, :]
                    nc.gpsimd.tensor_copy(hi, whole).then_inc(s_hi, 1)
                    pool.wait_ge(s_hi, i + 1)
                    nc.gpsimd.tensor_tensor(out=lo, in0=whole, in1=hi.bitcast(F32), op=ALU.subtract).then_inc(s_split, 1)

        @block.tensor
        def _(pe):
            pe.sem_inc(s_quad, RQ)
            for started in (s_kvp, s_kv_mm, s_big_mm, s_xn_tr):
                pe.sem_inc(started, 1)
            def turn_list(t, bank):
                for j in range(QC):
                    last = nc.tensor.transpose(bank[0:TR, j * NQ:(j + 1) * NQ], t[:, j * TR:(j + 1) * TR],
                                               ident[0:NQ, 0:NQ])
                last.then_inc(s_edge_tr, 1)

            pe.wait_ge(s_ident, 1)
            pe.wait_ge(s_srcf, 1)
            turn_list(src_f, ps_big[:, 1, :])
            for n in range(NT):
                pe.wait_ge(s_xn, n + 1)
                pe.wait_ge(s_xnT, 1 + max(n - 1, 0))
                for c in range(KC):
                    last = nc.tensor.transpose(ps_row[:, n % 2, c * TR:(c + 1) * TR],
                                               xn_rows[n // TG][:, n % TG, c * 128:(c + 1) * 128], ident[0:TR, 0:TR])
                last.then_inc(s_xn_tr, 1)
            pe.wait_ge(s_edges, 32)
            turn_list(ew_r, ps_att)
            pe.wait_ge(s_edge_ready, 1)
            turn_list(dst_f, ps_big[:, 0, :])

            def agg(first, qpg, g, q):
                place = q % RQ
                pe.wait_ge(s_hot, g * qpg + (first + q + 1))
                pe.wait_ge(s_add, g * qpg + (first + max(q - 1, 0) + 1))
                pe.wait_ge(s_msg[place], 16 * QC * (qpg // RQ) * g + 16 * QC * ((first + q) // RQ + 1))
                for k in range(KC):
                    for c in range(QC):
                        last = nc.tensor.matmul(ps_agg[:, q % 2, k * WIN:(k + 1) * WIN],
                                                msg[:, place * QC + c, k * 128:(k + 1) * 128],
                                                onehot[:, place * QC + c, :], start=(c == 0), stop=(c == QC - 1))
                last.then_inc(s_quad, 1)

            pe.wait_ge(s_wkv, 32)
            pe.wait_ge(s_srcT, 1)
            pe.wait_ge(s_lists, 1)
            with pe.Fori(0, NG) as g:
                def key_value_product(t):
                    pe.wait_ge(s_key, 1 + TG * g + t + 1)
                    if t == 0:
                        pe.wait_ge(s_kvsum, 1 + g)
                    for c in range(KC):
                        last = nc.tensor.matmul(ps_row[:, c, 0:129], rowB[:, t, c * 128:(c + 1) * 128],
                                                v_g[:, t, c, :], start=(t == 0), stop=(t == TG - 1))
                    last.then_inc(s_kvp, 1)

                for t in range(TG):
                    if t == 0:
                        pe.wait_ge(s_xnT, 1 + TG * NG)
                        pe.wait_ge(s_stage, 16 * g + 16)
                    pe.wait_ge(s_kv_ev, 1 + TG * g + max(t - 1, 0))
                    for c in range(KC):
                        last = nc.tensor.matmul(ps_big[0:TR, t % 2, :], colA[:, c, t * TR:(t + 1) * TR],
                                                wkv_sb[:, c, :], start=(c == 0), stop=(c == KC - 1))
                    last.then_inc(s_kv_mm, 1)
                    if t:
                        key_value_product(t - 1)
                    agg(0, QPG0, g, t)
                key_value_product(TG - 1)
            pe.wait_ge(s_kv_ev, 1 + TG * NG)

            pe.wait_ge(s_wmix, 16 * 6)

            def mix(stage, g, front, back):
                big, tr, row = Turns(stage, "QH", g), Turns(stage, "TN", g), Turns(stage, "MP", g)

                def turn(step, rows, t, ready, n):
                    i, bank = tr.take(step), turn_bank(step)
                    pe.wait_ge(ready, n)
                    pe.wait_ge(s_tr_free, tr.value(i if step[0] == "N" and t else 1 + i))
                    for c in range(KC):
                        last = nc.tensor.transpose(bank[:, c * TR:(c + 1) * TR], rows[:, t, c * 128:(c + 1) * 128],
                                                   ident[0:TR, 0:TR])
                    last.then_inc(s_tr_mm, 1)

                for step in STEPS[stage]:
                    kind, k = step
                    if kind == "Q":
                        t0, n = PARTS[k // KC]
                        m, i = k % KC, big.take(step)
                        pe.wait_ge(s_big_free, big.value(i + 1))
                        for c in range(KC):
                            last = nc.tensor.matmul(ps_big[:, i % 2, 0:n * TR], wq_sb[:, c, m * 128:(m + 1) * 128],
                                                    xnT[:, c, front.nodes(t0 * TR, n * TR)],
                                                    start=(c == 0), stop=(c == KC - 1))
                        last.then_inc(s_big_mm, 1)
                    elif kind == "A":
                        pe.wait_ge(s_q, front.value(2 * KC, 1 + (KC if k < PARTS[1][0] else 2 * KC)))
                        pe.wait_ge(s_att, front.value(TG, 1 + k))
                        if stage == OPEN and k == 0:
                            pe.wait_ge(s_bd, 1)
                        for c in range(KC):
                            last = nc.tensor.matmul(ps_att[0:TR, c * HW:(c + 1) * HW], colB[:, c, k * TR:(k + 1) * TR],
                                                    kv_bd[:, c, :], start=True, stop=True)
                        last.then_inc(s_att_mm, 1)
                    elif kind == "T":
                        turn(step, rowB, k, s_att, front.value(TG, 1 + k + 1))
                    elif kind == "M":
                        i = row.take(step)
                        pe.wait_ge(s_tr_free, tr.value(1 + tr.of["T", k] + 1))
                        pe.wait_ge(s_row_free, row.value(i + 1))
                        for c in range(KC):
                            last = nc.tensor.matmul(ps_row[0:TR, i % 2, 0:D], colC[:, c, k * TR:(k + 1) * TR],
                                                    wm_sb[:, c, :], start=(c == 0), stop=(c == KC - 1))
                        last.then_inc(s_row_mm, 1)
                    elif kind == "N":
                        turn(step, rowA, k, s_norm1, front.value(TG, k + 1))
                    elif kind == "H":
                        t0, n = PARTS[k // H1]
                        m, i = k % H1, big.take(step)
                        pe.wait_ge(s_tr_free, tr.value(1 + tr.start))
                        pe.wait_ge(s_big_free, big.value(i + 1))
                        for c in range(2 * KC):
                            col = (xnT[:, c, back.nodes(t0 * TR, n * TR)] if c < KC else
                                   colD[:, c - KC, t0 * TR:(t0 + n) * TR])
                            last = nc.tensor.matmul(ps_big[:, i % 2, 0:n * TR], w1_sb[:, c, m * 128:(m + 1) * 128],
                                                    col, start=(c == 0), stop=(c == 2 * KC - 1))
                        last.then_inc(s_big_mm, 1)
                    elif kind == "P":
                        i = row.take(step)
                        hidden = big.of["H", H1 - 1 if k < PARTS[1][0] else 2 * H1 - 1]
                        pe.wait_ge(s_big_free, big.value(2 + hidden + 1))
                        pe.wait_ge(s_row_free, row.value(i + 1))
                        for c in range(H1):
                            last = nc.tensor.matmul(ps_row[0:TR, i % 2, 0:D], hid[:, c, k * TR:(k + 1) * TR],
                                                    w2_sb[:, c, :], start=(c == 0), stop=(c == H1 - 1))
                        last.then_inc(s_row_mm, 1)
                    elif kind == "G":
                        agg(QUADS_BEFORE[stage], QUADS[stage], g, k)

            mix(OPEN, 0, Groups(0, 0), None)
            with pe.Fori(0, NG - 1) as g:
                mix(LOOP, g, Groups(g, 1), Groups(g, 0))
            mix(CLOSE, 0, None, Groups(0, NG - 1))
            pe.drain().then_inc(s_phase, 1)
            pe.wait_ge(s_phase, 3)

            pe.wait_ge(s_spill, 1)
            with pe.If(pe.value_load(spill_i[0:1, 0:1], min_val=0, max_val=N) > WIN - 1):
                with pe.Fori(0, NCH) as c:
                    hold(pe, "tensor", s_over_msg, 16 * c + 16)
                    with pe.Fori(0, MORE) as w:
                        pe.wait_ge(s_over_hot, MORE * c + w + 1)
                        for k in range(KC):
                            last = nc.tensor.matmul(ps_agg[:, 0, k * WIN:(k + 1) * WIN], msg[:, 0, k * 128:(k + 1) * 128],
                                                    onehot[:, 0, :], start=True, stop=True)
                        last.then_inc(s_over_mm, 1)
            pe.drain().then_inc(s_phase, 1)
            pe.wait_ge(s_phase, 5)

            def product(out, pairs):
                steps = [(w[a], x[b]) for w, x in pairs for a, b in ((0, 0), (0, 1), (1, 0))]
                for k, (w, x) in enumerate(steps):
                    last = nc.tensor.matmul(out, w, x, start=(k == 0),
                                            stop=(k == len(steps) - 1))
                return last

            def logits(g):
                pe.wait_ge(s_rh_ev, 2 * (g + 1))
                for n in range(g * TG, (g + 1) * TG):
                    t = n % TG
                    last = nc.tensor.matmul(ps_att[0:TR, n * NX:(n + 1) * NX], rhid[:, g % 2, t * TR:(t + 1) * TR],
                                            rw2_sb[:, :], start=True, stop=True)
                last.then_inc(s_lg_mm, 1)

            pe.wait_ge(s_wffn, 16 * 8)
            for g in range(NG + LAG):
                if g < NG:
                    for n in range(g * TG, (g + 1) * TG):
                        if n >= 2:
                            pe.wait_ge(s_proj_ev, n - 1)
                        rows = slice(n * TR, (n + 1) * TR)
                        for k, (col, w) in enumerate(((xnT, ws_sb), (accT, wn_sb))):
                            for c in range(KC):
                                last = nc.tensor.matmul(ps_row[0:TR, n % 2, 0:D], col[:, c, rows], w[:, c, :],
                                                        start=(k == 0 and c == 0), stop=(k == 1 and c == KC - 1))
                        last.then_inc(s_proj_mm, 1)
                turned = g - LAG
                if 0 <= turned < NG:
                    for n in range(turned * TG, (turned + 1) * TG):
                        pe.wait_ge(s_xn2, n + 1)
                        if n % TG == 3 and turned:
                            logits(turned - 1)
                        if n >= 3:
                            pe.wait_ge(s_tr2_ev, n - 2)
                        for c in range(KC):
                            last = nc.tensor.transpose(TURN_BANKS[n % 3][:, c * TR:(c + 1) * TR],
                                                       turn_rows[turned % 3][:, n % TG, c * 128:(c + 1) * 128],
                                                       ident[0:TR, 0:TR])
                        last.then_inc(s_tr2_mm, 1)
                    pe.wait_ge(s_rsplit, 2)
                    for part, (t0, n) in enumerate(PARTS):
                        pe.wait_ge(s_tr2_ev, turned * TG + min(t0 + n + 1, TG))
                        if turned:
                            pe.wait_ge(s_rh_ev, 2 * (turned - 1) + part + 1)
                        _, width, first = EVEN[part]
                        nodes = slice(turned * GN + first, turned * GN + first + width)
                        product(ps_big[:, part, 0:width],
                                [([rw1_hl[:, k, c, :] for k in range(2)], [x[:, c, nodes] for x in xT_hl])
                                 for c in range(KC)]).then_inc(s_rh_mm, 1)
            logits(NG - 1)

            pe.wait_ge(s_rh_ev, 2 * NG)
            with pe.Fori(0, NG) as g:
                def hidden(e, layer):
                    for part, (at, width, first) in enumerate(EVEN):
                        for m in range(KC):
                            i = e * 8 + layer * 4 + part * KC + m
                            pe.wait_ge(s_e_ev, EVS * g + (i + 1))
                            pe.wait_ge(s_split, layer * NX + e + 1)
                            if layer:
                                pe.wait_ge(s_lo, 4 + EVS * g + (e * 8 + (part + 1) * KC))
                            nodes, own = bass.ds(g * GN + first, width), slice(at, at + width)
                            product(EXPERT_BANKS[i % 4][:, 0:width],
                                    [([ew_sb[layer][:, k, e, c, m * 128:(m + 1) * 128] for k in range(2)],
                                      [x[:, c, own] for x in h1_hl] if layer else [x[:, c, nodes] for x in xT_hl])
                                     for c in range(KC)]).then_inc(s_e_mm, 1)

                def output(e):
                    for t in range(TG):
                        i = (e + (e == NX - 1)) * TG + t
                        pe.wait_ge(s_lo, 4 + EVS * g + (e * 8 + 4 + (KC if t < PARTS[1][0] else 2 * KC)))
                        pe.wait_ge(s_split, 2 * NX + e + 1)
                        pe.wait_ge(s_y_add, 1 + ROWS * g + added(i))
                        at = t * TR + (0 if t < PARTS[1][0] else EVEN[1][0] - EVEN[1][2])
                        product(OUTPUT_BANKS[t % 3][0:TR, 0:D],
                                [([h[:, c, at:at + TR] for h in h2_hl], [ew_sb[2][:, k, e, c, :] for k in range(2)])
                                 for c in range(KC)]).then_inc(s_y_mm, 1)

                for e in range(NX):
                    hidden(e, 0)
                    if e:
                        output(e - 1)
                    hidden(e, 1)
                    if e in GATES_AFTER:
                        part = GATES_AFTER.index(e)
                        t0, n = PARTS[part]
                        pe.wait_ge(s_gate, g + 1)
                        if part:
                            pe.wait_ge(s_gtr_ev, 2 * g + 1)
                        for t in range(n):
                            last = nc.tensor.transpose(ps_att[:, t * TR:(t + 1) * TR], gate_pad[:, t0 + t, :],
                                                       ident[0:TR, 0:TR])
                        last.then_inc(s_gtr_mm, 1)
                for t in range(TG):
                    i = (NX - 1) * TG + t
                    pe.wait_ge(s_gtr_ev, 2 * g + (1 if t < PARTS[1][0] else 2))
                    pe.wait_ge(s_y_add, 1 + ROWS * g + added(i))
                    nc.tensor.matmul(OUTPUT_BANKS[t % 3][0:TR, 0:D], gates_col[:, t * TR:(t + 1) * TR], b3_sb[:, :],
                                     start=True, stop=True).then_inc(s_y_mm, 1)
                output(NX - 1)

        @block.scalar
        def _(act):
            act.sem_inc(s_big_free, 2)
            act.sem_inc(s_row_free, 2)
            for started in (s_xnT, s_kv_ev, s_tr_free):
                act.sem_inc(started, 1)
            act.sem_inc(s_e_ev, 4)

            def cols(ps):
                return ps.rearrange("p (c n) -> p c n", c=KC)

            for k, (e, t) in enumerate(((src, src_i), (dst, dst_i), (edge_w, ew_r))):
                act.dma_start(t, edge_rows(e)).then_inc(s_src_in if k == 0 else s_edges, 16)
            act.wait_ge(s_src_in, 16)
            nc.scalar.copy(src_f, src_i).then_inc(s_srcf, 1)
            act.wait_ge(s_edge_tr, 1)
            nc.scalar.copy(srcT[:, 0:NCH].rearrange("p (q j) -> p j q", j=QC),
                           ps_big[0:TR, 1, 0:NCH].rearrange("p (j q) -> p j q", j=QC)).then_inc(s_srcT, 1)
            act.wait_ge(s_x[NG - 1], 16)
            for k, (t, w) in enumerate(((wkv_sb[:, :, 0:D], chunked(wk)), (wkv_sb[:, :, D:2 * D], chunked(wv)))):
                act.dma_start(t, w).then_inc(s_wkv, 16)
            for t, w in ((g2_bc, g2), (b2_bc, b2), (rb2_bc, rb2)):
                act.dma_start(t[:, :], w.partition_broadcast(TR)).then_inc(s_bc, 16)
            for n in range(NT):
                act.wait_ge(s_xn_tr, 1 + n + 1)
                nc.scalar.copy(xnT[:, :, n * TR:(n + 1) * TR], cols(ps_row[:, n % 2, 0:KC * TR])).then_inc(s_xnT, 1)

            act.wait_ge(s_edge_ready, 2)
            for k in range(2):
                act.dma_start(low_dram[k:k + 1, :].rearrange("k p -> p k"), low_i[:, k:k + 1],
                             allow_slow_non_contiguous=True).then_inc(s_low_out, 16)
            act.wait_ge(s_low_out, 32)
            act.dma_start(low_row[:, :, :], low_dram.rearrange("(a k) n -> a k n", a=1)).then_inc(s_low_in, 16)
            act.wait_ge(s_rows_out[NG - 1], 16)
            for t, w in ((wq_sb, chunked(wq)), (wm_sb, chunked(wm)), (w1_sb, chunked(w1)), (w2_sb, chunked(w2)),
                         (g1_sb, g1c), (b1_sb, b1c)):
                act.dma_start(t[:, :] if len(t.shape) == 2 else t[:, :, :], w).then_inc(s_wmix, 16)

            act.wait_ge(s_zero, 4)
            with act.Fori(0, NG) as g:
                for t in range(TG):
                    act.wait_ge(s_kv_mm, 1 + TG * g + (t + 1))
                    act.wait_ge(s_key, 1 + TG * g + max(t - 1, 0))
                    act.wait_ge(s_kvp, 1 + TG * g)
                    nc.scalar.activation(el_e[0:TR, t % 2, 0:D], ps_big[0:TR, t % 2, 0:D], ACT.Exp)
                    nc.scalar.activation(el_r[0:TR, t % 2, 0:D], ps_big[0:TR, t % 2, 0:D], ACT.Relu)
                    nc.scalar.activation(v_g[:, t, :, 0:128], cols(ps_big[0:TR, t % 2, D:2 * D]), ACT.Copy,
                                         scale=1.0 / N).then_inc(s_kv_ev, 1)
            act.wait_ge(s_key, 1 + TG * NG)

            act.wait_ge(s_wmix, 16 * 6)

            def mix(stage, g, front, back):
                big, tr, row = Turns(stage, "QH", g), Turns(stage, "TN", g), Turns(stage, "MP", g)
                for step in STEPS[stage]:
                    kind, k = step
                    if kind == "Q":
                        n, i = PARTS[k // KC][1], big.take(step)
                        act.wait_ge(s_big_mm, big.value(1 + i + 1))
                        act.wait_ge(s_q, front.value(2 * KC, 1 + max(k - 1, 0)))
                        nc.scalar.activation(el_e[:, k % 2, 0:n * TR], ps_big[:, i % 2, 0:n * TR], ACT.Exp)
                        nc.scalar.activation(el_r[:, k % 2, 0:n * TR], ps_big[:, i % 2, 0:n * TR],
                                             ACT.Relu).then_inc(s_big_free, 1)
                    elif kind == "T":
                        act.wait_ge(s_tr_mm, tr.value(tr.take(step) + 1))
                        nc.scalar.copy(colC[:, :, k * TR:(k + 1) * TR], cols(ps_tr[:, 0:KC * TR])).then_inc(s_tr_free, 1)
                    elif kind == "M":
                        i = row.take(step)
                        act.wait_ge(s_row_mm, row.value(i + 1))
                        nc.scalar.copy(rowA[:, k, :], ps_row[0:TR, i % 2, 0:D]).then_inc(s_row_free, 1)
                    elif kind == "N":
                        act.wait_ge(s_tr_mm, tr.value(tr.take(step) + 1))
                        for c in range(KC):
                            last = nc.scalar.activation(colD[:, c, k * TR:(k + 1) * TR],
                                                        turn_bank(step)[:, c * TR:(c + 1) * TR],
                                                        ACT.Identity, bias=b1_sb[:, c:c + 1], scale=g1_sb[:, c:c + 1])
                        last.then_inc(s_tr_free, 1)
                    elif kind == "H":
                        t0, n = PARTS[k // H1]
                        i = big.take(step)
                        act.wait_ge(s_big_mm, big.value(1 + i + 1))
                        nc.scalar.activation(hid[:, k % H1, t0 * TR:(t0 + n) * TR], ps_big[:, i % 2, 0:n * TR],
                                             ACT.Relu).then_inc(s_big_free, 1)
                    elif kind == "P":
                        i = row.take(step)
                        act.wait_ge(s_row_mm, row.value(i + 1))
                        act.wait_ge(s_h2done, back.value(TG, 1))
                        nc.scalar.copy(rowC[:, k, :], ps_row[0:TR, i % 2, 0:D]).then_inc(s_row_free, 1)

            mix(OPEN, 0, Groups(0, 0), None)
            with act.Fori(0, NG - 1) as g:
                mix(LOOP, g, Groups(g, 1), Groups(g, 0))
            mix(CLOSE, 0, None, Groups(0, NG - 1))
            act.drain().then_inc(s_phase, 1)
            act.wait_ge(s_phase, 3)
            act.wait_ge(s_wffn, 16 * 8)
            for g in range(NG + LAG):
                if g < NG:
                    for n in range(g * TG, (g + 1) * TG):
                        act.wait_ge(s_proj_mm, n + 1)
                        if g == 2:
                            act.wait_ge(s_h2done, 1 + NT)
                        if g > 2:
                            act.wait_ge(s_tr2_mm, (g - 2) * TG)
                        nc.scalar.copy(turn_rows[g % 3][:, n % TG, :], ps_row[0:TR, n % 2, 0:D])
                        nc.scalar.activation(el_r[0:TR, n % 2, 0:D], ps_row[0:TR, n % 2, 0:D], ACT.Square,
                                             accum_out=ve_all[:, n:n + 1]).then_inc(s_proj_ev, 1)
                turned = g - LAG
                if turned >= 0:
                    for n in range(turned * TG, (turned + 1) * TG):
                        act.wait_ge(s_tr2_mm, n + 1)
                        nc.scalar.copy(xT_hl[0][:, :, n * TR:(n + 1) * TR],
                                       cols(TURN_BANKS[n % 3][:, 0:KC * TR])).then_inc(s_tr2_hi, 1)
                    for part, (t0, n) in enumerate(PARTS):
                        act.wait_ge(s_rh_mm, 2 * turned + (part + 1))
                        if turned >= 2:
                            act.wait_ge(s_lg_mm, turned - 1)
                        nc.scalar.activation(rhid[:, turned % 2, t0 * TR:(t0 + n) * TR], ps_big[:, part, 0:n * TR],
                                             ACT.Relu, bias=rb1_sb[:, 0:1]).then_inc(s_rh_ev, 1)
            act.wait_ge(s_sm, 1)
            nc.scalar.activation(sm[:, 1, :, :], sm[:, 0, :, :], ACT.Exp).then_inc(s_ex, 1)
            act.wait_ge(s_sm, 2)
            nc.scalar.activation(sv[:, 5, :], sv[:, 4, :], ACT.Exp).then_inc(s_ex, 1)

            with act.Fori(0, NG) as g:
                for e in range(NX):
                    for layer, (hi, _) in enumerate((h1_hl, h2_hl)):
                        for part, (at, width, _) in enumerate(EVEN):
                            for m in range(KC):
                                i = e * 8 + layer * 4 + part * KC + m
                                act.wait_ge(s_e_mm, EVS * g + (i + 1))
                                bank, bias = EXPERT_BANKS[i % 4][:, 0:width], eb_sb[:, layer, e, m:m + 1]
                                nc.scalar.activation(hi[:, m, at:at + width], bank, ACT.Relu,
                                                     bias=bias)
                                act.wait_ge(s_lo, EVS * g + (i + 1))
                                nc.scalar.activation(WHOLE[i % 4][:, 0:width], bank, ACT.Relu, bias=bias
                                                     ).then_inc(s_e_ev, 1)
                    if e in GATES_AFTER:
                        part = GATES_AFTER.index(e)
                        t0, n = PARTS[part]
                        act.wait_ge(s_gtr_mm, 2 * g + (part + 1))
                        nc.scalar.copy(gates_col[:, t0 * TR:(t0 + n) * TR], ps_att[:, 0:n * TR]).then_inc(s_gtr_ev, 1)

        @block.vector
        def _(dve):
            dve.sem_inc(s_add, 1)
            dve.sem_inc(s_lo, 4)
            for started in (s_key, s_q, s_att, s_kvsum, s_y_add, s_h2done, s_over_chunk):
                dve.sem_inc(started, 1)

            def bc(ap, shape):
                return ap.unsqueeze(len(shape) - 1).broadcast_to(shape)

            ln = Links(dve, s_v0)
            for g in range(NG):
                dve.wait_ge(s_x[g], 16)
                for t in range(TG):
                    ln.add(nc.vector.bn_stats(st_all[:, g * TG + t, :], resid[:, g * TG + t, :]))
            for n in range(NT):
                if n == 0:
                    ln.wait()
                ln.add(nc.vector.bn_aggr(mv_all[:, n, :], st_all[:, n, :]))
            ln.wait()
            ln.link(nc.vector.tensor_scalar(ve_all[:, :], mv_all[:, :, 1], LN_EPS, None, ALU.add))
            rsqrt(nc, ln, rstd_all[:, :], ve_all[:, :], rtmp_all[:, :])
            for n in range(NT):
                nc.vector.tensor_scalar(xn_rows[n // TG][:, n % TG, :], resid[:, n, :], mv_all[:, n, 0:1],
                                        rstd_all[:, n:n + 1], ALU.subtract, ALU.mult).then_inc(s_xn, 1)

            def add_rows(*groups):
                for g in groups:
                    dve.wait_ge(s_xn, NT)
                    nc.vector.tensor_tensor(out=resid[:, g * TG:(g + 1) * TG, :], in0=resid[:, g * TG:(g + 1) * TG, :],
                                            in1=xn_rows[g], op=ALU.add).then_inc(s_v0b, 1)

            add_rows(*range(2, NG))
            p = Links(dve, s_prep)
            dve.wait_ge(s_edges, 32)
            p.link(nc.vector.tensor_copy(dst_f, dst_i))
            p.add(nc.vector.tensor_reduce(out=low_f[:, :], in_=dst_f, op=ALU.min, axis=AX))
            p.link(nc.vector.tensor_reduce(out=span_f[:, :], in_=dst_f, op=ALU.max, axis=AX))
            p.add(nc.vector.tensor_tensor(out=span_f[:, :], in0=span_f[:, :], in1=low_f[:, :], op=ALU.subtract))
            nc.vector.tensor_scalar(dst_f, dst_f, low_f[:, 0:1], None, ALU.subtract).then_inc(s_edge_ready, 1)
            p.wait()
            p.add(nc.vector.tensor_copy(low_i[:, 0:1], low_f[:, :]))
            nc.vector.tensor_copy(low_i[:, 1:2], span_f[:, :]).then_inc(s_edge_ready, 1)
            dve.wait_ge(s_ident, 2)
            p.link(nc.vector.tensor_copy(win_iota[:, :], win_iota_i))
            p.add(nc.vector.memset(gate_pad[:, :, :], 0.0))
            p.add(nc.vector.memset(relT[:, NCH:NCH + AHEAD * QC], -1.0))
            p.add(nc.vector.memset(wT[:, NCH:NCH + AHEAD * QC], 0.0))
            dve.wait_ge(s_edge_tr, 3)
            for t, bank in ((relT, ps_big[0:TR, 0, 0:NCH]), (wT, ps_att[0:TR, 0:NCH])):
                p.add(nc.vector.tensor_copy(t[:, 0:NCH].rearrange("p (q j) -> p j q", j=QC),
                                            bank.rearrange("p (j q) -> p j q", j=QC)))
            p.wait()
            nc.vector.memset(zr[:, :, :], 0.0).then_inc(s_lists, 1)

            def stage_edges(first, qpg, g, ln):
                n, off = qpg * QC, (first + AHEAD) * QC
                dve.wait_ge(s_hot, g * qpg + (first + AHEAD))
                ln.add(nc.vector.tensor_copy(rel_g[:, 0:n], relT[:, bass.ds(g * n + off, n)]))
                ln.link(nc.vector.tensor_copy(w_g[:, 0:n], wT[:, bass.ds(g * n + off, n)]))

            spots = {}

            def build(place, c0):
                for c in range(QC):
                    last = nc.vector.tensor_scalar(onehot[:, place * QC + c, :], win_iota[:, :], rel_g[:, c0 + c:c0 + c + 1],
                                                   w_g[:, c0 + c:c0 + c + 1], ALU.is_equal, ALU.mult)
                last.then_inc(s_hot, 1)

            def quad(first, qpg, g, q):
                if q < qpg:
                    dve.wait_ge(s_quad, g * qpg + (first + q + AHEAD + 1))
                    build((q + AHEAD) % RQ, q * QC)
                if not q:
                    return
                q -= 1
                if q % RQ == 0:
                    spots["starts"] = nc.values_load_multi_w_load_instructions(
                        low_row[0:1, 0, bass.ds(g * qpg + first + q, RQ)], engines=DVE_ONLY,
                        min_val=0, max_val=N - 1, skip_runtime_bounds_check_because="destinations are nodes")[1]
                w = accT[:, :, bass.ds(spots["starts"][q % RQ], WIN)]
                dve.wait_ge(s_quad, g * qpg + (first + q + RQ + 1))
                dve.wait_ge(s_add, g * qpg + (first + q + 1))
                nc.vector.tensor_tensor(out=w, in0=w,
                                        in1=ps_agg[:, q % 2, 0:KC * WIN].rearrange("p (k n) -> p k n", k=KC),
                                        op=ALU.add).then_inc(s_add, 1)

            dve.wait_ge(s_low_in, 16)
            dve.wait_ge(s_bc, 48)
            dve.wait_ge(s_zero, 4)
            ln = Links(dve, s_v0a)
            ln.link(nc.vector.tensor_reduce(out=over_at[:, 0:1], in_=low_row[:, 1, :], op=ALU.max, axis=AX))
            nc.vector.tensor_copy(spill_i[:, :], over_at[:, 0:1]).then_inc(s_spill, 1)
            ln.add(nc.vector.tensor_copy(rel_g[:, 0:AHEAD * QC], relT[:, 0:AHEAD * QC]))
            ln.link(nc.vector.tensor_copy(w_g[:, 0:AHEAD * QC], wT[:, 0:AHEAD * QC]))
            for q in range(AHEAD):
                build(q, q * QC)
            add_rows(0, 1)
            dve.wait_ge(s_v0b, NG)
            with dve.Fori(0, NG) as g:
                ln = Links(dve, s_v1, 3, g)
                stage_edges(0, QPG0, g, ln)
                for q in range(TG):
                    quad(0, QPG0, g, q)
                    dve.wait_ge(s_kv_ev, 1 + TG * g + (q + 1))
                    dve.wait_ge(s_kvp, 1 + TG * g)
                    nc.vector.scalar_tensor_tensor(out=rowB[:, q, :], in0=el_e[0:TR, q % 2, 0:D], scalar=1.0,
                                                   in1=el_r[0:TR, q % 2, 0:D], op0=ALU.min, op1=ALU.add
                                                   ).then_inc(s_key, 1)
                ln.link(nc.vector.tensor_tensor(out=resid[:, bass.ds(g * TG, TG), :],
                                                in0=resid[:, bass.ds(g * TG, TG), :],
                                                in1=b2_bc[:, :].unsqueeze(1).broadcast_to([TR, TG, D]), op=ALU.add))
                quad(0, QPG0, g, QPG0)
                dve.wait_ge(s_kvp, 1 + TG * g + TG)
                dve.wait_ge(s_kvsum, 1 + g)
                nc.vector.tensor_tensor(out=kv_acc[:, :, :], in0=kv_acc[:, :, :], in1=ps_row[:, :, 0:129],
                                        op=ALU.add).then_inc(s_kvsum, 1)
                dve.wait_ge(s_kvsum, 1 + g + 1)
                ln.close()
            for j in range(HPC):
                r = slice(HD * j, HD * (j + 1))
                nc.vector.tensor_copy(kv_bd[r, :, r], kv_acc[r, :, r])
                nc.vector.tensor_copy(kv_bd[r, :, 128 + j:129 + j], kv_acc[r, :, 128:129])
            dve.drain().then_inc(s_bd, 1)

            def mix(stage, g, front, back, ln):
                big, row = Turns(stage, "QH", g), Turns(stage, "MP", g)
                first, qpg = QUADS_BEFORE[stage], QUADS[stage]

                def spread():
                    hold(dve, "vector", ln.sem, ln.value())
                    for t in range(TG):
                        ln.add(nc.vector.bn_aggr(mv_g[:, t, :], st_g[:, t, :]))
                    ln.wait()
                    ln.link(nc.vector.tensor_scalar(ve_g[:, :], mv_g[:, :, 1], LN_EPS, None, ALU.add))
                    rsqrt(nc, ln, rs_g[:, :], ve_g[:, :], rt_g[:, :])

                if qpg:
                    stage_edges(first, qpg, g, ln)
                for step in STEPS[stage]:
                    kind, k = step
                    if kind == "Q":
                        (t0, n), m = PARTS[k // KC], k % KC
                        dve.wait_ge(s_big_free, big.value(2 + big.take(step) + 1))
                        nc.vector.scalar_tensor_tensor(out=colB[:, m, t0 * TR:(t0 + n) * TR], in0=el_e[:, k % 2, 0:n * TR],
                                                       scalar=1.0, in1=el_r[:, k % 2, 0:n * TR], op0=ALU.min,
                                                       op1=ALU.add).then_inc(s_q, 1)
                    elif kind == "H":
                        big.take(step)
                    elif kind == "A":
                        dve.wait_ge(s_att_mm, front.value(TG, k + 1))
                        halves = ps_att[0:TR, 0:KC * HW].rearrange("p (c n) -> p c n", c=KC)
                        ln.link(nc.vector.tensor_scalar(zr[:, :, :], halves[:, :, 128:HW], ATT_EPS, 1.0 / N, ALU.add,
                                                        ALU.mult))
                        ln.link(nc.vector.reciprocal(zr[:, :, :], zr[:, :, :]))
                        nc.vector.tensor_tensor(
                            out=rowB[:, k, :].rearrange("p (c j d) -> p c j d", c=KC, j=HPC),
                            in0=halves[:, :, 0:128].rearrange("p c (j d) -> p c j d", j=HPC),
                            in1=bc(zr[:, :, :], [TR, KC, HPC, HD]), op=ALU.mult).then_inc(s_att, 1)
                    elif kind in "MP":
                        dve.wait_ge(s_row_free, row.value(2 + row.take(step) + 1))
                        ln.add(nc.vector.bn_stats(st_g[:, k, :], (rowA if kind == "M" else rowC)[:, k, :]))
                    elif kind == "S":
                        spread()
                        for t in range(TG):
                            nc.vector.tensor_scalar(rowA[:, t, :], rowA[:, t, :], mv_g[:, t, 0:1], rs_g[:, t:t + 1],
                                                    ALU.subtract, ALU.mult).then_inc(s_norm1, 1)
                    elif kind == "R":
                        spread()
                        for t in range(TG):
                            ln.add(nc.vector.scalar_tensor_tensor(out=rowC[:, t, :], in0=rowC[:, t, :],
                                                                  scalar=mv_g[:, t, 0:1], in1=g2_bc[:, :],
                                                                  op0=ALU.subtract, op1=ALU.mult))
                        ln.wait()
                        for t in range(TG):
                            tile = resid[:, bass.ds(back.value(TG, t), 1), :].squeeze(1)
                            nc.vector.scalar_tensor_tensor(out=tile, in0=rowC[:, t, :], scalar=rs_g[:, t:t + 1],
                                                           in1=tile, op0=ALU.mult, op1=ALU.add).then_inc(s_h2done, 1)
                    elif kind in "GF":
                        quad(first, qpg, g, k if kind == "G" else qpg)

            mix(OPEN, 0, Groups(0, 0), None, Links(dve, s_open))
            with dve.Fori(0, NG - 1) as g:
                ln = Links(dve, s_v2, MIX_LINKS, g)
                mix(LOOP, g, Groups(g, 1), Groups(g, 0), ln)
                ln.close()
            mix(CLOSE, 0, None, Groups(0, NG - 1), Links(dve, s_close))
            dve.drain().then_inc(s_phase, 1)
            dve.wait_ge(s_phase, 3)

            nc.vector.tensor_copy(low_all.rearrange("p (q j) -> p q j", j=QC),
                                  low_row[:, 0, :].unsqueeze(2).broadcast_to([1, NQ, QC])).then_inc(s_low_all, 1)
            hold(dve, "vector", s_low_all, 1)

            with dve.If(dve.value_load(spill_i[0:1, 0:1], min_val=0, max_val=N) > WIN - 1):
                with dve.Fori(0, NCH) as c:
                    head = Links(dve, s_over_v, 3 + 3 * MORE, c)
                    head.add(nc.vector.tensor_copy(over_f[:, 0:1], relT[:, bass.ds(c, 1)]))
                    head.add(nc.vector.tensor_copy(over_f[:, 1:2], wT[:, bass.ds(c, 1)]))
                    head.add(nc.vector.tensor_copy(over_at[:, 0:1], low_all[:, bass.ds(c, 1)]))
                    hold(dve, "vector", s_over_v, head.value())
                    with dve.Fori(0, MORE) as w:
                        k = (3 + 3 * MORE) * c + 3 * w
                        nc.vector.tensor_scalar(over_at[:, 0:1], over_at[:, 0:1], float(WIN), float(N), ALU.add,
                                                ALU.min).then_inc(s_over_v, 1)
                        nc.vector.tensor_scalar(over_f[:, 0:1], over_f[:, 0:1], float(-WIN), None,
                                                ALU.add).then_inc(s_over_v, 1)
                        dve.wait_ge(s_over_v, k + 5)
                        nc.vector.tensor_copy(over_i[:, 0:1], over_at[:, 0:1]).then_inc(s_over_v, 1)
                        nc.vector.tensor_scalar(onehot[:, 0, :], win_iota[:, :], over_f[:, 0:1], over_f[:, 1:2],
                                                ALU.is_equal, ALU.mult).then_inc(s_over_hot, 1)
                        hold(dve, "vector", s_over_v, k + 6)
                        start = dve.value_load(over_i[0:1, 0:1], min_val=0, max_val=N)
                        dve.wait_ge(s_over_mm, MORE * c + w + 1)
                        window = accT[:, :, bass.ds(start, WIN)]
                        nc.vector.tensor_tensor(out=window, in0=window, op=ALU.add,
                                                in1=ps_agg[:, 0, 0:KC * WIN].rearrange("p (k n) -> p k n", k=KC)
                                                ).then_inc(s_over_add, 1)
                        dve.wait_ge(s_over_add, MORE * c + w + 1)
                    dve.sem_inc(s_over_chunk, 1)
            dve.drain().then_inc(s_phase, 1)
            dve.wait_ge(s_phase, 5)

            mix(FINISH, 0, None, Groups(0, NG - 1), Links(dve, s_finish))

            ln = Links(dve, s_v2b)

            def low_parts(g):
                for n in range(g * TG, (g + 1) * TG):
                    dve.wait_ge(s_tr2_hi, n + 1)
                    hi = xT_hl[0][:, :, n * TR:(n + 1) * TR].bitcast(F32)
                    bank = TURN_BANKS[n % 3][:, 0:KC * TR].rearrange("p (c n) -> p c n", c=KC)
                    nc.vector.tensor_tensor(out=xT_hl[1][:, :, n * TR:(n + 1) * TR], in0=bank, in1=hi,
                                            op=ALU.subtract).then_inc(s_tr2_ev, 1)

            for g in range(NG + 1):
                if g >= LAG:
                    low_parts(g - LAG)
                tiles = range(g * TG, (g + 1) * TG) if g < NG else ()
                lo, hi = (0 if g < NG else TG), (2 * TG if g else TG)
                if g:
                    ln.add(nc.vector.tensor_scalar(v2[:, TG:2 * TG], mv_all[:, (g - 1) * TG:g * TG, 1], LN_EPS, None,
                                                   ALU.add))
                if g < NG:
                    dve.wait_ge(s_proj_ev, (g + 1) * TG)
                    ln.add(nc.vector.tensor_scalar(v2[:, 0:TG], ve_all[:, g * TG:(g + 1) * TG], NORM_EPS ** 2, None,
                                                   ALU.max))
                ln.wait()
                rsqrt(nc, ln, r2[:, lo:hi], v2[:, lo:hi], t2[:, lo:hi])
                if g:
                    for n in range((g - 1) * TG, g * TG):
                        nc.vector.tensor_scalar(turn_rows[(g - 1) % 3][:, n % TG, :], resid[:, n, :], mv_all[:, n, 0:1],
                                                r2[:, TG + n % TG:TG + n % TG + 1], ALU.subtract, ALU.mult
                                                ).then_inc(s_xn2, 1)
                for n in tiles:
                    ln.add(nc.vector.scalar_tensor_tensor(out=resid[:, n, :], in0=turn_rows[g % 3][:, n % TG, :],
                                                          scalar=r2[:, n % TG:n % TG + 1], in1=resid[:, n, :],
                                                          op0=ALU.mult, op1=ALU.add))
                summed = ln.k
                for n in tiles:
                    dve.wait_ge(s_v2b, summed - TG + n % TG + 1)
                    ln.add(nc.vector.bn_stats(st_all[:, n, :], resid[:, n, :]))
                for n in tiles:
                    dve.wait_ge(s_v2b, summed + n % TG + 1)
                    ln.add(nc.vector.bn_aggr(mv_all[:, n, :], st_all[:, n, :]))
                ln.wait()
            for g in range(NG + 1 - LAG, NG):
                low_parts(g)

            shape = [TR, NT, NX]
            lg, ex, pr, o1, o2, tmp = (sm[:, k, :, :] for k in range(6))
            mx, rs, p1, p2, df, e2, top, next_ = (sv[:, k, :] for k in range(8))
            dve.wait_ge(s_lg_mm, NG)
            ln.link(nc.vector.tensor_tensor(out=lg, in0=ps_att[0:TR, 0:NT * NX].rearrange("p (t e) -> p t e", t=NT),
                                            in1=rb2_bc[:, :].unsqueeze(1).broadcast_to(shape), op=ALU.add))
            ln.link(nc.vector.tensor_reduce(out=mx, in_=lg, op=ALU.max, axis=AX))
            nc.vector.tensor_tensor(out=lg, in0=lg, in1=bc(mx, shape), op=ALU.subtract).then_inc(s_sm, 1)
            dve.wait_ge(s_ex, 1)
            ln.link(nc.vector.tensor_reduce(out=rs, in_=ex, op=ALU.add, axis=AX))
            ln.link(nc.vector.reciprocal(rs, rs))
            ln.link(nc.vector.tensor_tensor(out=pr, in0=ex, in1=bc(rs, shape), op=ALU.mult))

            def pick(values, top, one):
                ln.link(nc.vector.tensor_reduce(out=top, in_=values, op=ALU.max, axis=AX))
                ln.link(nc.vector.tensor_tensor(out=one, in0=values, in1=bc(top, shape), op=ALU.is_equal))
                ln.link(nc.vector.tensor_tensor(out=one, in0=one, in1=rev[:, :].unsqueeze(1).broadcast_to(shape),
                                                op=ALU.mult))
                ln.link(nc.vector.tensor_reduce(out=mx, in_=one, op=ALU.max, axis=AX))
                ln.link(nc.vector.tensor_tensor(out=one, in0=one, in1=bc(mx, shape), op=ALU.is_equal))

            pick(pr, p1, o1)
            ln.link(nc.vector.scalar_tensor_tensor(out=tmp, in0=o1, scalar=-2.0, in1=pr, op0=ALU.mult, op1=ALU.add))
            pick(tmp, p2, o2)
            nc.vector.tensor_tensor(out=df, in0=p2, in1=p1, op=ALU.subtract).then_inc(s_sm, 1)
            dve.wait_ge(s_ex, 2)
            ln.link(nc.vector.tensor_scalar(top, e2, 1.0, None, ALU.add))
            ln.link(nc.vector.reciprocal(top, top))
            ln.link(nc.vector.tensor_tensor(out=next_, in0=e2, in1=top, op=ALU.mult))
            ln.add(nc.vector.tensor_tensor(out=o1, in0=o1, in1=bc(top, shape), op=ALU.mult))
            ln.link(nc.vector.tensor_tensor(out=o2, in0=o2, in1=bc(next_, shape), op=ALU.mult))
            ln.link(nc.vector.tensor_tensor(out=gates_all[:, :, :], in0=o1, in1=o2, op=ALU.add))

            with dve.Fori(0, NG) as g:
                dve.wait_ge(s_y_add, 1 + ROWS * g)
                nc.vector.tensor_copy(gates_g[:, :, :], gates_all[:, bass.ds(g * TG, TG), :]).then_inc(s_v3, 1)
                nc.vector.tensor_copy(gate_pad[:, :, 0:NX], gates_all[:, bass.ds(g * TG, TG), :]).then_inc(s_gate, 1)
                dve.wait_ge(s_v3, g + 1)

                def low_parts(e, layer, products=range(4)):
                    hi, lo = (h1_hl, h2_hl)[layer]
                    for k in products:
                        (at, width, _), m = EVEN[k // KC], k % KC
                        i = e * 8 + layer * 4 + k
                        own = slice(at, at + width)
                        dve.wait_ge(s_e_ev, 4 + EVS * g + (i + 1))
                        nc.vector.tensor_tensor(out=lo[:, m, own], in0=WHOLE[i % 4][:, 0:width],
                                                in1=hi[:, m, own].bitcast(F32), op=ALU.subtract).then_inc(s_lo, 1)

                def add(k, e, tiles=range(TG)):
                    for t in tiles:
                        i = k * TG + t
                        tile = resid[:, bass.ds(g * TG + t, 1), :].squeeze(1)
                        dve.wait_ge(s_y_mm, ROWS * g + (i + 1))
                        if k:
                            dve.wait_ge(s_y_add, 1 + ROWS * g + (i + 1 - TG))
                        y = OUTPUT_BANKS[t % 3][0:TR, 0:D]
                        if e is None:
                            nc.vector.tensor_tensor(out=tile, in0=tile, in1=y, op=ALU.add).then_inc(s_y_add, 1)
                        else:
                            nc.vector.scalar_tensor_tensor(out=tile, in0=y, scalar=gates_g[:, t, e:e + 1], in1=tile,
                                                           op0=ALU.mult, op1=ALU.add).then_inc(s_y_add, 1)

                for e in range(NX):
                    if e:
                        low_parts(e, 0, range(3))
                        add(e - 1, e - 1, range(2))
                        low_parts(e, 0, (3,))
                        add(e - 1, e - 1, range(2, TG))
                    else:
                        low_parts(e, 0)
                    low_parts(e, 1, range(4 if e < NX - 1 else 3))
                add(NX - 1, None, range(2))
                low_parts(NX - 1, 1, (3,))
                add(NX - 1, None, range(2, TG))
                add(NX, NX - 1)


MIX_LINKS = 2 + 2 * 5 + 2 * (5 + 5 + 1 + 11) + 5


def _columns(a):
    import numpy as _np
    a = _np.asarray(a)
    return _np.ascontiguousarray(_np.moveaxis(a.reshape(a.shape[:-1] + (-1, 128)), -1, 0))


def kernel(**inputs):
    import numpy as _np
    import concourse.bacc as _bacc
    from concourse.bass_utils import run_bass_kernel_spmd as _run

    i = {k: _np.asarray(v) for k, v in inputs.items()}
    mix, ffn = "L0_mix_", "L0_ffn_"
    laid = {
        "x": i["x"], "src": i["src"], "dst": i["dst"], "edge_w": i["edge_weight"],
        "w_self_t": i["L0_gnn_w_self"].T, "w_neigh_t": i["L0_gnn_w_neigh"].T,
        "wq": i[mix + "Wq"], "wk": i[mix + "Wk"], "wv": i[mix + "Wv"], "wm": i[mix + "Wm"],
        "w1": i[mix + "W1"], "w2": i[mix + "W2"], "g1c": _columns(i[mix + "g1"]), "b1c": _columns(i[mix + "b1"]),
        "g2": i[mix + "g2"], "b2": i[mix + "b2"],
        "rw1": i[ffn + "router_w1"], "rb1c": _columns(i[ffn + "router_b1"]), "rw2": i[ffn + "router_w2"],
        "rb2": i[ffn + "router_b2"],
        "ew1": i[ffn + "expert_w1"], "eb1c": _columns(i[ffn + "expert_b1"]),
        "ew2": i[ffn + "expert_w2"], "eb2c": _columns(i[ffn + "expert_b2"]),
        "ew3": i[ffn + "expert_w3"], "eb3": i[ffn + "expert_b3"],
    }
    nc = _bacc.Bacc("TRN2", target_bir_lowering=False, num_devices=1)
    arrays, args = {}, []
    for name, a in laid.items():
        a = _np.ascontiguousarray(a)
        arrays[f"in_{name}"] = a
        args.append(nc.dram_tensor(f"in_{name}", a.shape, mybir.dt.from_np(a.dtype), kind="ExternalInput").ap())
    out = nc.dram_tensor("out_rows", i["x"].shape, F32, kind="ExternalOutput").ap()
    gps_layer_kernel(nc, *args, out)
    r = _run(nc, [arrays], core_ids=[0])
    return r.results[0]["out_rows"]
```
